# Optimizing a Trainium2 kernel written in Bass

```python
import numpy as np
import jax
import jax.numpy as jnp

def _softmax(x, axis=-1):
    return jax.nn.softmax(x, axis=axis)
def _gelu(x):
    return jax.nn.gelu(x, approximate=True)
def _silu(x):
    return jax.nn.silu(x)
def _sigmoid(x):
    return jax.nn.sigmoid(x)
def _layernorm(x, axis=-1, eps=1e-5):
    m = jnp.mean(x, axis=axis, keepdims=True)
    v = jnp.var(x, axis=axis, keepdims=True)
    return (x - m) / jnp.sqrt(v + eps)
def _scatter_add(tgt, idx, src, axis=0):
    return tgt.at[idx].add(src)
def _segment_sum(src, seg, n):
    return jax.ops.segment_sum(src, seg, n)

kernel_name = 'mk_conv_attn_hybrid_d2_conv_nchw128_a54a5c'

def setup_inputs(seed: int = 0):
    np.random.seed(seed)
    _w = jnp.asarray
    def _rec_inputs():
        import jax
        import jax.numpy as jnp
        _gk = jax.random.key(seed)
        x = -0.0002928 + 1 * jax.random.normal(jax.random.fold_in(_gk, 1), (8, 128, 64, 64), jnp.float32)
        return x
    x = _rec_inputs()
    def _L0_conv_setup():
        import jax, jax.numpy as jnp
        import numpy as np
        from jax import lax
        B, C, H, W = (8, 128, 64, 64)
        DS, HD = (64, 32)
        DIN = 2 * C
        NH = DIN // HD
        DCONV = 4
        CONVCH = DIN + 2 * DS
        NBR = 5
        GN_GROUPS = 8
        TEMP = 10000.0

        def _perms():
            idx = np.arange(H * W).reshape(H, W)
            row = idx.reshape(-1)
            col = idx.T.reshape(-1)
            sh = idx.copy()
            sh[1::2] = sh[1::2, ::-1]
            sv = idx.T.copy()
            sv[1::2] = sv[1::2, ::-1]
            perms = [row, col, sh.reshape(-1), sv.reshape(-1)]
            return ([jnp.asarray(p) for p in perms], [jnp.asarray(np.argsort(p)) for p in perms])
        PERMS, INVS = _perms()

        def _pos_emb():
            half = C // 2
            dim_t = TEMP ** (np.arange(0, half, 2, dtype=np.float32) / half)
            ph = np.arange(H, dtype=np.float32)[:, None] / dim_t
            pw = np.arange(W, dtype=np.float32)[:, None] / dim_t
            eh = np.stack([np.sin(ph), np.cos(ph)], 2).reshape(H, -1)[:, :half]
            ew = np.stack([np.sin(pw), np.cos(pw)], 2).reshape(W, -1)[:, :C - half]
            emb = np.concatenate([np.broadcast_to(eh[:, None, :], (H, W, half)), np.broadcast_to(ew[None, :, :], (H, W, C - half))], -1)
            return jnp.asarray(emb.transpose(2, 0, 1))
        POS = _pos_emb()

        def _mamba(u, Wi, cw, Alog, dtb, Dp, nw, Wo):
            b, L, _ = u.shape
            zxbcdt = u @ Wi
            z = zxbcdt[..., :DIN]
            xBC = zxbcdt[..., DIN:DIN + CONVCH]
            dt = zxbcdt[..., DIN + CONVCH:]
            xBC = lax.conv_general_dilated(xBC, cw[:, None, :], (1,), [(DCONV - 1, 0)], dimension_numbers=('NWC', 'WIO', 'NWC'), feature_group_count=CONVCH)
            xBC = jax.nn.silu(xBC)
            xh = xBC[..., :DIN].reshape(b, L, NH, HD)
            Bm = xBC[..., DIN:DIN + DS]
            Cm = xBC[..., DIN + DS:]
            dt = jax.nn.softplus(dt + dtb)
            dA = jnp.exp(dt * -jnp.exp(Alog))

            def step(h, inp):
                dA_t, dt_t, x_t, B_t, C_t = inp
                h = dA_t[:, :, None, None] * h + (dt_t[:, :, None] * x_t)[..., None] * B_t[:, None, None, :]
                y = jnp.einsum('bhdn,bn->bhd', h, C_t)
                return (h, y)
            xs = (dA.transpose(1, 0, 2), dt.transpose(1, 0, 2), xh.transpose(1, 0, 2, 3), Bm.transpose(1, 0, 2), Cm.transpose(1, 0, 2))
            h0 = jnp.zeros((b, NH, HD, DS), u.dtype)
            _, ys = lax.scan(step, h0, xs)
            y = ys.transpose(1, 0, 2, 3) + Dp[None, None, :, None] * xh
            y = y.reshape(b, L, DIN) * jax.nn.silu(z)
            y = y * lax.rsqrt(jnp.mean(y * y, -1, keepdims=True) + 1e-05) * nw
            return y @ Wo

        def _forward(x, pos_proj_w, local_w, W_in, conv_w, A_log, dt_bias, Dp, norm_w, W_out, se_w1, se_b1, se_w2, se_b2, proj_w, gn_gamma, gn_beta):
            xp = x + jnp.einsum('chw,oc->ohw', POS.astype(x.dtype), pos_proj_w)[None]
            local = jax.nn.gelu(lax.conv_general_dilated(xp, local_w, (1, 1), 'SAME', dimension_numbers=('NCHW', 'OIHW', 'NCHW'), feature_group_count=C))
            seq = xp.reshape(B, C, H * W).transpose(0, 2, 1)
            branches = [local]
            for i in range(4):
                u = jnp.take(seq, PERMS[i], axis=1)
                y = _mamba(u, W_in[i], conv_w[i], A_log[i], dt_bias[i], Dp[i], norm_w[i], W_out[i])
                y = jnp.take(y, INVS[i], axis=1)
                branches.append(y.transpose(0, 2, 1).reshape(B, C, H, W))
            stacked = jnp.stack(branches, 1)
            desc = stacked.mean(axis=(2, 3, 4))
            wts = jax.nn.sigmoid(jax.nn.gelu(desc @ se_w1 + se_b1) @ se_w2 + se_b2)
            fused = (stacked * wts[:, :, None, None, None]).sum(1)
            concat = stacked.reshape(B, NBR * C, H, W)
            proj = jnp.einsum('bihw,oi->bohw', concat, proj_w)
            g = proj.reshape(B, GN_GROUPS, -1)
            g = (g - g.mean(-1, keepdims=True)) * lax.rsqrt(g.var(-1, keepdims=True) + 1e-05)
            proj = jax.nn.gelu(g.reshape(B, C, H, W) * gn_gamma[None, :, None, None] + gn_beta[None, :, None, None])
            return x + fused + proj
        key = jax.random.key(seed)
        ks = jax.random.split(key, 20)
        n = lambda k, s, sc: jax.random.normal(k, s, jnp.float32) * sc
        return {'x': n(ks[0], (B, C, H, W), 1.0), 'pos_proj_w': n(ks[1], (C, C), C ** (-0.5)), 'local_w': n(ks[2], (C, 1, 3, 3), 0.2), 'W_in': n(ks[3], (4, C, DIN + CONVCH + NH), C ** (-0.5)), 'conv_w': n(ks[4], (4, DCONV, CONVCH), 0.3), 'A_log': n(ks[5], (4, NH), 0.5), 'dt_bias': n(ks[6], (4, NH), 0.5), 'Dp': n(ks[7], (4, NH), 1.0), 'norm_w': jnp.ones((4, DIN), jnp.float32) + n(ks[8], (4, DIN), 0.02), 'W_out': n(ks[9], (4, DIN, C), DIN ** (-0.5)), 'se_w1': n(ks[10], (NBR, 2), 0.5), 'se_b1': n(ks[11], (2,), 0.1), 'se_w2': n(ks[12], (2, NBR), 0.5), 'se_b2': n(ks[13], (NBR,), 0.1), 'proj_w': n(ks[14], (C, NBR * C), (NBR * C) ** (-0.5)), 'gn_gamma': jnp.ones((C,), jnp.float32), 'gn_beta': jnp.zeros((C,), jnp.float32)}
    _L0_conv_all = _L0_conv_setup()
    _L0_conv_in = {k: v for k, v in _L0_conv_all.items() if k in ('pos_proj_w', 'local_w', 'W_in', 'conv_w', 'A_log', 'dt_bias', 'Dp', 'norm_w', 'W_out', 'se_w1', 'se_b1', 'se_w2', 'se_b2', 'proj_w', 'gn_gamma', 'gn_beta', )}
    del _L0_conv_all

    def _L1_attn_setup():
        import jax, jax.numpy as jnp
        import numpy as np
        B, N, D = (4, 1024, 128)
        key = jax.random.key(seed)
        ks = jax.random.split(key, 4)
        scale = 1.0 / np.sqrt(D)
        return {'inputs': jax.random.normal(ks[0], (B, N, D), dtype=jnp.float32), 'Wq': jax.random.normal(ks[1], (D, D), dtype=jnp.float32) * scale, 'bq': jnp.zeros((D,), dtype=jnp.float32), 'Wk': jax.random.normal(ks[2], (D, D), dtype=jnp.float32) * scale, 'bk': jnp.zeros((D,), dtype=jnp.float32), 'Wv': jax.random.normal(ks[3], (D, D), dtype=jnp.float32) * scale, 'bv': jnp.zeros((D,), dtype=jnp.float32)}
    _L1_attn_all = _L1_attn_setup()
    _L1_attn_in = {k: v for k, v in _L1_attn_all.items() if k in ('Wq', 'bq', 'Wk', 'bk', 'Wv', 'bv', )}
    del _L1_attn_all

    def _L1_ffn_setup():
        import jax, jax.numpy as jnp
        import numpy as np
        B, N, D, C, E, K = (8, 8192, 128, 128, 8, 2)
        key = jax.random.key(seed)
        k0, k1, k2 = jax.random.split(key, 3)
        x = jax.random.normal(k0, (B, N, D), dtype=jnp.float32)
        router_w = jax.random.normal(k1, (D, E), dtype=jnp.float32) * 0.05
        router_b = jnp.zeros((E,), dtype=jnp.float32)
        expert_w = jax.random.normal(k2, (E, D, C), dtype=jnp.float32) * (1.0 / np.sqrt(D))
        expert_b = jnp.zeros((E, C), dtype=jnp.float32)
        return {'x': x, 'router_w': router_w, 'router_b': router_b, 'expert_w': expert_w, 'expert_b': expert_b}
    _L1_ffn_all = _L1_ffn_setup()
    _L1_ffn_in = {k: v for k, v in _L1_ffn_all.items() if k in ('router_w', 'router_b', 'expert_w', 'expert_b', )}
    del _L1_ffn_all

    return {
        "x": x,
        "L0_conv_pos_proj_w": _L0_conv_in["pos_proj_w"],
        "L0_conv_local_w": _L0_conv_in["local_w"],
        "L0_conv_W_in": _L0_conv_in["W_in"],
        "L0_conv_conv_w": _L0_conv_in["conv_w"],
        "L0_conv_A_log": _L0_conv_in["A_log"],
        "L0_conv_dt_bias": _L0_conv_in["dt_bias"],
        "L0_conv_Dp": _L0_conv_in["Dp"],
        "L0_conv_norm_w": _L0_conv_in["norm_w"],
        "L0_conv_W_out": _L0_conv_in["W_out"],
        "L0_conv_se_w1": _L0_conv_in["se_w1"],
        "L0_conv_se_b1": _L0_conv_in["se_b1"],
        "L0_conv_se_w2": _L0_conv_in["se_w2"],
        "L0_conv_se_b2": _L0_conv_in["se_b2"],
        "L0_conv_proj_w": _L0_conv_in["proj_w"],
        "L0_conv_gn_gamma": _L0_conv_in["gn_gamma"],
        "L0_conv_gn_beta": _L0_conv_in["gn_beta"],
        "L1_attn_Wq": _L1_attn_in["Wq"],
        "L1_attn_bq": _L1_attn_in["bq"],
        "L1_attn_Wk": _L1_attn_in["Wk"],
        "L1_attn_bk": _L1_attn_in["bk"],
        "L1_attn_Wv": _L1_attn_in["Wv"],
        "L1_attn_bv": _L1_attn_in["bv"],
        "L1_ffn_router_w": _L1_ffn_in["router_w"],
        "L1_ffn_router_b": _L1_ffn_in["router_b"],
        "L1_ffn_expert_w": _L1_ffn_in["expert_w"],
        "L1_ffn_expert_b": _L1_ffn_in["expert_b"],
    }

def reference(x, L0_conv_pos_proj_w, L0_conv_local_w, L0_conv_W_in, L0_conv_conv_w, L0_conv_A_log, L0_conv_dt_bias, L0_conv_Dp, L0_conv_norm_w, L0_conv_W_out, L0_conv_se_w1, L0_conv_se_b1, L0_conv_se_w2, L0_conv_se_b2, L0_conv_proj_w, L0_conv_gn_gamma, L0_conv_gn_beta, L1_attn_Wq, L1_attn_bq, L1_attn_Wk, L1_attn_bk, L1_attn_Wv, L1_attn_bv, L1_ffn_router_w, L1_ffn_router_b, L1_ffn_expert_w, L1_ffn_expert_b):
    import jax
    import jax.numpy as jnp
    def _L0_conv_ref(x, pos_proj_w, local_w, W_in, conv_w, A_log, dt_bias, Dp, norm_w, W_out, se_w1, se_b1, se_w2, se_b2, proj_w, gn_gamma, gn_beta):
        import jax, jax.numpy as jnp
        import numpy as np
        from jax import lax
        B, C, H, W = (8, 128, 64, 64)
        DS, HD = (64, 32)
        DIN = 2 * C
        NH = DIN // HD
        DCONV = 4
        CONVCH = DIN + 2 * DS
        NBR = 5
        GN_GROUPS = 8
        TEMP = 10000.0

        def _perms():
            idx = np.arange(H * W).reshape(H, W)
            row = idx.reshape(-1)
            col = idx.T.reshape(-1)
            sh = idx.copy()
            sh[1::2] = sh[1::2, ::-1]
            sv = idx.T.copy()
            sv[1::2] = sv[1::2, ::-1]
            perms = [row, col, sh.reshape(-1), sv.reshape(-1)]
            return ([jnp.asarray(p) for p in perms], [jnp.asarray(np.argsort(p)) for p in perms])
        PERMS, INVS = _perms()

        def _pos_emb():
            half = C // 2
            dim_t = TEMP ** (np.arange(0, half, 2, dtype=np.float32) / half)
            ph = np.arange(H, dtype=np.float32)[:, None] / dim_t
            pw = np.arange(W, dtype=np.float32)[:, None] / dim_t
            eh = np.stack([np.sin(ph), np.cos(ph)], 2).reshape(H, -1)[:, :half]
            ew = np.stack([np.sin(pw), np.cos(pw)], 2).reshape(W, -1)[:, :C - half]
            emb = np.concatenate([np.broadcast_to(eh[:, None, :], (H, W, half)), np.broadcast_to(ew[None, :, :], (H, W, C - half))], -1)
            return jnp.asarray(emb.transpose(2, 0, 1))
        POS = _pos_emb()

        def _mamba(u, Wi, cw, Alog, dtb, Dp, nw, Wo):
            b, L, _ = u.shape
            zxbcdt = u @ Wi
            z = zxbcdt[..., :DIN]
            xBC = zxbcdt[..., DIN:DIN + CONVCH]
            dt = zxbcdt[..., DIN + CONVCH:]
            xBC = lax.conv_general_dilated(xBC, cw[:, None, :], (1,), [(DCONV - 1, 0)], dimension_numbers=('NWC', 'WIO', 'NWC'), feature_group_count=CONVCH)
            xBC = jax.nn.silu(xBC)
            xh = xBC[..., :DIN].reshape(b, L, NH, HD)
            Bm = xBC[..., DIN:DIN + DS]
            Cm = xBC[..., DIN + DS:]
            dt = jax.nn.softplus(dt + dtb)
            dA = jnp.exp(dt * -jnp.exp(Alog))

            def step(h, inp):
                dA_t, dt_t, x_t, B_t, C_t = inp
                h = dA_t[:, :, None, None] * h + (dt_t[:, :, None] * x_t)[..., None] * B_t[:, None, None, :]
                y = jnp.einsum('bhdn,bn->bhd', h, C_t)
                return (h, y)
            xs = (dA.transpose(1, 0, 2), dt.transpose(1, 0, 2), xh.transpose(1, 0, 2, 3), Bm.transpose(1, 0, 2), Cm.transpose(1, 0, 2))
            h0 = jnp.zeros((b, NH, HD, DS), u.dtype)
            _, ys = lax.scan(step, h0, xs)
            y = ys.transpose(1, 0, 2, 3) + Dp[None, None, :, None] * xh
            y = y.reshape(b, L, DIN) * jax.nn.silu(z)
            y = y * lax.rsqrt(jnp.mean(y * y, -1, keepdims=True) + 1e-05) * nw
            return y @ Wo

        def _forward(x, pos_proj_w, local_w, W_in, conv_w, A_log, dt_bias, Dp, norm_w, W_out, se_w1, se_b1, se_w2, se_b2, proj_w, gn_gamma, gn_beta):
            xp = x + jnp.einsum('chw,oc->ohw', POS.astype(x.dtype), pos_proj_w)[None]
            local = jax.nn.gelu(lax.conv_general_dilated(xp, local_w, (1, 1), 'SAME', dimension_numbers=('NCHW', 'OIHW', 'NCHW'), feature_group_count=C))
            seq = xp.reshape(B, C, H * W).transpose(0, 2, 1)
            branches = [local]
            for i in range(4):
                u = jnp.take(seq, PERMS[i], axis=1)
                y = _mamba(u, W_in[i], conv_w[i], A_log[i], dt_bias[i], Dp[i], norm_w[i], W_out[i])
                y = jnp.take(y, INVS[i], axis=1)
                branches.append(y.transpose(0, 2, 1).reshape(B, C, H, W))
            stacked = jnp.stack(branches, 1)
            desc = stacked.mean(axis=(2, 3, 4))
            wts = jax.nn.sigmoid(jax.nn.gelu(desc @ se_w1 + se_b1) @ se_w2 + se_b2)
            fused = (stacked * wts[:, :, None, None, None]).sum(1)
            concat = stacked.reshape(B, NBR * C, H, W)
            proj = jnp.einsum('bihw,oi->bohw', concat, proj_w)
            g = proj.reshape(B, GN_GROUPS, -1)
            g = (g - g.mean(-1, keepdims=True)) * lax.rsqrt(g.var(-1, keepdims=True) + 1e-05)
            proj = jax.nn.gelu(g.reshape(B, C, H, W) * gn_gamma[None, :, None, None] + gn_beta[None, :, None, None])
            return x + fused + proj
        return _forward(x, pos_proj_w, local_w, W_in, conv_w, A_log, dt_bias, Dp, norm_w, W_out, se_w1, se_b1, se_w2, se_b2, proj_w, gn_gamma, gn_beta)

    def _L1_attn_ref(inputs, Wq, bq, Wk, bk, Wv, bv):
        import jax, jax.numpy as jnp
        import numpy as np
        B, N, D = (4, 1024, 128)
        q = inputs @ Wq + bq
        k = inputs @ Wk + bk
        v = inputs @ Wv + bv
        kv = jnp.sum(k * v, axis=1, keepdims=True)
        return q * kv

    def _L1_ffn_ref(x, router_w, router_b, expert_w, expert_b):
        import jax, jax.numpy as jnp
        import numpy as np
        B, N, D, C, E, K = (8, 8192, 128, 128, 8, 2)
        router_probs = jax.nn.softmax(x @ router_w + router_b, axis=-1)
        top_p, top_i = jax.lax.top_k(router_probs, K)
        top_p = top_p / jnp.sum(top_p, axis=-1, keepdims=True)
        expert_out = jnp.einsum('bnd,edc->bnec', x, expert_w) + expert_b
        gathered = jnp.take_along_axis(expert_out, top_i[..., None], axis=2)
        return jnp.einsum('bnk,bnkc->bnc', top_p, gathered)

    def _gn(v, G=32, eps=1e-5):
        B_, C_, H_, W_ = v.shape
        g = v.reshape(B_, G, C_ // G, H_, W_)
        m = jnp.mean(g, axis=(2, 3, 4), keepdims=True)
        s = jnp.var(g, axis=(2, 3, 4), keepdims=True)
        return ((g - m) / jnp.sqrt(s + eps)).reshape(v.shape)

    def _ln_c(v, eps=1e-6):
        m = jnp.mean(v, axis=1, keepdims=True)
        s = jnp.var(v, axis=1, keepdims=True)
        return (v - m) / jnp.sqrt(s + eps)

    def _ln_t(v, eps=1e-5):
        m = jnp.mean(v, axis=-1, keepdims=True)
        s = jnp.var(v, axis=-1, keepdims=True)
        return (v - m) / jnp.sqrt(s + eps)

    def _to_tokens(v):
        B_, C_, H_, W_ = v.shape
        return v.reshape(B_, C_, H_ * W_).transpose(0, 2, 1)
    def _from_tokens(t, like):
        B_, C_, H_, W_ = like.shape
        return t.transpose(0, 2, 1).reshape(B_, C_, H_, W_)

    x = _L0_conv_ref(x, L0_conv_pos_proj_w, L0_conv_local_w, L0_conv_W_in, L0_conv_conv_w, L0_conv_A_log, L0_conv_dt_bias, L0_conv_Dp, L0_conv_norm_w, L0_conv_W_out, L0_conv_se_w1, L0_conv_se_b1, L0_conv_se_w2, L0_conv_se_b2, L0_conv_proj_w, L0_conv_gn_gamma, L0_conv_gn_beta)
    t = _to_tokens(x)
    t = t + _L1_attn_ref(_ln_t(t), L1_attn_Wq, L1_attn_bq, L1_attn_Wk, L1_attn_bk, L1_attn_Wv, L1_attn_bv)
    t = t + _L1_ffn_ref(_ln_t(t), L1_ffn_router_w, L1_ffn_router_b, L1_ffn_expert_w, L1_ffn_expert_b)
    x = _from_tokens(t, x)
    return x


_drawn_inputs = setup_inputs


def setup_inputs(seed=0):
    import zlib

    import numpy as np

    out = dict(_drawn_inputs(seed))
    spreads = {'L0_conv_gn_gamma': (1.0, 0.2),
     'L0_conv_gn_beta': (0.0, 0.1),
     'L1_attn_bq': (0.0, 0.1),
     'L1_attn_bk': (0.0, 0.1),
     'L1_attn_bv': (0.0, 0.1),
     'L1_ffn_router_b': (0.0, 2.0),
     'L1_ffn_expert_b': (0.0, 2.0)}
    factors = {'L0_conv_norm_w': 3.049,
     'L0_conv_se_w1': 8.0,
     'L0_conv_se_b1': 8.0,
     'L0_conv_se_w2': 8.0,
     'L1_ffn_router_w': 27.83,
     'L1_ffn_expert_w': 25.743}
    for name, (base, spread) in spreads.items():
        noise = np.random.default_rng([zlib.crc32(name.encode()), seed]).standard_normal(out[name].shape)
        drawn = base * np.exp(spread * noise) if base else spread * noise
        out[name] = jnp.asarray(drawn.astype(out[name].dtype))
    for name, factor in factors.items():
        out[name] = (out[name] * factor).astype(out[name].dtype)
    return out
```

```python
from contextlib import ExitStack

import numpy as np

import concourse.bass as bass
from concourse import mybir

F32 = mybir.dt.float32
BF16 = mybir.dt.bfloat16
ALU = mybir.AluOpType
ACT = mybir.ActivationFunctionType
AX = mybir.AxisListType

P = 128
NB = 8
HW = 64
L = HW * HW
NBR = 4
DIN, DS, NH, HD = 256, 64, 8, 32
TAPS = 4
XT = 3
Q = 128
UT = 2 * Q
ROWS = UT // HW
NG = L // UT
BG = 2
BU = BG * NBR
ROWF = HW + 6
HEAD = 4
NE = 8
TT = 512
NT = L // TT
NEVER = -1e30
LN_EPS, GN_EPS = 1e-5, 1e-5
CONVS = NG * NBR + 1
AHEAD = 2 * NG * NBR + 1
GC = 2 * NBR * NH
SE_STEPS, GN_STEPS, GATE_STEPS = 7, 5, 19
TROW = TT // HW

LOG1P = [0.9999999991556807, -0.499999794913725, 0.33332497543045325, -0.24986496454167328, 0.19885820254416264,
         -0.16087622903223123, 0.12377995638908859, -0.0818804061299571, 0.041006571120306035,
         -0.013187825375511738, 0.0019866963583891365]


def hybrid_kernel(nc, a):
    with ExitStack() as ctx:
        def sb(name, shape, dt=F32):
            return ctx.enter_context(nc.sbuf_tensor(name, shape, dt))

        def sem(name):
            return ctx.enter_context(nc.semaphore(name))

        ident = sb("ident", [P, P])
        upto = sb("upto", [P, P])
        after = sb("after", [P, P])
        ones = sb("ones", [P, P])
        mean_w = sb("mean_w", [P, P])
        group_avg = sb("group_avg", [P, P])
        selbase = sb("selbase", [96, 32])
        sel = sb("sel", [96, 32], BF16)
        ident_b = sb("ident_b", [P, P], BF16)
        never = sb("never", [P, P], BF16)
        nsel = sb("nsel", [96, 32], BF16)
        small = sb("small", [P, 256])
        w_in = sb("w_in", [P, NBR, 648])
        conv_w = sb("conv_w", [P, NBR, XT, TAPS])
        w_out = sb("w_out", [P, NBR, 2, P])
        norm_w = sb("norm_w", [P, NBR, 2])
        proj_w = sb("proj_w", [P, 5, P])
        wqkv = sb("wqkv", [P, 3, P])
        router = sb("router", [P, NE])
        expert_b = sb("expert_b", [NE, P])
        pos_t = sb("pos_t", [P, HW])
        pos_w = sb("pos_w", [P, P])
        pos = sb("pos", [P, 2, HW])
        local_w = sb("local_w", [P, 9])
        at = {}
        col = 0
        for name, n in (("A", 32), ("dtb", 32), ("Dp", 32), ("w1", 10), ("b1", 2), ("w2", 10), ("b2", 5), ("rb", NE),
                        ("lt", NE * NE), ("gamma", 1), ("beta", 1), ("bq", 1), ("bk", 1), ("bv", 1)):
            at[name] = (col, col + n)
            col += n
        assert col <= 256

        def par(name):
            return small[:, at[name][0]:at[name][1]]

        xp = sb("xp", [P, ROWF, ROWF])
        arena = sb("arena", [P, L])
        br = [sb(f"br{i}", [P, HW, HW]) for i in range(NBR)] + [arena[:].rearrange("c (h w) -> c h w", h=HW)]
        brf = [(t if t is br[4] else t[:]).rearrange("c h w -> c (h w)") for t in br]
        ust = [[sb(f"ust{p}{i}", [P, UT]) for i in range(NBR)] for p in range(2)]
        pre = [sb(f"pre{i}", [P, XT, 3 + UT]) for i in range(2)]
        past = [sb(f"past{i}", [P, XT, 3]) for i in range(NBR)]
        acc = [arena[:, i * XT * UT:(i + 1) * XT * UT].rearrange("c (t n) -> c t n", t=XT) for i in range(2)]
        th = sb("th", [P, XT, UT])
        xbc = [arena[:, i * XT * UT:(i + 1) * XT * UT].rearrange("c (t n) -> c t n", t=XT) for i in range(2, 4)]
        bt = [arena[:, 3072 + i * UT:3072 + (i + 1) * UT] for i in range(2)]
        xtok = [sb(f"xtok{i}", [P, XT, P]) for i in range(2)]
        ebuf = sb("ebuf", [P, NH, P])
        gm = [sb(f"gm{i}", [P, P]) for i in range(2)]
        mix = [sb(f"mix{i}", [P, NH, P]) for i in range(2)]
        xd = [sb(f"xd{i}", [P, 2, DIN]) for i in range(2)]
        dx = [sb(f"dx{i}", [P, DIN]) for i in range(2)]
        state = [sb(f"state{i}", [P, 2, DIN]) for i in range(NBR)]
        hd = [arena[:, 3584 + i * UT:3584 + (i + 1) * UT] for i in range(2)]
        y1 = sb("y1", [P, DIN])
        y2 = sb("y2", [P, DIN])
        y3 = sb("y3", [P, DIN])
        y4 = [sb(f"y4{i}", [P, 2, DIN]) for i in range(2)]
        sqj = sb("sqj", [P, DIN])
        ss = sb("ss", [P, 2])
        sv = sb("sv", [P, 2])
        rs = sb("rs", [P, 2])
        mhalf = sb("mhalf", [P, 2])
        epsy = sb("epsy", [P, 2])
        tz = sb("tz", [P, 2, DIN])
        zg = [sb(f"zg{i}", [P, 2, DIN]) for i in range(2)]
        y5 = sb("y5", [P, 2, DIN])
        yts = sb("yts", [P, 2, UT])
        dtx = sb("dtx", [P, GC])
        dte = sb("dte", [P, 3, GC])
        dtp = sb("dtp", [P, GC])
        lna = sb("lna", [P, GC])
        ec = [sb(f"ec{i}", [P, 3, GC]) for i in range(2)]
        wd = [sb(f"wd{i}", [P, 2 * NBR, 2, NH]) for i in range(2)]
        cum = [sb(f"cum{i}", [96, UT], BF16) for i in range(2)]
        cr = sb("cr", [96, UT])
        cr2 = sb("cr2", [96, UT])
        sums = sb("sums", [P, 8])
        bnst = sb("bnst", [P, NT, 6])
        gst = sb("gst", [P, 16])
        se = sb("se", [P, 40])
        sew = sb("sew", [P, 5])
        gmx = sb("gmx", [P, L // P])
        eps = sb("eps", [P, 1])
        kvp = sb("kvp", [P, 16])
        expert_w = sb("expert_w", [P, NE, P])
        lna3 = sb("lna3", [P, 2, 96])
        ks = [zg[i][:].rearrange("c j d -> c (j d)") for i in range(2)]
        dump = tz[:].rearrange("c j d -> c (j d)")
        gates = ebuf[:].rearrange("c a (s e) -> c (a s) e", e=NE).rearrange("c (q s) e -> c q s e", q=4)
        xst = [y5[:, i, 0:P] for i in range(2)]
        rk = [mix[i][:].rearrange("c e n -> c (e n)")[:, 0:NE * 64].rearrange("c (s e j) -> c s e j", s=8, j=NE)
              for i in range(2)]
        lnb = [y4[i][:].rearrange("c j d -> c (j d)") for i in range(2)]
        C = slice(DS, P)

        def bank(name, n=1):
            return ctx.enter_context(nc.psum_tensor(name, [P, 512 * n], F32))
        px = bank("px", 2)
        pz = bank("pz")
        pd = bank("pd", 2)
        py = bank("py")
        pt = bank("pt")
        pyt = bank("pyt")
        XS = XT * UT

        x_tile_in = [sem("x_tile_in0"), sem("x_tile_in1")]
        pool_set, image_begun, row_added, local_step, fuse_step, norm_step = (sem(n) for n in
            ("pool_set", "image_begun", "row_added", "local_step", "fuse_step", "norm_step"))
        weights_in, pos_mm, params_scaled, selectors_made, a_step, image_in = (sem(n) for n in
            ("weights_in", "pos_mm", "params_scaled", "selectors_made", "a_step", "image_in"))
        xp_ready, local_ready, image_done, out_stored, abs_ready, log_step = (sem(n) for n in
            ("xp_ready", "local_ready", "image_done", "out_stored", "abs_ready", "log_step"))
        poly_step, part_step, past_kept, tap_step, y1_ready, y3_ready = (sem(n) for n in
            ("poly_step", "part_step", "past_kept", "tap_step", "y1_ready", "y3_ready"))
        sv_ready, sums_act, sums_dve, desc_mm, se_step, se_nonlin = (sem(n) for n in
            ("sv_ready", "sums_act", "sums_dve", "desc_mm", "se_step", "se_nonlin"))
        se_ready, gn_step, group_mm, group_rsqrt, affine_ready, gelu_ready = (sem(n) for n in
            ("se_ready", "gn_step", "group_mm", "group_rsqrt", "affine_ready", "gelu_ready"))
        x1_ready, kv_step, logits_mm, logits_step, gate_step, gates_exp = (sem(n) for n in
            ("x1_ready", "kv_step", "logits_mm", "logits_step", "gate_step", "gates_exp"))
        gates_ready, gates_turned, gates_copied = (sem(n) for n in
            ("gates_ready", "gates_turned", "gates_copied"))
        staged, wd_ready, dx_ready, hd_ready, y4_ready, rs_ready = (sem(n) for n in
            ("staged", "wd_ready", "dx_ready", "hd_ready", "y4_ready", "rs_ready"))
        dt_mm, cum_mm, x_mm, pairs_mm, decay_mm = (sem(n) for n in
            ("dt_mm", "cum_mm", "x_mm", "pairs_mm", "decay_mm"))
        y_mm, state_mm, z_mm, yt_mm, out_mm, proj_mm = (sem(n) for n in
            ("y_mm", "state_mm", "z_mm", "yt_mm", "out_mm", "proj_mm"))
        mean_mm, var_mm, kv_mm, q_mm, expert_mm, comb_mm = (sem(n) for n in
            ("mean_mm", "var_mm", "kv_mm", "q_mm", "expert_mm", "comb_mm"))
        dt_exp, cum_exp, pre_copied, conv_tanh_ready, bt_ready, xtok_ready = (sem(n) for n in
            ("dt_exp", "cum_exp", "pre_copied", "conv_tanh_ready", "bt_ready", "xtok_ready"))
        gm_ready, ebuf_ready, squared, tz_ready, yts_ready, branch_copied = (sem(n) for n in
            ("gm_ready", "ebuf_ready", "squared", "tz_ready", "yts_ready", "branch_copied"))
        proj_copied, squares_ready, rstd_ready, k_ready, q_ready, xst_ready = (sem(n) for n in
            ("proj_copied", "squares_ready", "rstd_ready", "k_ready", "q_ready", "xst_ready"))
        ln_ready, y5_ready = (sem(n) for n in
            ("ln_ready", "y5_ready"))
        dtx_ready, lna_ready, cum_ready, acc_ready, xbc_ready, mix_ready = (sem(n) for n in
            ("dtx_ready", "lna_ready", "cum_ready", "acc_ready", "xbc_ready", "mix_ready"))
        xd_ready, state_ready, y2_ready, zg_ready, fused_ready = (sem(n) for n in
            ("xd_ready", "state_ready", "y2_ready", "zg_ready", "fused_ready"))
        centered, normed, kv_summed, x2_ready, weighed, out_ready = (sem(n) for n in
            ("centered", "normed", "kv_summed", "x2_ready", "weighed", "out_ready"))

        def head_start(eng, guards):
            for guard in guards:
                eng.sem_inc(guard, HEAD)

        def order(i, image, g):
            if i % 2 == 0:
                return image[:, bass.ds(g * ROWS, ROWS), 0:HW]
            return image[:, 0:HW, bass.ds(g * ROWS, ROWS)].rearrange("c s r -> c r s")

        def scan_rows(i, seq):
            if i < 2:
                return [(slice(0, ROWS), seq)]
            return [(slice(0, ROWS, 2), seq[:, 0:ROWS:2, :]), (slice(1, ROWS, 2), seq[:, 1:ROWS:2, ::-1])]

        interior = xp[:, 1:ROWF, 1:ROWF]
        loads = [
            (ident[:], a["c_ident"]), (upto[:], a["c_upto"]), (after[:], a["c_after"]),
            (group_avg[:], a["c_group"]), (selbase[:], a["c_sel"]), (pos_t[:], a["c_pos"]),
            (small[:, 0:col], a["small"]), (w_in[:], a["w_in"].rearrange("i c n -> c i n")),
            (conv_w[:], a["conv_w"]), *[(w_out[:, i, :, :], a["w_out"][i].rearrange("(k c) n -> c k n", k=2)) for i in range(NBR)],
            (norm_w[:], a["norm_w"]), (proj_w[:], a["proj_w"].rearrange("(j i) o -> i j o", j=5)),
            (wqkv[:, 0, :], a["wq"]), (wqkv[:, 1, :], a["wk"]), (wqkv[:, 2, :], a["wv"]),
            (router[:], a["router"]), (expert_b[:], a["expert_b"]), (pos_w[:], a["pos_w"]), (local_w[:], a["local_w"]),
            (expert_w[:], a["expert_w"].rearrange("e d c -> d e c")),
        ]
        block = ctx.enter_context(nc.Block())

        @block.sync
        def _(sp):
            head_start(sp, (out_stored,))
            for dst, src in loads:
                sp.dma_start(dst, src).then_inc(weights_in, 16)
            with sp.Fori(0, NB) as b:
                sp.wait_ge(image_done, HEAD + b)
                sp.wait_ge(out_stored, HEAD + b * 16 * (L // (2 * P)))
                sp.dma_start(brf[0], a["x"][bass.ds(b, 1)].rearrange("o c n -> (o c) n")).then_inc(image_in, 16)
                with sp.Fori(0, NT // 2) as tp:
                    for h in range(2):
                        t = tp * 2 + h
                        sp.wait_ge(se_ready, b + 1)
                        sp.wait_ge(fused_ready, HEAD + b * NT + t - 1)
                        sp.dma_start(ks[h], a["x"][bass.ds(b, 1), :, bass.ds(t * TT, TT)]
                                     .rearrange("o c n -> (o c) n")).then_inc(x_tile_in[h], 16)
                with sp.Fori(0, L // (2 * P)) as sp2:
                    sp.wait_ge(out_ready, HEAD + b * (L // P) + sp2 * 2 + 2)
                    sp.dma_start(a["out"][bass.ds(b, 1), :, bass.ds(sp2 * 2 * P, 2 * P)]
                                 .rearrange("o c n -> (o c) n"),
                                 brf[3][:, bass.ds(sp2 * 2 * P, 2 * P)]).then_inc(out_stored, 16)
            sp.wait_ge(out_stored, HEAD + NB * 16 * (L // (2 * P)))

        @block.gpsimd
        def _(pool):
            head_start(pool, (staged, wd_ready, dx_ready, hd_ready, y4_ready, rs_ready))
            pool.memset(ones[:], 1.0)
            pool.memset(mean_w[:], 1.0 / P)
            pool.memset(epsy[:], 4e-5)
            pool.memset(mhalf[:], -0.5).then_inc(pool_set, 1)
            pool.wait_ge(weights_in, 16 * len(loads))
            pool.wait_ge(pool_set, 1)

            def stage(b, g, i, p):
                pieces = scan_rows(i, ust[p][i][:].rearrange("c (r s) -> c r s", r=ROWS))
                for k, (rows, dst) in enumerate(pieces):
                    ins = pool.tensor_copy(dst, order(i, interior, g)[:, rows, :])
                ins.then_inc(staged, 1)

            with pool.Fori(0, NB) as b:
                pool.wait_ge(xp_ready, b + 1)
                pool.tensor_tensor(sv[:], epsy[:], epsy[:], ALU.mult).then_inc(image_begun, 1)
                for i in range(NBR):
                    pieces = scan_rows(i, ust[0][i][:].rearrange("c (r s) -> c r s", r=ROWS))
                    src = (interior[:, 0:ROWS, 0:HW] if i % 2 == 0 else
                           interior[:, 0:HW, 0:ROWS].rearrange("c s r -> c r s"))
                    for rows, dst in pieces:
                        ins = pool.tensor_copy(dst, src[:, rows, :])
                    ins.then_inc(staged, 1)
                pool.wait_ge(cum_exp, HEAD + b * (NG + 1) + 1)
                pool.tensor_tensor(wd[0][:, :, 1, :], ec[0][:, 1, :].rearrange("c (u h) -> c u h", h=NH),
                                       wd[0][:, :, 0, :], ALU.mult).then_inc(wd_ready, 1)

                def y34(n, m, j, k):
                    pool.wait_ge(y2_ready, HEAD + m + 1)
                    pool.wait_ge(y4_ready, HEAD + m)
                    pool.wait_ge(dx_ready, HEAD + m + 1)
                    pool.tensor_tensor(y3[:], y2[:], dx[j][:], ALU.add).then_inc(y3_ready, 1)
                    pool.wait_ge(y3_ready, m + 1)
                    pool.wait_ge(zg_ready, HEAD + n + 1)
                    pool.wait_ge(y5_ready, HEAD + n - 1)
                    pool.tensor_tensor(y4[k % 2][:, j, :], y3[:], zg[k % 2][:, j, :], ALU.mult).then_inc(y4_ready, 1)

                def norm_factor(n):
                    pool.wait_ge(squared, HEAD + 2 * n + 2)
                    pool.wait_ge(y5_ready, HEAD + n)
                    pool.tensor_tensor(sv[:], ss[:], epsy[:], ALU.add).then_inc(sv_ready, 1)
                    pool.wait_ge(sv_ready, n + 1)
                    pool.tensor_tensor(rs[:], sv[:], mhalf[:], ALU.pow).then_inc(rs_ready, 1)

                with pool.Fori(0, NG // BG) as gg:
                    u, c = pool.snap(b * (NG * NBR) + gg * BU), pool.snap(b * (NG * NBR * 2) + gg * 2 * BU)
                    a_ = pool.snap(b * AHEAD + gg * 2 * BU)
                    g17, g2 = pool.snap(b * (NG + 1) + gg * BG), pool.snap(gg * BG)
                    def skip_term(j, m, t):
                        pool.wait_ge(xtok_ready, HEAD + t + 1)
                        pool.wait_ge(y4_ready, HEAD + m - 1)
                        pool.tensor_tensor(
                            dx[j][:].rearrange("c (h d) -> c h d", h=NH),
                            xtok[j][:, 0:2, :].rearrange("c a (h d) -> c (a h) d", d=HD),
                            par("Dp")[:, i * NH:(i + 1) * NH].unsqueeze(2).broadcast_to([P, NH, HD]),
                            ALU.mult).then_inc(dx_ready, 1)

                    def decay_state(j, m):
                        pool.wait_ge(cum_exp, HEAD + g17 + p + 1)
                        pool.wait_ge(state_ready, HEAD + (m - 1 if j == 0 else m))
                        dec = ec[p][:, 2, (j * NBR + i) * NH:(j * NBR + i + 1) * NH]
                        pool.tensor_tensor(
                            hd[j].rearrange("c (h d) -> c h d", h=NH),
                            state[i][:, j, :].rearrange("c (h d) -> c h d", h=NH),
                            dec.unsqueeze(2).broadcast_to([P, NH, HD]), ALU.mult).then_inc(hd_ready, 1)

                    for k in range(BU):
                        i, p = k % NBR, k // NBR
                        n, m = u + k, c + 2 * k
                        decay_state(0, m)
                        if k > 0:
                            y34(n - 1, m - 1, 1, k - 1)
                        skip_term(0, m, a_ + 2 * k)
                        if k > 0:
                            norm_factor(n - 1)
                        if i == 0:
                            pool.wait_ge(z_mm, HEAD + n)
                        skip_term(1, m + 1, a_ + 2 * k + 1)
                        decay_state(1, m + 1)
                        if i < 2:
                            for q in (2 * i, 2 * i + 1):
                                stage(b, g2 + p + 1, q, 1 - p)
                        if i == 3:
                            pool.wait_ge(cum_exp, HEAD + g17 + p + 2)
                            pool.wait_ge(xd_ready, HEAD + m - 6)
                            w = 1 - p
                            pool.tensor_tensor(
                                wd[w][:, :, 1, :], ec[w][:, 1, :].rearrange("c (u h) -> c u h", h=NH),
                                wd[w][:, :, 0, :], ALU.mult).then_inc(wd_ready, 1)
                        y34(n, m, 0, k)
                    y34(u + BU - 1, c + 2 * BU - 1, 1, BU - 1)
                    norm_factor(u + BU - 1)
                pool.wait_ge(gn_step, b * GN_STEPS + 4)
                pool.tensor_tensor(gst[:, 8:9], gst[:, 7:8], mhalf[:, 0:1], ALU.pow).then_inc(group_rsqrt, 1)

        @block.tensor
        def _(pe):
            mm = nc.tensor.matmul
            head_start(pe, (dt_mm, cum_mm, x_mm, pairs_mm, decay_mm, y_mm, state_mm, z_mm, yt_mm, out_mm,
                            proj_mm, mean_mm, var_mm, kv_mm, q_mm, expert_mm, comb_mm))
            pe.wait_ge(weights_in, 16 * len(loads))
            mm(pt[:, 0:HW], pos_w[0:DS, :], pos_t[0:DS, :], start=True, stop=True)
            mm(pyt[:, 0:HW], pos_w[DS:P, :], pos_t[DS:P, :], start=True, stop=True).then_inc(pos_mm, 1)
            pe.wait_ge(selectors_made, 1)

            def project_steps(p):
                for j in range(2):
                    for i in range(NBR):
                        o = XS + (j * NBR + i) * NH
                        ins = mm(px[:, o:o + NH], ust[p][i][:, j * Q:(j + 1) * Q], w_in[:, i, 640:648],
                                 start=True, stop=True, skip_group_check=True)
                ins.then_inc(dt_mm, 1)

            def sum_decays(p):
                for q, w in enumerate((upto, after, ones)):
                    mm(px[:, XS + GC * (q + 1):XS + GC * (q + 2)], w[:], lna[:], start=True, stop=True,
                       skip_group_check=True)
                for j in range(2):
                    rows = lna3[:, j, :]
                    ins = mm(px[0:96, 2 * UT + j * Q:2 * UT + (j + 1) * Q], rows, upto[:], start=True, stop=True,
                             skip_group_check=True)
                ins.then_inc(cum_mm, 1)

            def project_x(i, p):
                for t in range(XT):
                    ins = mm(px[:, t * UT:(t + 1) * UT], w_in[:, i, DIN + t * P:DIN + (t + 1) * P], ust[p][i][:],
                             start=True, stop=True, skip_group_check=True)
                ins.then_inc(x_mm, 1)

            with pe.Fori(0, NB) as b:
                pe.wait_ge(xp_ready, b + 1)
                pe.wait_ge(staged, HEAD + (b * (NG + 1) + 1) * NBR)
                project_steps(0)
                pe.wait_ge(lna_ready, HEAD + b * (NG + 1) + 1)
                sum_decays(0)
                pe.wait_ge(cum_exp, HEAD + b * (NG + 1) + 1)
                pe.wait_ge(cum_ready, HEAD + b * (NG + 1) + 1)
                project_x(0, 0)

                def decays(k, j, g, q):
                    p, i = k // NBR % 2, k % NBR
                    pe.wait_ge(cum_ready, HEAD + g + k // NBR + 1)
                    pe.wait_ge(ebuf_ready, HEAD + q)
                    part = cum[p][:, j * Q:(j + 1) * Q]
                    for half in range(2):
                        r = i * NH + half * 4
                        mm(pd[:, half * 512:(half + 1) * 512], ident_b[:], never[:].unsqueeze(1).broadcast_to([P, 4, P]),
                           start=True, stop=False, skip_group_check=True)
                        mm(pd[:, half * 512:(half + 1) * 512], part, nsel[:, r:r + 4].unsqueeze(2).broadcast_to([96, 4, P]),
                           start=False, stop=False, skip_group_check=True)
                        for h in range(4):
                            ins = mm(pd[:, half * 512 + h * Q:half * 512 + (h + 1) * Q],
                                     sel[:, r + h:r + h + 1].broadcast_to([96, P]), part,
                                     start=False, stop=(h == 3), skip_group_check=True)
                    ins.then_inc(decay_mm, 1)

                def turn_and_pair(k, j, v_, q):
                    pe.wait_ge(xbc_ready, HEAD + v_ + k + 1)
                    pe.wait_ge(xtok_ready, HEAD + q)
                    pe.wait_ge(gm_ready, HEAD + q)
                    for t in range(XT):
                        nc.tensor.transpose(pt[:, t * P:(t + 1) * P], xbc[k % 2][:, t, j * Q:(j + 1) * Q], ident[:])
                    pe.wait_ge(bt_ready, HEAD + v_ + k + 1)
                    mm(pt[:, XT * P:XT * P + P], bt[k % 2][C, j * Q:(j + 1) * Q],
                       xbc[k % 2][C, 2, j * Q:(j + 1) * Q], start=True, stop=True,
                       skip_group_check=True).then_inc(pairs_mm, 1)

                decays(0, 0, b * (NG + 1), b * AHEAD)
                pe.wait_ge(pre_copied, HEAD + b * CONVS + 1)
                project_x(1, 0)
                turn_and_pair(0, 0, b * CONVS, b * AHEAD)
                with pe.Fori(0, NG // BG) as gg:
                    u, c = pe.snap(b * (NG * NBR) + gg * BU), pe.snap(b * (NG * NBR * 2) + gg * 2 * BU)
                    x, g17 = pe.snap(b * CONVS + gg * BU), pe.snap(b * (NG + 1) + gg * BG)
                    us, a_ = pe.snap(b * ((NG + 1) * NBR) + gg * BU), pe.snap(b * AHEAD + gg * 2 * BU)

                    def add_state(k, j, m):
                        pe.wait_ge(xd_ready, HEAD + m + 1)
                        pe.wait_ge(state_ready, HEAD + m)
                        if j == 0:
                            pe.wait_ge(pre_copied, HEAD + x + k + 2)
                        mm(px[C, XS:XS + DIN], xtok[j][:, 2, 0:DS], xd[j][:, 1, :], start=True, stop=True,
                               skip_group_check=True).then_inc(state_mm, 1)

                    def outputs(k, j, m):
                        pe.wait_ge(mix_ready, HEAD + m + 1)
                        pe.wait_ge(xd_ready, HEAD + m + 1)
                        pe.wait_ge(y2_ready, HEAD + m)
                        pe.wait_ge(state_ready, HEAD + m)
                        for h in range(NH):
                            mm(py[:, h * HD:(h + 1) * HD], mix[j][:, h, :], xd[j][:, 0, h * HD:(h + 1) * HD],
                               start=True, stop=True, skip_group_check=True)
                        mm(py[:, DIN:2 * DIN], xbc[k % 2][C, 2, j * Q:(j + 1) * Q], state[k % NBR][C, j, :],
                               start=True, stop=True, skip_group_check=True).then_inc(y_mm, 1)

                    def gate(k, n):
                        pe.wait_ge(branch_copied, HEAD + (n if k == 0 else n - 1))
                        p, i = k // NBR, k % NBR
                        for j in range(2):
                            ins = mm(pz[:, j * DIN:(j + 1) * DIN], ust[p][i][:, j * Q:(j + 1) * Q], w_in[:, i, 0:DIN],
                                     start=True, stop=True, skip_group_check=True)
                        ins.then_inc(z_mm, 1)

                    def turn_back(n):
                        pe.wait_ge(y5_ready, HEAD + n + 1)
                        pe.wait_ge(yts_ready, HEAD + n)
                        for j in range(2):
                            for t in range(2):
                                ins = nc.tensor.transpose(pyt[:, t * UT + j * Q:t * UT + (j + 1) * Q],
                                                          y5[:, j, t * P:(t + 1) * P], ident[:])
                        ins.then_inc(yt_mm, 1)

                    def project_out(i, n, last):
                        pe.wait_ge(yts_ready, HEAD + n + 1)
                        pe.wait_ge(zg_ready, HEAD + (n + 1 if last else n + 2))
                        for t in range(2):
                            ins = mm(pz[:, 0:UT], w_out[:, i, t, :], yts[:, t, :], start=(t == 0), stop=(t == 1),
                                     skip_group_check=True)
                        ins.then_inc(out_mm, 1)

                    for k in range(BU):
                        n, m = u + k, c + 2 * k
                        p, i = k // NBR, k % NBR
                        decays(k, 1, g17, a_ + 2 * k + 1)
                        turn_and_pair(k, 1, x, a_ + 2 * k + 1)
                        if i == 2:
                            pe.wait_ge(staged, HEAD + us + NBR * (p + 2))
                            pe.wait_ge(pre_copied, HEAD + x + k + 2)
                            pe.wait_ge(state_ready, HEAD + m)
                            project_steps(1 - p)
                        if i == 3:
                            pe.wait_ge(lna_ready, HEAD + g17 + p + 2)
                            pe.wait_ge(pre_copied, HEAD + x + k + 2)
                            pe.wait_ge(state_ready, HEAD + m)
                            sum_decays(1 - p)
                        outputs(k, 0, m)
                        if i == 2:
                            pe.wait_ge(dtx_ready, HEAD + g17 + p + 2)
                        if i == 3:
                            pe.wait_ge(cum_exp, HEAD + g17 + p + 2)
                            pe.wait_ge(cum_ready, HEAD + g17 + p + 2)
                        add_state(k, 0, m)
                        gate(k, n)
                        decays(k + 1, 0, g17, a_ + 2 * k + 2)
                        if k > 0:
                            turn_back(n - 1)
                        add_state(k, 1, m + 1)
                        outputs(k, 1, m + 1)
                        if k > 0:
                            project_out((k - 1) % NBR, n - 1, False)
                        pe.wait_ge(staged, HEAD + us + k + 3)
                        pe.wait_ge(pre_copied, HEAD + x + k + 2)
                        pe.wait_ge(state_ready, HEAD + m + 2)
                        project_x((k + 2) % NBR, ((k + 2) // NBR) % 2)
                        turn_and_pair(k + 1, 0, x, a_ + 2 * k + 2)
                    turn_back(u + BU - 1)
                    project_out(NBR - 1, u + BU - 1, True)

                pe.wait_ge(sums_act, b * 3 + 3)
                pe.wait_ge(sums_dve, b * 2 + 2)
                mm(pt[:, 0:5], ones[:], sums[:, 0:5], start=True, stop=True).then_inc(desc_mm, 1)
                with pe.Fori(0, NT // 2) as tp:
                    for h in range(2):
                        t = tp * 2 + h
                        pe.wait_ge(proj_copied, HEAD + b * NT + t - 1)
                        for j in range(5):
                            src = brf[(j + 4) % 5][:, bass.ds(t * TT, TT)]
                            ins = mm(px[:, h * TT:(h + 1) * TT], proj_w[:, j, :], src, start=(j == 0), stop=(j == 4))
                        ins.then_inc(proj_mm, 1)
                pe.wait_ge(gn_step, b * GN_STEPS + 3)
                mm(pt[:, 8:10], group_avg[:], gst[:, 2:4], start=True, stop=True).then_inc(group_mm, 1)

                def tile(buf, t):
                    return buf[:, bass.ds(t * TT, TT)]

                def norm_tokens(pass_):
                    with pe.Fori(0, NT // 2) as tp:
                        for h in range(2):
                            t = tp * 2 + h
                            e = (b * 2 + pass_) * NT + t
                            pe.wait_ge(centered, HEAD + e - 1)
                            if pass_ == 0:
                                pe.wait_ge(x1_ready, b * 4 + 4)
                            else:
                                pe.wait_ge(q_ready, HEAD + (b + 1) * NT)
                            if pass_ == 1:
                                pe.wait_ge(x2_ready, HEAD + b * NT + t + 1)
                            mm((pz, py)[h][:], mean_w[:], tile(brf[0], t), start=True, stop=True).then_inc(mean_mm, 1)
                    with pe.Fori(0, NT // 2) as tp:
                        for h in range(2):
                            t = tp * 2 + h
                            e = (b * 2 + pass_) * NT + t
                            pe.wait_ge(ln_ready, HEAD + e - 1)
                            pe.wait_ge(squares_ready, HEAD + e + 1)
                            mm((pt, pyt)[h][:], mean_w[:], tile(brf[2], t), start=True, stop=True).then_inc(var_mm, 1)

                norm_tokens(0)
                with pe.Fori(0, NT // 2) as tp:
                    for h in range(2):
                        t = tp * 2 + h
                        pe.wait_ge(normed, HEAD + b * (2 * NT) + t + 1)
                        pe.wait_ge(kv_summed, HEAD + b * NT + t - 1)
                        mm(pd[:, h * TT:(h + 1) * TT], wqkv[:, 1, :], tile(brf[1], t), start=True, stop=True)
                        mm(px[:, h * TT:(h + 1) * TT], wqkv[:, 2, :], tile(brf[1], t), start=True, stop=True).then_inc(kv_mm, 1)
                with pe.Fori(0, NT // 2) as tp:
                    for h in range(2):
                        t = tp * 2 + h
                        pe.wait_ge(q_ready, HEAD + b * NT + t - 1)
                        mm((pz, py)[h][:], wqkv[:, 0, :], tile(brf[1], t), start=True, stop=True).then_inc(q_mm, 1)
                norm_tokens(1)
                pe.wait_ge(normed, HEAD + (b + 1) * (2 * NT))
                for s in range(L // P):
                    ins = mm(pz[:, s * NE:(s + 1) * NE], brf[1][:, s * P:(s + 1) * P], router[:], start=True, stop=True,
                             skip_group_check=True)
                ins.then_inc(logits_mm, 1)
                pe.wait_ge(gates_ready, b + 1)
                for t in range(NT):
                    if t >= 2:
                        pe.wait_ge(gates_copied, b * NT + t - 1)
                    for s in range(4):
                        ins = nc.tensor.transpose((pt, pyt)[t % 2][0:NE, s * P:(s + 1) * P],
                                                  gates[:, 0, 4 * t + s, :], ident[:])
                    ins.then_inc(gates_turned, 1)
                with pe.Fori(0, L // (2 * P)) as s2:
                    e = pe.snap(b * (L // P) + s2 * 2)
                    for h in range(2):
                        pe.wait_ge(xst_ready, HEAD + e + h + 1)
                        pe.wait_ge(weighed, HEAD + e + h - 1)
                        for half in range(2):
                            ins = mm((px, pd)[h][:, half * 512:(half + 1) * 512], xst[h],
                                     expert_w[:, 4 * half:4 * half + 4, :].rearrange("d e c -> d (e c)"),
                                     start=True, stop=True)
                        ins.then_inc(expert_mm, 1)
                    for h in range(2):
                        pe.wait_ge(weighed, HEAD + e + h + 1)
                        pe.wait_ge(out_ready, HEAD + e + h - 1)
                        pe.wait_ge(gates_copied, b * NT + NT)
                        o = (pz, py)[h][:, 0:P]
                        mm(o, expert_b[:], brf[2][0:NE, bass.ds(s2 * (2 * P) + h * P, P)], start=True, stop=False)
                        for x_ in range(NE):
                            ins = mm(o, mix[h][:, x_, :], ident[:], start=False, stop=(x_ == NE - 1))
                        ins.then_inc(comb_mm, 1)

        @block.scalar
        def _(act):
            af = nc.scalar.activation
            head_start(act, (dt_exp, cum_exp, pre_copied, conv_tanh_ready, bt_ready, xtok_ready, gm_ready, ebuf_ready,
                             squared, tz_ready, yts_ready, branch_copied, proj_copied, squares_ready, rstd_ready, k_ready,
                             q_ready, xst_ready, ln_ready, y5_ready))
            act.wait_ge(weights_in, 16 * len(loads))
            af(sel[:], selbase[:], ACT.Copy)
            af(ident_b[:], ident[:], ACT.Copy)
            af(never[:], after[:], ACT.Copy, scale=NEVER)
            af(nsel[:], selbase[:], ACT.Copy, scale=-1.0).then_inc(selectors_made, 1)
            af(par("A"), par("A"), ACT.Exp).then_inc(a_step, 1)

            def step_sizes(q):
                act.wait_ge(dtx_ready, HEAD + q + 1)
                act.wait_ge(lna_ready, HEAD + q)
                af(dte[:, 0, :], dtx[:], ACT.Relu)
                af(dte[:, 1, :], dtx[:], ACT.Abs).then_inc(abs_ready, 1)
                act.wait_ge(abs_ready, q + 1)
                af(dte[:, 2, :], dte[:, 1, :], ACT.Exp, scale=-1.0).then_inc(dt_exp, 1)

            def decay_factors(q, p):
                act.wait_ge(cum_mm, HEAD + q + 1)
                act.wait_ge(cum_ready, HEAD + q + 1)
                af(ec[p][:].rearrange("c a n -> c (a n)"), px[:, XS + GC:XS + 4 * GC], ACT.Exp).then_inc(cum_exp, 1)

            def copy_pre(k, i, b, xn):
                act.wait_ge(x_mm, HEAD + xn + b + 1)
                act.wait_ge(acc_ready, HEAD + xn - 1)
                o = pre[k % 2]
                af(o[:, :, 0:3], past[i][:], ACT.Copy)
                af(o[:, :, 3:3 + UT], px[:, 0:XS].rearrange("c (t n) -> c t n", t=XT), ACT.Copy).then_inc(pre_copied, 1)
                act.wait_ge(pre_copied, HEAD + xn + 1)
                af(past[i][:], o[:, :, UT:UT + 3], ACT.Copy).then_inc(past_kept, 1)

            def conv_tanh(k, xn):
                act.wait_ge(acc_ready, HEAD + xn + 1)
                act.wait_ge(xbc_ready, HEAD + xn)
                af(th[:], acc[k % 2], ACT.Tanh).then_inc(conv_tanh_ready, 1)

            def copy_b(k, xn):
                act.wait_ge(xbc_ready, HEAD + xn + 1)
                af(bt[k % 2][C, :], xbc[k % 2][0:DS, 2, :], ACT.Copy).then_inc(bt_ready, 1)

            with act.Fori(0, NB) as b:
                step_sizes(b * (NG + 1))
                act.wait_ge(hd_ready, HEAD + b * (NG * NBR * 2))
                decay_factors(b * (NG + 1), 0)
                copy_pre(0, 0, b, b * CONVS)
                conv_tanh(0, b * CONVS)
                copy_b(0, b * CONVS)

                def copy_tokens(j, m, q):
                    act.wait_ge(pairs_mm, HEAD + q + 1)
                    act.wait_ge(xd_ready, HEAD + m - 1)
                    act.wait_ge(dx_ready, HEAD + m - 1)
                    act.wait_ge(state_mm, HEAD + m - 1)
                    af(xtok[j][:], pt[:, 0:XT * P].rearrange("c (t n) -> c t n", t=XT), ACT.Copy).then_inc(xtok_ready, 1)
                    act.wait_ge(mix_ready, HEAD + m - 1)
                    af(gm[j][:], pt[:, XT * P:(XT + 1) * P], ACT.Copy).then_inc(gm_ready, 1)

                def decay_exp(m, q):
                    act.wait_ge(decay_mm, HEAD + q + 1)
                    act.wait_ge(mix_ready, HEAD + m)
                    af(ebuf[:].rearrange("c h t -> c (h t)"), pd[:], ACT.Exp).then_inc(ebuf_ready, 1)

                decay_exp(b * (NG * NBR * 2), b * AHEAD)
                copy_tokens(0, b * (NG * NBR * 2), b * AHEAD)
                with act.Fori(0, NG // BG) as gg:
                    u, c = act.snap(b * (NG * NBR) + gg * BU), act.snap(b * (NG * NBR * 2) + gg * 2 * BU)
                    x, a_ = act.snap(b * CONVS + gg * BU), act.snap(b * AHEAD + gg * 2 * BU)
                    g17 = act.snap(b * (NG + 1) + gg * BG)
                    g2 = act.snap(gg * BG)

                    def square(k, j, m):
                        act.wait_ge(y4_ready, HEAD + m + 1)
                        act.wait_ge(rs_ready, HEAD + u + k)
                        act.wait_ge(squared, HEAD + m)
                        af(sqj[:], y4[k % 2][:, j, :], ACT.Square, scale=DIN ** -0.5, accum_out=ss[:, j:j + 1]).then_inc(squared, 1)

                    def copy_turned(n):
                        act.wait_ge(yt_mm, HEAD + n + 1)
                        act.wait_ge(out_mm, HEAD + n)
                        af(yts[:].rearrange("c t n -> c (t n)"), pyt[:], ACT.Copy).then_inc(yts_ready, 1)

                    def store_branch(i, n, g):
                        act.wait_ge(out_mm, HEAD + n + 1)
                        pieces = scan_rows(i, pz[:, 0:UT].rearrange("c (r s) -> c r s", r=ROWS))
                        for rows, src in pieces:
                            ins = af(order(i, br[i][:], g)[:, rows, :], src, ACT.Copy)
                        ins.then_inc(branch_copied, 1)

                    def norm_outputs(k, n):
                        act.wait_ge(rs_ready, HEAD + n + 1)
                        act.wait_ge(yt_mm, HEAD + n)
                        for j in range(2):
                            ins = af(y5[:, j, :], y4[k % 2][:, j, :], ACT.Copy, scale=rs[:, j:j + 1])
                        ins.then_inc(y5_ready, 1)

                    for k in range(BU):
                        n, m = u + k, c + 2 * k
                        p, i = k // NBR, k % NBR
                        copy_pre(k + 1, (k + 1) % NBR, b, x + k + 1)
                        if k > 0:
                            square(k - 1, 1, m - 1)
                        copy_tokens(1, m + 1, a_ + 2 * k + 1)
                        if i == 3:
                            act.wait_ge(y2_ready, HEAD + m - 6)
                            act.wait_ge(hd_ready, HEAD + m - 6)
                            decay_factors(g17 + p + 1, 1 - p)
                        decay_exp(m + 1, a_ + 2 * k + 1)
                        if i == 2:
                            step_sizes(g17 + p + 1)
                        if k > 0:
                            norm_outputs(k - 1, n - 1)
                        act.wait_ge(z_mm, HEAD + n + 1)
                        act.wait_ge(zg_ready, HEAD + n)
                        af(tz[:].rearrange("c j d -> c (j d)"), pz[:], ACT.Tanh, scale=0.5).then_inc(tz_ready, 1)
                        if k > 0:
                            copy_turned(n - 1)
                        conv_tanh(k + 1, x + k + 1)
                        decay_exp(m + 2, a_ + 2 * k + 2)
                        copy_b(k + 1, x + k + 1)
                        copy_tokens(0, m + 2, a_ + 2 * k + 2)
                        if k > 0:
                            store_branch((k - 1) % NBR, n - 1, g2 + (k - 1) // NBR)
                        square(k, 0, m)
                    square(BU - 1, 1, c + 2 * BU - 1)
                    norm_outputs(BU - 1, u + BU - 1)
                    copy_turned(u + BU - 1)
                    store_branch(NBR - 1, u + BU - 1, g2 + BG - 1)

                act.wait_ge(branch_copied, HEAD + (b + 1) * (NG * NBR))
                act.wait_ge(local_ready, b + 1)
                af(brf[4], brf[4], ACT.Gelu_apprx_tanh, accum_out=sums[:, 0:1]).then_inc(sums_act, 1)
                for i in range(2):
                    af(brf[i], brf[i], ACT.Copy, accum_out=sums[:, i + 1:i + 2]).then_inc(sums_act, 1)
                act.wait_ge(se_step, b * SE_STEPS + 4)
                af(se[:, 20:22], se[:, 18:20], ACT.Gelu_apprx_tanh).then_inc(se_nonlin, 1)
                act.wait_ge(se_step, b * SE_STEPS + 7)
                af(se[:, 35:40], se[:, 30:35], ACT.Tanh, scale=0.5).then_inc(se_nonlin, 1)

                def tile(buf, t):
                    return buf[:, bass.ds(t * TT, TT)]

                with act.Fori(0, NT // 2) as tp:
                    for h in range(2):
                        t = tp * 2 + h
                        act.wait_ge(proj_mm, HEAD + b * NT + t + 1)
                        act.wait_ge(fused_ready, HEAD + b * NT + t + 1)
                        af(tile(brf[1], t), px[:, h * TT:(h + 1) * TT], ACT.Copy).then_inc(proj_copied, 1)
                act.wait_ge(affine_ready, b + 1)
                for q in range(4):
                    s = slice(q * L // 4, (q + 1) * L // 4)
                    af(brf[1][:, s], brf[1][:, s], ACT.Gelu_apprx_tanh, bias=gst[:, 12:13], scale=gst[:, 11:12]).then_inc(gelu_ready, 1)

                def norm_tokens(pass_):
                    with act.Fori(0, NT // 2) as tp:
                        for h in range(2):
                            t = tp * 2 + h
                            e = (b * 2 + pass_) * NT + t
                            act.wait_ge(centered, HEAD + e + 1)
                            af(tile(brf[2], t), tile(brf[1], t), ACT.Square).then_inc(squares_ready, 1)
                    with act.Fori(0, NT // 2) as tp:
                        for h in range(2):
                            t = tp * 2 + h
                            e = (b * 2 + pass_) * NT + t
                            act.wait_ge(var_mm, HEAD + e + 1)
                            act.wait_ge(rstd_ready, HEAD + e - 1)
                            af(lnb[h], (pt, pyt)[h][:], ACT.Ln, bias=eps[:, 0:1]).then_inc(ln_ready, 1)
                            act.wait_ge(ln_ready, HEAD + e + 1)
                            act.wait_ge(normed, HEAD + e - 1)
                            af(ks[h], lnb[h], ACT.Exp, scale=-0.5).then_inc(rstd_ready, 1)

                norm_tokens(0)
                with act.Fori(0, NT // 2) as tp:
                    for h in range(2):
                        t = tp * 2 + h
                        act.wait_ge(kv_mm, HEAD + b * NT + t + 1)
                        act.wait_ge(kv_summed, HEAD + b * NT + t - 1)
                        act.wait_ge(normed, HEAD + b * (2 * NT) + NT)
                        af(ks[h], pd[:, h * TT:(h + 1) * TT], ACT.Identity, bias=par("bk")).then_inc(k_ready, 1)
                with act.Fori(0, NT // 2) as tp:
                    for h in range(2):
                        t = tp * 2 + h
                        act.wait_ge(q_mm, HEAD + b * NT + t + 1)
                        act.wait_ge(kv_step, b * 2 + 2)
                        af(tile(brf[2], t), (pz, py)[h][:], ACT.Identity, bias=kvp[:, 9:10], scale=kvp[:, 8:9]).then_inc(q_ready, 1)
                norm_tokens(1)
                act.wait_ge(logits_step, b * 3 + 3)
                g_ = [gates[:, q, :, :].rearrange("c s e -> c (s e)") for q in range(4)]
                af(g_[0], g_[2], ACT.Exp).then_inc(gates_exp, 1)
                for t in range(NT):
                    act.wait_ge(gates_turned, b * NT + t + 1)
                    af(brf[2][0:NE, t * TT:(t + 1) * TT], (pt, pyt)[t % 2][0:NE, :], ACT.Copy).then_inc(gates_copied, 1)
                with act.Fori(0, L // (2 * P)) as s2:
                    e = act.snap(b * (L // P) + s2 * 2)
                    for h in range(2):
                        act.wait_ge(expert_mm, HEAD + e + h - 1)
                        af(xst[h], brf[1][:, bass.ds(s2 * (2 * P) + h * P, P)], ACT.Copy).then_inc(xst_ready, 1)

        @block.vector
        def _(dve):
            v = nc.vector
            head_start(dve, (image_done, dtx_ready, lna_ready, cum_ready, acc_ready, xbc_ready, mix_ready, xd_ready, state_ready,
                             y2_ready, zg_ready, fused_ready, centered, normed, kv_summed, x2_ready, weighed,
                             out_ready))
            v.memset(xp[:], 0.0)
            v.memset(eps[:], LN_EPS)
            dve.wait_ge(weights_in, 16 * len(loads))
            dve.wait_ge(pos_mm, 1)
            v.tensor_scalar(conv_w[:], conv_w[:], 0.5, None, ALU.mult)
            for i in range(NBR):
                for t in range(2):
                    v.tensor_scalar(w_out[:, i, t, :], w_out[:, i, t, :], norm_w[:, i, t:t + 1], None, ALU.mult)
            v.tensor_copy(pos[:, 0, :], pt[:, 0:HW])
            v.tensor_copy(pos[:, 1, :], pyt[:, 0:HW]).then_inc(params_scaled, 1)
            dve.wait_ge(params_scaled, 1)
            dve.wait_ge(a_step, 1)
            v.tensor_scalar(par("A"), par("A"), -1.0, None, ALU.mult).then_inc(a_step, 1)
            dve.wait_ge(a_step, 2)

            def step_bias(q):
                dve.wait_ge(dt_mm, HEAD + q + 1)
                dve.wait_ge(dt_exp, HEAD + q)
                v.tensor_tensor(dtx[:].rearrange("c (j n) -> c j n", j=2),
                                    px[:, XS:XS + GC].rearrange("c (j n) -> c j n", j=2),
                                    par("dtb").unsqueeze(1).broadcast_to([P, 2, NBR * NH]), ALU.add).then_inc(dtx_ready, 1)

            def softplus(q, p):
                dve.wait_ge(dt_exp, HEAD + q + 1)
                dve.wait_ge(cum_mm, HEAD + q)
                steps = len(LOG1P)
                e = dte[:, 2, :]
                v.tensor_scalar(dtp[:], e, LOG1P[-1], None, ALU.mult).then_inc(poly_step, 1)
                for r, cf in enumerate(LOG1P[-2::-1]):
                    dve.wait_ge(poly_step, q * steps + r + 1)
                    ins = v.scalar_tensor_tensor(dtp[:], dtp[:], cf, e, ALU.add, ALU.mult)
                    ins.then_inc(poly_step, 1)
                dve.wait_ge(poly_step, (q + 1) * steps)
                dt = wd[p][:, :, 0, :]
                v.tensor_tensor(dt, dtp[:].rearrange("c (u h) -> c u h", h=NH),
                                    dte[:, 0, :].rearrange("c (u h) -> c u h", h=NH), ALU.add).then_inc(log_step, 1)
                dve.wait_ge(log_step, q * 2 + 1)
                av = par("A").rearrange("c (i h) -> c i h", h=NH)
                for j in range(2):
                    ins = v.tensor_tensor(lna[:, j * 32:(j + 1) * 32].rearrange("c (i h) -> c i h", h=NH),
                                          wd[p][:, j * NBR:(j + 1) * NBR, 0, :], av, ALU.mult)
                ins.then_inc(log_step, 1)
                dve.wait_ge(log_step, q * 2 + 2)
                v.tensor_copy(lna3[:].rearrange("c j (a n) -> c j a n", a=3),
                                  lna[:].rearrange("c (j n) -> c j n", j=2).unsqueeze(2).broadcast_to([P, 2, 3, 32])).then_inc(lna_ready, 1)

            def split_sums(q, p):
                src = px[0:96, 2 * UT:3 * UT]
                base = q * 5
                dve.wait_ge(cum_mm, HEAD + q + 1)
                v.tensor_copy(cum[p][:], src).then_inc(part_step, 1)
                dve.wait_ge(part_step, base + 1)
                v.tensor_tensor(cr[:], src, cum[p][:], ALU.subtract).then_inc(part_step, 1)
                dve.wait_ge(part_step, base + 2)
                v.tensor_copy(cum[p][32:64, :], cr[32:64, :]).then_inc(part_step, 1)
                v.tensor_copy(cum[p][64:96, :], cr[64:96, :]).then_inc(part_step, 1)
                dve.wait_ge(part_step, base + 4)
                v.tensor_tensor(cr2[64:96, :], cr[64:96, :], cum[p][64:96, :], ALU.subtract).then_inc(part_step, 1)
                dve.wait_ge(part_step, base + 5)
                v.tensor_copy(cum[p][64:96, :], cr2[64:96, :]).then_inc(cum_ready, 1)

            def convolve(k, i, xn, taps):
                base = xn * (XT * (TAPS - 1))
                o = acc[k % 2]
                for r in taps:
                    for t in range(XT):
                        if r == 0:
                            dve.wait_ge(pre_copied, HEAD + xn + 1)
                            dve.wait_ge(xbc_ready, HEAD + xn - 1)
                            ins = v.tensor_scalar(o[:, t, :], pre[k % 2][:, t, 0:UT], conv_w[:, i, t, 0:1], None, ALU.mult)
                        else:
                            dve.wait_ge(tap_step, base + (r - 1) * XT + t + 1)
                            ins = v.scalar_tensor_tensor(o[:, t, :], pre[k % 2][:, t, r:r + UT], conv_w[:, i, t, r:r + 1],
                                                         o[:, t, :], ALU.mult, ALU.add)
                        if r < TAPS - 1:
                            ins.then_inc(tap_step, 1)
                if TAPS - 1 in taps:
                    ins.then_inc(acc_ready, 1)

            def silu(k, xn, m):
                dve.wait_ge(conv_tanh_ready, HEAD + xn + 1)
                dve.wait_ge(y_mm, HEAD + m)
                dve.wait_ge(bt_ready, HEAD + xn - 1)
                v.scalar_tensor_tensor(xbc[k % 2].rearrange("c t n -> c (t n)"),
                                           th[:].rearrange("c t n -> c (t n)"), 1.0,
                                           acc[k % 2].rearrange("c t n -> c (t n)"), ALU.add, ALU.mult).then_inc(xbc_ready, 1)

            with dve.Fori(0, NB) as b:
                dve.wait_ge(image_in, (b + 1) * 16)
                for i in range(NBR):
                    v.memset(state[i][:], 0.0)
                    v.memset(past[i][:], 0.0)
                v.tensor_tensor(interior[:, 0:HW, 0:HW], br[0][:], pos[:, 0, :].unsqueeze(2).broadcast_to([P, HW, HW]),
                                    ALU.add).then_inc(row_added, 1)
                dve.wait_ge(row_added, b + 1)
                v.tensor_tensor(interior[:, 0:HW, 0:HW], interior[:, 0:HW, 0:HW],
                                    pos[:, 1, :].unsqueeze(1).broadcast_to([P, HW, HW]), ALU.add).then_inc(xp_ready, 1)
                step_bias(b * (NG + 1))
                softplus(b * (NG + 1), 0)
                split_sums(b * (NG + 1), 0)
                convolve(0, 0, b * CONVS, range(TAPS))
                silu(0, b * CONVS, b * (NG * NBR * 2))
                with dve.Fori(0, NG // BG) as gg:
                    u, c = dve.snap(b * (NG * NBR) + gg * BU), dve.snap(b * (NG * NBR * 2) + gg * 2 * BU)
                    x, a_ = dve.snap(b * CONVS + gg * BU), dve.snap(b * AHEAD + gg * 2 * BU)
                    g17 = dve.snap(b * (NG + 1) + gg * BG)

                    def scale_tokens(k, j, m, q):
                        p, i = k // NBR, k % NBR
                        dve.wait_ge(xtok_ready, HEAD + q + 1)
                        dve.wait_ge(wd_ready, HEAD + g17 + p + 1)
                        dve.wait_ge(y_mm, HEAD + m - 1)
                        ji = j * NBR + i
                        v.tensor_tensor(
                            xd[j][:].rearrange("c q (h d) -> c q h d", h=NH),
                            xtok[j][:, 0:2, :].rearrange("c a (h d) -> c (a h) d", d=HD)
                            .unsqueeze(1).broadcast_to([P, 2, NH, HD]),
                            wd[p][:, ji, :, :].unsqueeze(3).broadcast_to([P, 2, NH, HD]), ALU.mult).then_inc(xd_ready, 1)

                    def mix_pairs(j, m, q):
                        dve.wait_ge(ebuf_ready, HEAD + q + 1)
                        dve.wait_ge(gm_ready, HEAD + q + 1)
                        dve.wait_ge(y_mm, HEAD + m - 1)
                        v.tensor_tensor(mix[j][:], ebuf[:], gm[j][:].unsqueeze(1)
                                            .broadcast_to([P, NH, P]), ALU.mult).then_inc(mix_ready, 1)

                    def update_state(i, j, m):
                        dve.wait_ge(state_mm, HEAD + m + 1)
                        dve.wait_ge(hd_ready, HEAD + m + 1)
                        v.tensor_tensor(state[i][C, 1 - j, :], hd[j][C, :], px[C, XS:XS + DIN], ALU.add).then_inc(state_ready, 1)

                    def add_outputs(k, j, m):
                        p, i = k // NBR, k % NBR
                        ji = j * NBR + i
                        dve.wait_ge(y_mm, HEAD + m + 1)
                        dve.wait_ge(y2_ready, HEAD + m)
                        v.tensor_tensor(y1[:].rearrange("c (h d) -> c h d", h=NH),
                                            py[:, DIN:2 * DIN].rearrange("c (h d) -> c h d", h=NH),
                                            ec[p][:, 0, ji * NH:(ji + 1) * NH].unsqueeze(2).broadcast_to([P, NH, HD]),
                                            ALU.mult).then_inc(y1_ready, 1)
                        dve.wait_ge(y1_ready, m + 1)
                        dve.wait_ge(y3_ready, m)
                        v.tensor_tensor(y2[:], y1[:], py[:, 0:DIN], ALU.add).then_inc(y2_ready, 1)

                    for k in range(BU):
                        n, m = u + k, c + 2 * k
                        p, i = k // NBR, k % NBR
                        mix_pairs(0, m, a_ + 2 * k)
                        scale_tokens(k, 0, m, a_ + 2 * k)
                        if i == 2:
                            step_bias(g17 + p + 1)
                        if i == 3:
                            split_sums(g17 + p + 1, 1 - p)
                        convolve(k + 1, (k + 1) % NBR, x + k + 1, (0, 1))
                        scale_tokens(k, 1, m + 1, a_ + 2 * k + 1)
                        mix_pairs(1, m + 1, a_ + 2 * k + 1)
                        add_outputs(k, 0, m)
                        update_state(i, 0, m)
                        convolve(k + 1, (k + 1) % NBR, x + k + 1, (2,))
                        update_state(i, 1, m + 1)
                        convolve(k + 1, (k + 1) % NBR, x + k + 1, (3,))
                        dve.wait_ge(tz_ready, HEAD + n + 1)
                        dve.wait_ge(y4_ready, HEAD + m - 2)
                        v.scalar_tensor_tensor(zg[k % 2][:].rearrange("c j d -> c (j d)"),
                                               tz[:].rearrange("c j d -> c (j d)"), 1.0, pz[:],
                                               ALU.add, ALU.mult).then_inc(zg_ready, 1)
                        silu(k + 1, x + k + 1, m)
                        add_outputs(k, 1, m + 1)
                        if i == 2:
                            softplus(g17 + p + 1, 1 - p)

                dve.wait_ge(branch_copied, HEAD + (b + 1) * (NG * NBR))
                dve.wait_ge(bt_ready, HEAD + (b + 1) * CONVS)
                dve.wait_ge(xp_ready, b + 1)
                v.tensor_scalar(br[4], xp[:, 0:HW, 0:HW], local_w[:, 0:1], None, ALU.mult).then_inc(local_step, 1)
                for r in range(1, 9):
                    dve.wait_ge(local_step, b * 8 + r)
                    dy, dx_ = r // 3, r % 3
                    ins = v.scalar_tensor_tensor(br[4], xp[:, dy:dy + HW, dx_:dx_ + HW], local_w[:, r:r + 1], br[4],
                                                 ALU.mult, ALU.add)
                    ins.then_inc(local_step if r < 8 else local_ready, 1)
                for i in range(2, 4):
                    v.tensor_reduce(sums[:, i + 1:i + 2], brf[i], AX.X, ALU.add).then_inc(sums_dve, 1)
                dve.wait_ge(desc_mm, b + 1)
                v.tensor_scalar(se[:, 0:5], pt[:, 0:5], 1.0 / (P * L), None, ALU.mult).then_inc(se_step, 1)
                dve.wait_ge(se_step, b * SE_STEPS + 1)
                v.tensor_tensor(se[:, 5:15].rearrange("c (a j) -> c a j", a=2),
                                    se[:, 0:5].unsqueeze(1).broadcast_to([P, 2, 5]),
                                    par("w1").rearrange("c (a j) -> c a j", a=2), ALU.mult).then_inc(se_step, 1)
                dve.wait_ge(se_step, b * SE_STEPS + 2)
                v.tensor_reduce(se[:, 15:17], se[:, 5:15].rearrange("c (a j) -> c a j", a=2), AX.X, ALU.add).then_inc(se_step, 1)
                dve.wait_ge(se_step, b * SE_STEPS + 3)
                v.tensor_tensor(se[:, 18:20], se[:, 15:17], par("b1"), ALU.add).then_inc(se_step, 1)
                dve.wait_ge(se_step, b * SE_STEPS + 4)
                dve.wait_ge(se_nonlin, b * 2 + 1)
                v.tensor_tensor(se[:, 5:15].rearrange("c (j a) -> c j a", a=2),
                                    se[:, 20:22].unsqueeze(1).broadcast_to([P, 5, 2]),
                                    par("w2").rearrange("c (j a) -> c j a", a=2), ALU.mult).then_inc(se_step, 1)
                dve.wait_ge(se_step, b * SE_STEPS + 5)
                v.tensor_reduce(se[:, 22:27], se[:, 5:15].rearrange("c (j a) -> c j a", a=2), AX.X, ALU.add).then_inc(se_step, 1)
                dve.wait_ge(se_step, b * SE_STEPS + 6)
                v.tensor_tensor(se[:, 30:35], se[:, 22:27], par("b2"), ALU.add).then_inc(se_step, 1)
                dve.wait_ge(se_step, b * SE_STEPS + 7)
                dve.wait_ge(se_nonlin, b * 2 + 2)
                v.tensor_scalar(sew[:], se[:, 35:40], 1.0, 0.5, ALU.add, ALU.mult).then_inc(se_ready, 1)

                def tile(buf, t):
                    return buf[:, bass.ds(t * TT, TT)]

                with dve.Fori(0, NT // 2) as tp:
                    for h in range(2):
                        t = tp * 2 + h
                        dve.wait_ge(se_ready, b + 1)
                        dve.wait_ge(proj_mm, HEAD + b * NT + t + 1)
                        dve.wait_ge(x_tile_in[h], (b * (NT // 2) + tp + 1) * 16)
                        out = tile(brf[0], t)
                        v.scalar_tensor_tensor(out, out, sew[:, 1:2], ks[h], ALU.mult, ALU.add).then_inc(fuse_step, 1)
                        for r, j in enumerate((1, 2, 3, 4)):
                            w = (j + 1) % 5
                            dve.wait_ge(fuse_step, (b * NT + t) * 4 + r + 1)
                            ins = v.scalar_tensor_tensor(out, tile(brf[j], t), sew[:, w:w + 1], out, ALU.mult, ALU.add)
                            ins.then_inc(fuse_step if r < 3 else fused_ready, 1)
                dve.wait_ge(proj_copied, HEAD + b * NT + NT)
                for t in range(NT):
                    ins = v.bn_stats(bnst[:, t, :], brf[1][:, t * TT:(t + 1) * TT])
                ins.then_inc(gn_step, 1)
                dve.wait_ge(gn_step, b * GN_STEPS + 1)
                v.memset(gst[:, 15:16], 0.0)
                v.bn_aggr(gst[:, 0:2], bnst[:]).then_inc(gn_step, 1)
                dve.wait_ge(gn_step, b * GN_STEPS + 2)
                v.tensor_copy(gst[:, 2:3], gst[:, 0:1])
                v.scalar_tensor_tensor(gst[:, 3:4], gst[:, 0:1], gst[:, 0:1], gst[:, 1:2], ALU.mult, ALU.add).then_inc(gn_step, 1)
                dve.wait_ge(gn_step, b * GN_STEPS + 3)
                dve.wait_ge(group_mm, b + 1)
                v.tensor_copy(gst[:, 5:6], pt[:, 8:9])
                v.tensor_scalar(gst[:, 6:7], pt[:, 9:10], GN_EPS, None, ALU.add).then_inc(norm_step, 1)
                dve.wait_ge(norm_step, b * 3 + 1)
                v.tensor_tensor(gst[:, 4:5], gst[:, 5:6], gst[:, 5:6], ALU.mult).then_inc(norm_step, 1)
                dve.wait_ge(norm_step, b * 3 + 2)
                v.tensor_tensor(gst[:, 7:8], gst[:, 6:7], gst[:, 4:5], ALU.subtract).then_inc(gn_step, 1)
                dve.wait_ge(gn_step, b * GN_STEPS + 4)
                dve.wait_ge(group_rsqrt, b + 1)
                v.tensor_tensor(gst[:, 11:12], gst[:, 8:9], par("gamma"), ALU.mult).then_inc(gn_step, 1)
                dve.wait_ge(gn_step, b * GN_STEPS + 5)
                v.tensor_tensor(gst[:, 13:14], gst[:, 5:6], gst[:, 11:12], ALU.mult).then_inc(norm_step, 1)
                dve.wait_ge(norm_step, b * 3 + 3)
                v.tensor_tensor(gst[:, 12:13], par("beta"), gst[:, 13:14], ALU.subtract).then_inc(affine_ready, 1)
                for q in range(4):
                    s = slice(q * L // 4, (q + 1) * L // 4)
                    dve.wait_ge(gelu_ready, b * 4 + q + 1)
                    v.tensor_tensor(brf[0][:, s], brf[0][:, s], brf[1][:, s], ALU.add).then_inc(x1_ready, 1)
                def norm_tokens(pass_):
                    with dve.Fori(0, NT // 2) as tp:
                        for h in range(2):
                            t = tp * 2 + h
                            e = (b * 2 + pass_) * NT + t
                            dve.wait_ge(mean_mm, HEAD + e + 1)
                            if pass_ == 0:
                                dve.wait_ge(x1_ready, b * 4 + 4)
                            v.tensor_tensor(tile(brf[1], t), tile(brf[0], t), (pz, py)[h][:], ALU.subtract).then_inc(centered, 1)
                    with dve.Fori(0, NT // 2) as tp:
                        for h in range(2):
                            t = tp * 2 + h
                            e = (b * 2 + pass_) * NT + t
                            dve.wait_ge(rstd_ready, HEAD + e + 1)
                            v.tensor_tensor(tile(brf[1], t), tile(brf[1], t), ks[h], ALU.mult).then_inc(normed, 1)

                norm_tokens(0)
                for t in range(NT):
                    h = t % 2
                    dve.wait_ge(kv_mm, HEAD + b * NT + t + 1)
                    dve.wait_ge(k_ready, HEAD + b * NT + t + 1)
                    if t >= 1:
                        dve.wait_ge(kv_summed, HEAD + b * NT + t)
                    v.scalar_tensor_tensor(dump, px[:, h * TT:(h + 1) * TT], par("bv"), ks[h], ALU.add, ALU.mult,
                                               accum_out=kvp[:, t:t + 1]).then_inc(kv_summed, 1)
                dve.wait_ge(kv_summed, HEAD + b * NT + NT)
                v.tensor_reduce(kvp[:, 8:9], kvp[:, 0:8], AX.X, ALU.add).then_inc(kv_step, 1)
                dve.wait_ge(kv_step, b * 2 + 1)
                v.tensor_tensor(kvp[:, 9:10], kvp[:, 8:9], par("bq"), ALU.mult).then_inc(kv_step, 1)
                with dve.Fori(0, NT // 2) as tp:
                    for h in range(2):
                        t = tp * 2 + h
                        dve.wait_ge(q_ready, HEAD + b * NT + t + 1)
                        v.tensor_tensor(tile(brf[0], t), tile(brf[0], t), tile(brf[2], t), ALU.add).then_inc(x2_ready, 1)
                norm_tokens(1)
                NS = L // P
                g3 = [gates[:, q, :, :] for q in range(4)]
                dve.wait_ge(logits_mm, b + 1)
                v.tensor_tensor(g3[1], pz[:, 0:NS * NE].rearrange("c (s e) -> c s e", e=NE),
                                    par("rb").unsqueeze(1).broadcast_to([P, NS, NE]), ALU.add).then_inc(logits_step, 1)
                dve.wait_ge(logits_step, b * 3 + 1)
                v.tensor_reduce(gmx[:], g3[1], AX.X, ALU.max).then_inc(logits_step, 1)
                dve.wait_ge(logits_step, b * 3 + 2)
                v.tensor_tensor(g3[2], g3[1], gmx[:].unsqueeze(2).broadcast_to([P, NS, NE]), ALU.subtract).then_inc(logits_step, 1)
                for q in range(4):
                    s = slice(q * NS // 4, (q + 1) * NS // 4)
                    n4 = NS // 4 * NE
                    le = g3[1][:, s, :].rearrange("c s e -> c (s e)").unsqueeze(2).broadcast_to([P, n4, NE])
                    for s_ in range(NS // 4):
                        sl = g3[1][:, q * NS // 4 + s_, :]
                        lj = sl.unsqueeze(1).broadcast_to([P, NE, NE])
                        li = sl.unsqueeze(2).broadcast_to([P, NE, NE])
                        v.tensor_tensor(rk[0][:, s_, :, :], lj, li, ALU.is_gt)
                        ins = v.tensor_tensor(rk[1][:, s_, :, :], lj, li, ALU.is_equal)
                    ins.then_inc(gate_step, 1)
                    dve.wait_ge(gate_step, b * GATE_STEPS + 4 * q + 1)
                    f = [rk[z].rearrange("c s e j -> c s (e j)") for z in range(2)]
                    v.tensor_tensor(f[1], f[1], par("lt").unsqueeze(1).broadcast_to([P, NS // 4, NE * NE]), ALU.mult).then_inc(gate_step, 1)
                    dve.wait_ge(gate_step, b * GATE_STEPS + 4 * q + 2)
                    v.tensor_tensor(f[0], f[0], f[1], ALU.add).then_inc(gate_step, 1)
                    dve.wait_ge(gate_step, b * GATE_STEPS + 4 * q + 3)
                    v.tensor_reduce(g3[3][:, s, :].rearrange("c s e -> c (s e)"),
                                        rk[0].rearrange("c s e j -> c (s e) j"), AX.X, ALU.add).then_inc(gate_step, 1)
                    dve.wait_ge(gate_step, b * GATE_STEPS + 4 * q + 4)
                dve.wait_ge(gates_exp, b + 1)
                v.scalar_tensor_tensor(g3[1].rearrange("c s e -> c (s e)"), g3[3].rearrange("c s e -> c (s e)"), 2.0,
                                           g3[0].rearrange("c s e -> c (s e)"), ALU.is_lt, ALU.mult).then_inc(gate_step, 1)
                dve.wait_ge(gate_step, b * GATE_STEPS + 16 + 1)
                v.tensor_reduce(gmx[:], g3[1], AX.X, ALU.add).then_inc(gate_step, 1)
                dve.wait_ge(gate_step, b * GATE_STEPS + 16 + 2)
                v.reciprocal(gmx[:], gmx[:]).then_inc(gate_step, 1)
                dve.wait_ge(gate_step, b * GATE_STEPS + 16 + 3)
                v.tensor_tensor(g3[0], g3[1], gmx[:].unsqueeze(2).broadcast_to([P, NS, NE]), ALU.mult).then_inc(gates_ready, 1)
                with dve.Fori(0, NS // 2) as s2:
                    e = dve.snap(b * NS + s2 * 2)

                    def weigh(h):
                        dve.wait_ge(gates_ready, b + 1)
                        dve.wait_ge(expert_mm, HEAD + e + h + 1)
                        dve.wait_ge(comb_mm, HEAD + e + h - 1)
                        v.tensor_tensor(mix[h][:], (px, pd)[h][:].rearrange("c (e n) -> c e n", e=NE),
                                            gates[:, 0, bass.ds(s2 * 2 + h, 1), :].rearrange("c o e -> c (o e)")
                                            .unsqueeze(2).broadcast_to([P, NE, P]), ALU.mult).then_inc(weighed, 1)

                    weigh(0)
                    weigh(1)
                    for h in range(2):
                        dve.wait_ge(comb_mm, HEAD + e + h + 1)
                        cols = bass.ds(s2 * (2 * P) + h * P, P)
                        v.tensor_tensor(brf[3][:, cols], brf[0][:, cols], (pz, py)[h][:, 0:P], ALU.add).then_inc(out_ready, 1)
                dve.wait_ge(out_ready, HEAD + (b + 1) * NS)
                v.memset(y1[:, 0:1], 0.0).then_inc(image_done, 1)


def kernel(**inputs):
    import concourse.bacc as _bacc
    from concourse.bass_utils import run_bass_kernel_spmd as _run

    f32 = np.float32
    pre = "L0_conv_"
    w = {k: np.ascontiguousarray(v) for k, v in inputs.items()}
    half = P // 2
    dim_t = 10000.0 ** (np.arange(0, half, 2, dtype=f32) / half)
    ang = np.arange(HW, dtype=f32)[:, None] / dim_t
    emb = np.stack([np.sin(ang), np.cos(ang)], 2).reshape(HW, -1).T.astype(f32)
    r = np.arange(P)
    c_sel = np.tile(np.eye(NBR * NH, dtype=f32), (3, 1))
    lower = (np.arange(NE)[None, :] < np.arange(NE)[:, None]).astype(f32).reshape(-1)
    rows = [w[pre + "A_log"].reshape(-1), w[pre + "dt_bias"].reshape(-1), w[pre + "Dp"].reshape(-1),
            w[pre + "se_w1"].T.reshape(-1), w[pre + "se_b1"], w[pre + "se_w2"].T.reshape(-1), w[pre + "se_b2"],
            w["L1_ffn_router_b"], lower]
    cols = [w[pre + "gn_gamma"], w[pre + "gn_beta"], w["L1_attn_bq"], w["L1_attn_bk"], w["L1_attn_bv"]]
    small = np.concatenate([np.broadcast_to(np.concatenate(rows), (P, sum(x.size for x in rows))),
                            np.stack(cols, 1)], 1)
    arrays = {
        "x": w["x"].reshape(NB, P, L),
        "c_ident": np.eye(P, dtype=f32),
        "c_upto": (r[:, None] <= r[None, :]).astype(f32),
        "c_after": (r[:, None] > r[None, :]).astype(f32),
        "c_group": (r[:, None] // 16 == r[None, :] // 16).astype(f32) / f32(16),
        "c_sel": c_sel,
        "c_pos": np.concatenate([emb, emb]),
        "small": small,
        "w_in": w[pre + "W_in"],
        "conv_w": w[pre + "conv_w"].reshape(NBR, TAPS, XT, P).transpose(3, 0, 2, 1),
        "w_out": w[pre + "W_out"].reshape(NBR, DIN, P),
        "norm_w": w[pre + "norm_w"].reshape(NBR, 2, P).transpose(2, 0, 1),
        "proj_w": w[pre + "proj_w"].T,
        "pos_w": w[pre + "pos_proj_w"].T,
        "local_w": w[pre + "local_w"].reshape(P, 9),
        "wq": w["L1_attn_Wq"], "wk": w["L1_attn_Wk"], "wv": w["L1_attn_Wv"],
        "router": w["L1_ffn_router_w"], "expert_w": w["L1_ffn_expert_w"], "expert_b": w["L1_ffn_expert_b"],
    }
    arrays = {k: np.ascontiguousarray(v) for k, v in arrays.items()}
    nc = _bacc.Bacc("TRN2", target_bir_lowering=False, num_devices=1)
    aps = {k: nc.dram_tensor(f"in_{k}", v.shape, mybir.dt.from_np(v.dtype), kind="ExternalInput").ap()
           for k, v in arrays.items()}
    aps["out"] = nc.dram_tensor("out_0", (NB, P, L), F32, kind="ExternalOutput").ap()
    hybrid_kernel(nc, aps)
    res = _run(nc, [{f"in_{k}": v for k, v in arrays.items()}], core_ids=[0])
    return res.results[0]["out_0"].reshape(NB, P, HW, HW)
```

```python
from contextlib import ExitStack

import numpy as np

import concourse.bass as bass
from concourse import mybir

F32 = mybir.dt.float32
BF16 = mybir.dt.bfloat16
ALU = mybir.AluOpType
ACT = mybir.ActivationFunctionType
AX = mybir.AxisListType

P = 128
NB = 8
HW = 64
L = HW * HW
NBR = 4
DIN, DS, NH, HD = 256, 64, 8, 32
TAPS = 4
XT = 3
Q = 128
UT = 2 * Q
ROWS = UT // HW
NG = L // UT
BG = 2
BU = BG * NBR
ROWF = HW + 6
HEAD = 4
NE = 8
TT = 512
NT = L // TT
NEVER = -1e30
LN_EPS, GN_EPS = 1e-5, 1e-5
CONVS = NG * NBR + 2
SILUS = NG * NBR + 1
AHEAD = 2 * NG * NBR + 1
GC = 2 * NBR * NH
SE_STEPS, GN_STEPS, GATE_STEPS = 7, 5, 14
TROW = TT // HW

LOG1P = [0.9999999991556807, -0.499999794913725, 0.33332497543045325, -0.24986496454167328, 0.19885820254416264,
         -0.16087622903223123, 0.12377995638908859, -0.0818804061299571, 0.041006571120306035,
         -0.013187825375511738, 0.0019866963583891365]


def hybrid_kernel(nc, a):
    with ExitStack() as ctx:
        def sb(name, shape, dt=F32):
            return ctx.enter_context(nc.sbuf_tensor(name, shape, dt))

        def sem(name):
            return ctx.enter_context(nc.semaphore(name))

        ident = sb("ident", [P, P])
        upto = sb("upto", [P, P])
        after = sb("after", [P, P])
        ones = sb("ones", [P, P])
        mean_w = sb("mean_w", [P, P])
        group_avg = sb("group_avg", [P, P])
        selbase = sb("selbase", [96, 32])
        sel = sb("sel", [96, 32], BF16)
        ident_b = sb("ident_b", [P, P], BF16)
        never = sb("never", [P, P], BF16)
        nsel = sb("nsel", [96, 32], BF16)
        small = sb("small", [P, 256])
        w_in = sb("w_in", [P, NBR, 648])
        conv_w = sb("conv_w", [P, NBR, XT, TAPS])
        w_out = sb("w_out", [P, NBR, 2, P])
        norm_w = sb("norm_w", [P, NBR, 2])
        proj_w = sb("proj_w", [P, 5, P])
        wqkv = sb("wqkv", [P, 3, P])
        router = sb("router", [P, NE])
        expert_b = sb("expert_b", [NE, P])
        pos_t = sb("pos_t", [P, HW])
        pos_w = sb("pos_w", [P, P])
        pos = sb("pos", [P, 2, HW])
        local_w = sb("local_w", [P, 9])
        at = {}
        col = 0
        for name, n in (("A", 32), ("dtb", 32), ("Dp", 32), ("w1", 10), ("b1", 2), ("w2", 10), ("b2", 5), ("rb", NE),
                        ("first", NE), ("gamma", 1), ("beta", 1), ("bq", 1), ("bk", 1), ("bv", 1)):
            at[name] = (col, col + n)
            col += n
        assert col <= 256

        def par(name):
            return small[:, at[name][0]:at[name][1]]

        xp = sb("xp", [P, ROWF, ROWF])
        arena = sb("arena", [P, L])
        br = [sb(f"br{i}", [P, HW, HW]) for i in range(NBR)] + [arena[:].rearrange("c (h w) -> c h w", h=HW)]
        brf = [(t if t is br[4] else t[:]).rearrange("c h w -> c (h w)") for t in br]
        ust = [[sb(f"ust{p}{i}", [P, UT]) for i in range(NBR)] for p in range(2)]
        pre = [sb(f"pre{i}", [P, XT, 3 + UT]) for i in range(2)]
        past = [sb(f"past{i}", [P, XT, 3]) for i in range(NBR)]
        acc = [arena[:, i * XT * UT:(i + 1) * XT * UT].rearrange("c (t n) -> c t n", t=XT) for i in range(2)]
        th = sb("th", [P, XT, UT])
        xbc = [arena[:, i * XT * UT:(i + 1) * XT * UT].rearrange("c (t n) -> c t n", t=XT) for i in range(2, 4)]
        bt = [arena[:, 3072 + i * UT:3072 + (i + 1) * UT] for i in range(2)]
        xtok = [sb(f"xtok{i}", [P, XT, P]) for i in range(2)]
        ebuf = sb("ebuf", [P, NH, P])
        gm = [sb(f"gm{i}", [P, P]) for i in range(2)]
        mix = [sb(f"mix{i}", [P, NH, P]) for i in range(2)]
        xd = [sb(f"xd{i}", [P, 2, DIN]) for i in range(2)]
        dx = [sb(f"dx{i}", [P, DIN]) for i in range(2)]
        state = [sb(f"state{i}", [P, 2, DIN]) for i in range(NBR)]
        hd = [arena[:, 3584 + i * UT:3584 + (i + 1) * UT] for i in range(2)]
        y1 = sb("y1", [P, DIN])
        y2 = sb("y2", [P, DIN])
        y3 = sb("y3", [P, DIN])
        y4 = [sb(f"y4{i}", [P, 2, DIN]) for i in range(2)]
        sqj = sb("sqj", [P, DIN])
        ss = sb("ss", [P, 2])
        sv = sb("sv", [P, 2])
        rs = sb("rs", [P, 2])
        mhalf = sb("mhalf", [P, 2])
        epsy = sb("epsy", [P, 2])
        tz = sb("tz", [P, 2, DIN])
        zg = [sb(f"zg{i}", [P, 2, DIN]) for i in range(2)]
        y5 = sb("y5", [P, 2, DIN])
        yts = sb("yts", [P, 2, UT])
        dtx = sb("dtx", [P, GC])
        dte = sb("dte", [P, 3, GC])
        dtp = sb("dtp", [P, GC])
        lna = sb("lna", [P, GC])
        ec = [sb(f"ec{i}", [P, 3, GC]) for i in range(2)]
        wd = [sb(f"wd{i}", [P, 2 * NBR, 2, NH]) for i in range(2)]
        cum = [sb(f"cum{i}", [96, UT], BF16) for i in range(2)]
        cr = sb("cr", [96, UT])
        cr2 = sb("cr2", [96, UT])
        sums = sb("sums", [P, 8])
        bnst = sb("bnst", [P, NT, 6])
        gst = sb("gst", [P, 16])
        se = sb("se", [P, 40])
        sew = sb("sew", [P, 5])
        gmx = sb("gmx", [P, 4, L // P])
        eps = sb("eps", [P, 1])
        kvp = sb("kvp", [P, 16])
        expert_w = sb("expert_w", [P, NE, P])
        lna3 = sb("lna3", [P, 2, 96])
        ks = [zg[i][:].rearrange("c j d -> c (j d)") for i in range(2)]
        dump = tz[:].rearrange("c j d -> c (j d)")
        gates = ebuf[:].rearrange("c a (s e) -> c (a s) e", e=NE).rearrange("c (q s) e -> c q s e", q=4)
        xst = [y5[:, i, 0:P] for i in range(2)]
        top = [mix[0][:].rearrange("c e n -> c (e n)")[:, i * (L // P) * NE:(i + 1) * (L // P) * NE]
               .rearrange("c (s e) -> c s e", e=NE) for i in range(4)]
        half_sum = [y4[i][:].rearrange("c j (e n) -> c (j e) n", n=P) for i in range(2)]
        quarter_sum = [y[:].rearrange("c (e n) -> c e n", n=P) for y in (y2, y3)]
        C = slice(DS, P)

        def bank(name, n=1):
            return ctx.enter_context(nc.psum_tensor(name, [P, 512 * n], F32))
        px = bank("px", 2)
        pz = bank("pz")
        pd = bank("pd", 2)
        py = bank("py")
        pt = bank("pt")
        pyt = bank("pyt")
        XS = XT * UT

        x_tile_in = [sem("x_tile_in0"), sem("x_tile_in1")]
        pool_set, image_begun, row_added, local_step, fuse_step, norm_step = (sem(n) for n in
            ("pool_set", "image_begun", "row_added", "local_step", "fuse_step", "norm_step"))
        weights_in, pos_mm, params_scaled, selectors_made, a_step, image_in = (sem(n) for n in
            ("weights_in", "pos_mm", "params_scaled", "selectors_made", "a_step", "image_in"))
        xp_ready, local_ready, image_done, out_stored, abs_ready, log_step = (sem(n) for n in
            ("xp_ready", "local_ready", "image_done", "out_stored", "abs_ready", "log_step"))
        poly_step, part_step, past_kept, tap_step, y1_ready, y3_ready = (sem(n) for n in
            ("poly_step", "part_step", "past_kept", "tap_step", "y1_ready", "y3_ready"))
        sv_ready, sums_act, sums_dve, desc_mm, se_step, se_nonlin = (sem(n) for n in
            ("sv_ready", "sums_act", "sums_dve", "desc_mm", "se_step", "se_nonlin"))
        se_ready, gn_step, group_mm, group_rsqrt, affine_ready, gelu_ready = (sem(n) for n in
            ("se_ready", "gn_step", "group_mm", "group_rsqrt", "affine_ready", "gelu_ready"))
        x1_ready, kv_step, logits_mm, logits_step, gate_step, gates_exp = (sem(n) for n in
            ("x1_ready", "kv_step", "logits_mm", "logits_step", "gate_step", "gates_exp"))
        gates_ready, gates_turned, gates_copied = (sem(n) for n in
            ("gates_ready", "gates_turned", "gates_copied"))
        staged, wd_ready, dx_ready, hd_ready, y4_ready, rs_ready = (sem(n) for n in
            ("staged", "wd_ready", "dx_ready", "hd_ready", "y4_ready", "rs_ready"))
        dt_mm, cum_mm, x_mm, pairs_mm, decay_mm = (sem(n) for n in
            ("dt_mm", "cum_mm", "x_mm", "pairs_mm", "decay_mm"))
        y_mm, state_mm, z_mm, yt_mm, out_mm, proj_mm = (sem(n) for n in
            ("y_mm", "state_mm", "z_mm", "yt_mm", "out_mm", "proj_mm"))
        mean_mm, var_mm, kv_mm, q_mm, expert_mm, comb_mm = (sem(n) for n in
            ("mean_mm", "var_mm", "kv_mm", "q_mm", "expert_mm", "comb_mm"))
        dt_exp, cum_exp, pre_copied, conv_tanh_ready, bt_ready, xtok_ready = (sem(n) for n in
            ("dt_exp", "cum_exp", "pre_copied", "conv_tanh_ready", "bt_ready", "xtok_ready"))
        gm_ready, ebuf_ready, squared, tz_ready, yts_ready, branch_copied = (sem(n) for n in
            ("gm_ready", "ebuf_ready", "squared", "tz_ready", "yts_ready", "branch_copied"))
        proj_copied, squares_ready, rstd_ready, k_ready, q_ready, xst_ready = (sem(n) for n in
            ("proj_copied", "squares_ready", "rstd_ready", "k_ready", "q_ready", "xst_ready"))
        ln_ready, half_ready, quarter_ready, y5_ready, tap0_ready = (sem(n) for n in
            ("ln_ready", "half_ready", "quarter_ready", "y5_ready", "tap0_ready"))
        dtx_ready, lna_ready, cum_ready, acc_ready, xbc_ready, mix_ready = (sem(n) for n in
            ("dtx_ready", "lna_ready", "cum_ready", "acc_ready", "xbc_ready", "mix_ready"))
        xd_ready, state_ready, y2_ready, zg_ready, fused_ready = (sem(n) for n in
            ("xd_ready", "state_ready", "y2_ready", "zg_ready", "fused_ready"))
        centered, normed, kv_summed, x2_ready, weighed, out_ready = (sem(n) for n in
            ("centered", "normed", "kv_summed", "x2_ready", "weighed", "out_ready"))

        def head_start(eng, guards):
            for guard in guards:
                eng.sem_inc(guard, HEAD)

        def order(i, image, g):
            if i % 2 == 0:
                return image[:, bass.ds(g * ROWS, ROWS), 0:HW]
            return image[:, 0:HW, bass.ds(g * ROWS, ROWS)].rearrange("c s r -> c r s")

        def scan_rows(i, seq):
            if i < 2:
                return [(slice(0, ROWS), seq)]
            return [(slice(0, ROWS, 2), seq[:, 0:ROWS:2, :]), (slice(1, ROWS, 2), seq[:, 1:ROWS:2, ::-1])]

        interior = xp[:, 1:ROWF, 1:ROWF]
        loads = [
            (ident[:], a["c_ident"]), (upto[:], a["c_upto"]), (after[:], a["c_after"]),
            (group_avg[:], a["c_group"]), (selbase[:], a["c_sel"]), (pos_t[:], a["c_pos"]),
            (small[:, 0:col], a["small"]), (w_in[:], a["w_in"].rearrange("i c n -> c i n")),
            (conv_w[:], a["conv_w"]), *[(w_out[:, i, :, :], a["w_out"][i].rearrange("(k c) n -> c k n", k=2)) for i in range(NBR)],
            (norm_w[:], a["norm_w"]), (proj_w[:], a["proj_w"].rearrange("(j i) o -> i j o", j=5)),
            (wqkv[:, 0, :], a["wq"]), (wqkv[:, 1, :], a["wk"]), (wqkv[:, 2, :], a["wv"]),
            (router[:], a["router"]), (expert_b[:], a["expert_b"]), (pos_w[:], a["pos_w"]), (local_w[:], a["local_w"]),
            (expert_w[:], a["expert_w"].rearrange("e d c -> d e c")),
        ]
        block = ctx.enter_context(nc.Block())

        @block.sync
        def _(sp):
            head_start(sp, (out_stored,))
            for dst, src in loads:
                sp.dma_start(dst, src).then_inc(weights_in, 16)
            with sp.Fori(0, NB) as b:
                sp.wait_ge(image_done, HEAD + b)
                sp.wait_ge(out_stored, HEAD + b * 16 * (L // (2 * P)))
                sp.dma_start(brf[0], a["x"][bass.ds(b, 1)].rearrange("o c n -> (o c) n")).then_inc(image_in, 16)
                with sp.Fori(0, NT // 2) as tp:
                    for h in range(2):
                        t = tp * 2 + h
                        sp.wait_ge(se_ready, b + 1)
                        sp.wait_ge(fused_ready, HEAD + b * NT + t - 1)
                        sp.dma_start(ks[h], a["x"][bass.ds(b, 1), :, bass.ds(t * TT, TT)]
                                     .rearrange("o c n -> (o c) n")).then_inc(x_tile_in[h], 16)
                with sp.Fori(0, L // (2 * P)) as sp2:
                    sp.wait_ge(out_ready, HEAD + b * (L // P) + sp2 * 2 + 2)
                    sp.dma_start(a["out"][bass.ds(b, 1), :, bass.ds(sp2 * 2 * P, 2 * P)]
                                 .rearrange("o c n -> (o c) n"),
                                 brf[3][:, bass.ds(sp2 * 2 * P, 2 * P)]).then_inc(out_stored, 16)
            sp.wait_ge(out_stored, HEAD + NB * 16 * (L // (2 * P)))

        @block.gpsimd
        def _(pool):
            head_start(pool, (staged, wd_ready, dx_ready, hd_ready, y4_ready, rs_ready, half_ready))
            pool.memset(ones[:], 1.0)
            pool.memset(mean_w[:], 1.0 / P)
            pool.memset(epsy[:], 4e-5)
            pool.memset(mhalf[:], -0.5).then_inc(pool_set, 1)
            pool.wait_ge(weights_in, 16 * len(loads))
            pool.wait_ge(pool_set, 1)

            def stage(b, g, i, p):
                pieces = scan_rows(i, ust[p][i][:].rearrange("c (r s) -> c r s", r=ROWS))
                for k, (rows, dst) in enumerate(pieces):
                    ins = pool.tensor_copy(dst, order(i, interior, g)[:, rows, :])
                ins.then_inc(staged, 1)

            with pool.Fori(0, NB) as b:
                pool.wait_ge(xp_ready, b + 1)
                pool.tensor_tensor(sv[:], epsy[:], epsy[:], ALU.mult).then_inc(image_begun, 1)
                for i in range(NBR):
                    pieces = scan_rows(i, ust[0][i][:].rearrange("c (r s) -> c r s", r=ROWS))
                    src = (interior[:, 0:ROWS, 0:HW] if i % 2 == 0 else
                           interior[:, 0:HW, 0:ROWS].rearrange("c s r -> c r s"))
                    for rows, dst in pieces:
                        ins = pool.tensor_copy(dst, src[:, rows, :])
                    ins.then_inc(staged, 1)
                pool.wait_ge(cum_exp, HEAD + b * (NG + 1) + 1)
                pool.tensor_tensor(wd[0][:, :, 1, :], ec[0][:, 1, :].rearrange("c (u h) -> c u h", h=NH),
                                       wd[0][:, :, 0, :], ALU.mult).then_inc(wd_ready, 1)

                def y34(n, m, j, k):
                    pool.wait_ge(y2_ready, HEAD + m + 1)
                    pool.wait_ge(y4_ready, HEAD + m)
                    pool.wait_ge(dx_ready, HEAD + m + 1)
                    pool.tensor_tensor(y3[:], y2[:], dx[j][:], ALU.add).then_inc(y3_ready, 1)
                    pool.wait_ge(y3_ready, m + 1)
                    pool.wait_ge(zg_ready, HEAD + n + 1)
                    pool.wait_ge(y5_ready, HEAD + n - 1)
                    pool.tensor_tensor(y4[k % 2][:, j, :], y3[:], zg[k % 2][:, j, :], ALU.mult).then_inc(y4_ready, 1)

                def norm_factor(n):
                    pool.wait_ge(squared, HEAD + 2 * n + 2)
                    pool.wait_ge(y5_ready, HEAD + n)
                    pool.tensor_tensor(sv[:], ss[:], epsy[:], ALU.add).then_inc(sv_ready, 1)
                    pool.wait_ge(sv_ready, n + 1)
                    pool.tensor_tensor(rs[:], sv[:], mhalf[:], ALU.pow).then_inc(rs_ready, 1)

                with pool.Fori(0, NG // BG) as gg:
                    u, c = pool.snap(b * (NG * NBR) + gg * BU), pool.snap(b * (NG * NBR * 2) + gg * 2 * BU)
                    a_ = pool.snap(b * AHEAD + gg * 2 * BU)
                    g17, g2 = pool.snap(b * (NG + 1) + gg * BG), pool.snap(gg * BG)
                    def skip_term(j, m, t):
                        pool.wait_ge(xtok_ready, HEAD + t + 1)
                        pool.wait_ge(y4_ready, HEAD + m - 1)
                        pool.tensor_tensor(
                            dx[j][:].rearrange("c (h d) -> c h d", h=NH),
                            xtok[j][:, 0:2, :].rearrange("c a (h d) -> c (a h) d", d=HD),
                            par("Dp")[:, i * NH:(i + 1) * NH].unsqueeze(2).broadcast_to([P, NH, HD]),
                            ALU.mult).then_inc(dx_ready, 1)

                    def decay_state(j, m):
                        pool.wait_ge(cum_exp, HEAD + g17 + p + 1)
                        pool.wait_ge(state_ready, HEAD + (m - 1 if j == 0 else m))
                        dec = ec[p][:, 2, (j * NBR + i) * NH:(j * NBR + i + 1) * NH]
                        pool.tensor_tensor(
                            hd[j].rearrange("c (h d) -> c h d", h=NH),
                            state[i][:, j, :].rearrange("c (h d) -> c h d", h=NH),
                            dec.unsqueeze(2).broadcast_to([P, NH, HD]), ALU.mult).then_inc(hd_ready, 1)

                    for k in range(BU):
                        i, p = k % NBR, k // NBR
                        n, m = u + k, c + 2 * k
                        decay_state(0, m)
                        if k > 0:
                            y34(n - 1, m - 1, 1, k - 1)
                        skip_term(0, m, a_ + 2 * k)
                        if k > 0:
                            norm_factor(n - 1)
                        if i == 0:
                            pool.wait_ge(z_mm, HEAD + n)
                        skip_term(1, m + 1, a_ + 2 * k + 1)
                        decay_state(1, m + 1)
                        if i < 2:
                            for q in (2 * i, 2 * i + 1):
                                stage(b, g2 + p + 1, q, 1 - p)
                        if i == 3:
                            pool.wait_ge(cum_exp, HEAD + g17 + p + 2)
                            pool.wait_ge(xd_ready, HEAD + m - 6)
                            w = 1 - p
                            pool.tensor_tensor(
                                wd[w][:, :, 1, :], ec[w][:, 1, :].rearrange("c (u h) -> c u h", h=NH),
                                wd[w][:, :, 0, :], ALU.mult).then_inc(wd_ready, 1)
                        y34(n, m, 0, k)
                    y34(u + BU - 1, c + 2 * BU - 1, 1, BU - 1)
                    norm_factor(u + BU - 1)
                pool.wait_ge(gn_step, b * GN_STEPS + 4)
                pool.tensor_tensor(gst[:, 8:9], gst[:, 7:8], mhalf[:, 0:1], ALU.pow).then_inc(group_rsqrt, 1)
                with pool.Fori(0, L // (2 * P)) as s2:
                    e = pool.snap(b * (L // P) + s2 * 2)
                    for h in range(2):
                        pool.wait_ge(weighed, HEAD + e + h + 1)
                        pool.wait_ge(quarter_ready, HEAD + e + h - 1)
                        pool.tensor_tensor(half_sum[h], mix[h][:, 0:4, :], mix[h][:, 4:8, :], ALU.add).then_inc(half_ready, 1)

        @block.tensor
        def _(pe):
            mm = nc.tensor.matmul
            head_start(pe, (dt_mm, cum_mm, x_mm, pairs_mm, decay_mm, y_mm, state_mm, z_mm, yt_mm, out_mm,
                            proj_mm, mean_mm, var_mm, kv_mm, q_mm, expert_mm, comb_mm))
            pe.wait_ge(weights_in, 16 * len(loads))
            mm(pt[:, 0:HW], pos_w[0:DS, :], pos_t[0:DS, :], start=True, stop=True)
            mm(pyt[:, 0:HW], pos_w[DS:P, :], pos_t[DS:P, :], start=True, stop=True).then_inc(pos_mm, 1)
            pe.wait_ge(selectors_made, 1)

            def project_steps(p):
                for j in range(2):
                    for i in range(NBR):
                        o = XS + (j * NBR + i) * NH
                        ins = mm(px[:, o:o + NH], ust[p][i][:, j * Q:(j + 1) * Q], w_in[:, i, 640:648],
                                 start=True, stop=True, skip_group_check=True)
                ins.then_inc(dt_mm, 1)

            def sum_decays(p):
                for q, w in enumerate((upto, after, ones)):
                    mm(px[:, XS + GC * (q + 1):XS + GC * (q + 2)], w[:], lna[:], start=True, stop=True,
                       skip_group_check=True)
                for j in range(2):
                    rows = lna3[:, j, :]
                    ins = mm(px[0:96, 2 * UT + j * Q:2 * UT + (j + 1) * Q], rows, upto[:], start=True, stop=True,
                             skip_group_check=True)
                ins.then_inc(cum_mm, 1)

            def project_x(i, p):
                for t in range(XT):
                    ins = mm(px[:, t * UT:(t + 1) * UT], w_in[:, i, DIN + t * P:DIN + (t + 1) * P], ust[p][i][:],
                             start=True, stop=True, skip_group_check=True)
                ins.then_inc(x_mm, 1)

            with pe.Fori(0, NB) as b:
                pe.wait_ge(xp_ready, b + 1)
                pe.wait_ge(staged, HEAD + (b * (NG + 1) + 1) * NBR)
                project_steps(0)
                pe.wait_ge(lna_ready, HEAD + b * (NG + 1) + 1)
                sum_decays(0)
                pe.wait_ge(cum_exp, HEAD + b * (NG + 1) + 1)
                pe.wait_ge(cum_ready, HEAD + b * (NG + 1) + 1)
                project_x(0, 0)

                def decays(k, j, g, q):
                    p, i = k // NBR % 2, k % NBR
                    pe.wait_ge(cum_ready, HEAD + g + k // NBR + 1)
                    pe.wait_ge(ebuf_ready, HEAD + q)
                    part = cum[p][:, j * Q:(j + 1) * Q]
                    for half in range(2):
                        r = i * NH + half * 4
                        mm(pd[:, half * 512:(half + 1) * 512], ident_b[:], never[:].unsqueeze(1).broadcast_to([P, 4, P]),
                           start=True, stop=False, skip_group_check=True)
                        mm(pd[:, half * 512:(half + 1) * 512], part, nsel[:, r:r + 4].unsqueeze(2).broadcast_to([96, 4, P]),
                           start=False, stop=False, skip_group_check=True)
                        for h in range(4):
                            ins = mm(pd[:, half * 512 + h * Q:half * 512 + (h + 1) * Q],
                                     sel[:, r + h:r + h + 1].broadcast_to([96, P]), part,
                                     start=False, stop=(h == 3), skip_group_check=True)
                    ins.then_inc(decay_mm, 1)

                def turn_and_pair(k, j, v_, q):
                    pe.wait_ge(xbc_ready, HEAD + v_ + k + 1)
                    pe.wait_ge(xtok_ready, HEAD + q)
                    pe.wait_ge(gm_ready, HEAD + q)
                    for t in range(XT):
                        nc.tensor.transpose(pt[:, t * P:(t + 1) * P], xbc[k % 2][:, t, j * Q:(j + 1) * Q], ident[:])
                    pe.wait_ge(bt_ready, HEAD + v_ + k + 1)
                    mm(pt[:, XT * P:XT * P + P], bt[k % 2][C, j * Q:(j + 1) * Q],
                       xbc[k % 2][C, 2, j * Q:(j + 1) * Q], start=True, stop=True,
                       skip_group_check=True).then_inc(pairs_mm, 1)

                decays(0, 0, b * (NG + 1), b * AHEAD)
                pe.wait_ge(pre_copied, HEAD + b * CONVS + 1)
                project_x(1, 0)
                turn_and_pair(0, 0, b * SILUS, b * AHEAD)
                pe.wait_ge(pre_copied, HEAD + b * CONVS + 2)
                project_x(2, 0)
                with pe.Fori(0, NG // BG) as gg:
                    u, c = pe.snap(b * (NG * NBR) + gg * BU), pe.snap(b * (NG * NBR * 2) + gg * 2 * BU)
                    x, g17 = pe.snap(b * CONVS + gg * BU), pe.snap(b * (NG + 1) + gg * BG)
                    us, a_ = pe.snap(b * ((NG + 1) * NBR) + gg * BU), pe.snap(b * AHEAD + gg * 2 * BU)
                    v_ = pe.snap(b * SILUS + gg * BU)

                    def add_state(k, j, m):
                        pe.wait_ge(xd_ready, HEAD + m + 1)
                        pe.wait_ge(state_ready, HEAD + m)
                        if j == 0:
                            pe.wait_ge(pre_copied, HEAD + x + k + 3)
                        mm(px[C, XS:XS + DIN], xtok[j][:, 2, 0:DS], xd[j][:, 1, :], start=True, stop=True,
                               skip_group_check=True).then_inc(state_mm, 1)

                    def outputs(k, j, m):
                        pe.wait_ge(mix_ready, HEAD + m + 1)
                        pe.wait_ge(xd_ready, HEAD + m + 1)
                        pe.wait_ge(y2_ready, HEAD + m)
                        pe.wait_ge(state_ready, HEAD + m)
                        for h in range(NH):
                            mm(py[:, h * HD:(h + 1) * HD], mix[j][:, h, :], xd[j][:, 0, h * HD:(h + 1) * HD],
                               start=True, stop=True, skip_group_check=True)
                        mm(py[:, DIN:2 * DIN], xbc[k % 2][C, 2, j * Q:(j + 1) * Q], state[k % NBR][C, j, :],
                               start=True, stop=True, skip_group_check=True).then_inc(y_mm, 1)

                    def gate(k, n):
                        pe.wait_ge(branch_copied, HEAD + (n if k == 0 else n - 1))
                        p, i = k // NBR, k % NBR
                        for j in range(2):
                            ins = mm(pz[:, j * DIN:(j + 1) * DIN], ust[p][i][:, j * Q:(j + 1) * Q], w_in[:, i, 0:DIN],
                                     start=True, stop=True, skip_group_check=True)
                        ins.then_inc(z_mm, 1)

                    def turn_back(n):
                        pe.wait_ge(y5_ready, HEAD + n + 1)
                        pe.wait_ge(yts_ready, HEAD + n)
                        for j in range(2):
                            for t in range(2):
                                ins = nc.tensor.transpose(pyt[:, t * UT + j * Q:t * UT + (j + 1) * Q],
                                                          y5[:, j, t * P:(t + 1) * P], ident[:])
                        ins.then_inc(yt_mm, 1)

                    def project_out(i, n, last):
                        pe.wait_ge(yts_ready, HEAD + n + 1)
                        pe.wait_ge(zg_ready, HEAD + (n + 1 if last else n + 2))
                        for t in range(2):
                            ins = mm(pz[:, 0:UT], w_out[:, i, t, :], yts[:, t, :], start=(t == 0), stop=(t == 1),
                                     skip_group_check=True)
                        ins.then_inc(out_mm, 1)

                    for k in range(BU):
                        n, m = u + k, c + 2 * k
                        p, i = k // NBR, k % NBR
                        decays(k, 1, g17, a_ + 2 * k + 1)
                        turn_and_pair(k, 1, v_, a_ + 2 * k + 1)
                        if i == 2:
                            pe.wait_ge(staged, HEAD + us + NBR * (p + 2))
                            pe.wait_ge(pre_copied, HEAD + x + k + 3)
                            pe.wait_ge(state_ready, HEAD + m)
                            project_steps(1 - p)
                        if i == 3:
                            pe.wait_ge(lna_ready, HEAD + g17 + p + 2)
                            pe.wait_ge(pre_copied, HEAD + x + k + 3)
                            pe.wait_ge(state_ready, HEAD + m)
                            sum_decays(1 - p)
                        outputs(k, 0, m)
                        if i == 2:
                            pe.wait_ge(dtx_ready, HEAD + g17 + p + 2)
                        if i == 3:
                            pe.wait_ge(cum_exp, HEAD + g17 + p + 2)
                            pe.wait_ge(cum_ready, HEAD + g17 + p + 2)
                        add_state(k, 0, m)
                        gate(k, n)
                        decays(k + 1, 0, g17, a_ + 2 * k + 2)
                        if k > 0:
                            turn_back(n - 1)
                        turn_and_pair(k + 1, 0, v_, a_ + 2 * k + 2)
                        add_state(k, 1, m + 1)
                        outputs(k, 1, m + 1)
                        if k > 0:
                            project_out((k - 1) % NBR, n - 1, False)
                        pe.wait_ge(staged, HEAD + us + k + 4)
                        pe.wait_ge(pre_copied, HEAD + x + k + 3)
                        pe.wait_ge(state_ready, HEAD + m + 2)
                        project_x((k + 3) % NBR, ((k + 3) // NBR) % 2)
                    turn_back(u + BU - 1)
                    project_out(NBR - 1, u + BU - 1, True)

                pe.wait_ge(sums_act, b * 3 + 3)
                pe.wait_ge(sums_dve, b * 2 + 2)
                mm(pt[:, 0:5], ones[:], sums[:, 0:5], start=True, stop=True).then_inc(desc_mm, 1)
                with pe.Fori(0, NT // 2) as tp:
                    for h in range(2):
                        t = tp * 2 + h
                        pe.wait_ge(proj_copied, HEAD + b * NT + t - 1)
                        for j in range(5):
                            src = brf[(j + 4) % 5][:, bass.ds(t * TT, TT)]
                            ins = mm(px[:, h * TT:(h + 1) * TT], proj_w[:, j, :], src, start=(j == 0), stop=(j == 4))
                        ins.then_inc(proj_mm, 1)
                pe.wait_ge(gn_step, b * GN_STEPS + 3)
                mm(pt[:, 8:10], group_avg[:], gst[:, 2:4], start=True, stop=True).then_inc(group_mm, 1)

                def tile(buf, t):
                    return buf[:, bass.ds(t * TT, TT)]

                def norm_tokens(pass_):
                    with pe.Fori(0, NT // 2) as tp:
                        for h in range(2):
                            t = tp * 2 + h
                            e = (b * 2 + pass_) * NT + t
                            pe.wait_ge(centered, HEAD + e - 1)
                            if pass_ == 0:
                                pe.wait_ge(x1_ready, b * 4 + tp + 1)
                            else:
                                pe.wait_ge(q_ready, HEAD + (b + 1) * NT)
                            if pass_ == 1:
                                pe.wait_ge(x2_ready, HEAD + b * NT + t + 1)
                            mm((pz, py)[h][:], mean_w[:], tile(brf[0], t), start=True, stop=True).then_inc(mean_mm, 1)
                    with pe.Fori(0, NT // 2) as tp:
                        for h in range(2):
                            t = tp * 2 + h
                            e = (b * 2 + pass_) * NT + t
                            pe.wait_ge(ln_ready, HEAD + e - 1)
                            pe.wait_ge(squares_ready, HEAD + e + 1)
                            mm((pt, pyt)[h][:], mean_w[:], tile(brf[2], t), start=True, stop=True).then_inc(var_mm, 1)

                norm_tokens(0)
                with pe.Fori(0, NT // 2) as tp:
                    for h in range(2):
                        t = tp * 2 + h
                        pe.wait_ge(normed, HEAD + b * (2 * NT) + t + 1)
                        pe.wait_ge(kv_summed, HEAD + b * NT + t - 1)
                        mm(pd[:, h * TT:(h + 1) * TT], wqkv[:, 1, :], tile(brf[1], t), start=True, stop=True)
                        mm(px[:, h * TT:(h + 1) * TT], wqkv[:, 2, :], tile(brf[1], t), start=True, stop=True).then_inc(kv_mm, 1)
                with pe.Fori(0, NT // 2) as tp:
                    for h in range(2):
                        t = tp * 2 + h
                        pe.wait_ge(q_ready, HEAD + b * NT + t - 1)
                        mm((pz, py)[h][:], wqkv[:, 0, :], tile(brf[1], t), start=True, stop=True).then_inc(q_mm, 1)
                norm_tokens(1)
                for s in range(L // P):
                    pe.wait_ge(normed, HEAD + b * (2 * NT) + NT + s * P // TT + 1)
                    ins = mm(pz[:, s * NE:(s + 1) * NE], brf[1][:, s * P:(s + 1) * P], router[:], start=True, stop=True,
                             skip_group_check=True)
                ins.then_inc(logits_mm, 1)
                pe.wait_ge(gates_ready, b + 1)
                for t in range(NT):
                    if t >= 2:
                        pe.wait_ge(gates_copied, b * NT + t - 1)
                    for s in range(4):
                        ins = nc.tensor.transpose((pt, pyt)[t % 2][0:NE, s * P:(s + 1) * P],
                                                  gates[:, 0, 4 * t + s, :], ident[:])
                    ins.then_inc(gates_turned, 1)

                def experts(h, e, s):
                    pe.wait_ge(xst_ready, HEAD + e + 1)
                    pe.wait_ge(weighed, HEAD + e - 1)
                    for half in range(2):
                        ins = mm((px, pd)[h][:, half * 512:(half + 1) * 512], xst[h],
                                 expert_w[:, 4 * half:4 * half + 4, :].rearrange("d e c -> d (e c)"),
                                 start=True, stop=True)
                    ins.then_inc(expert_mm, 1)

                def combine(h, e, s):
                    pe.wait_ge(quarter_ready, HEAD + e + 1)
                    pe.wait_ge(out_ready, HEAD + e - 1)
                    pe.wait_ge(gates_copied, b * NT + NT)
                    o = (pz, py)[h][:, 0:P]
                    cols = slice(s * P, (s + 1) * P) if isinstance(s, int) else bass.ds(s * P, P)
                    mm(o, expert_b[:], brf[2][0:NE, cols], start=True, stop=False)
                    for half in range(2):
                        ins = mm(o, quarter_sum[h][:, half, :], ident[:], start=False, stop=(half == 1))
                    ins.then_inc(comb_mm, 1)

                e0 = pe.snap(b * (L // P))
                for h in range(2):
                    experts(h, e0 + h, h)
                with pe.Fori(1, L // (2 * P)) as s2:
                    e = pe.snap(b * (L // P) + s2 * 2)
                    for h in range(2):
                        experts(h, e + h, s2 * 2 + h)
                        combine(h, e + h - 2, s2 * 2 + h - 2)
                for h in range(2):
                    combine(h, e0 + L // P - 2 + h, L // P - 2 + h)

        @block.scalar
        def _(act):
            af = nc.scalar.activation
            head_start(act, (rstd_ready, ln_ready, dt_exp, cum_exp, pre_copied, conv_tanh_ready, bt_ready, xtok_ready, gm_ready, ebuf_ready,
                             squared, tz_ready, yts_ready, branch_copied, proj_copied, squares_ready, k_ready,
                             q_ready, xst_ready, y5_ready, tap0_ready))
            act.wait_ge(weights_in, 16 * len(loads))
            af(sel[:], selbase[:], ACT.Copy)
            af(ident_b[:], ident[:], ACT.Copy)
            af(never[:], after[:], ACT.Copy, scale=NEVER)
            af(nsel[:], selbase[:], ACT.Copy, scale=-1.0).then_inc(selectors_made, 1)
            af(par("A"), par("A"), ACT.Exp).then_inc(a_step, 1)

            def step_sizes(q):
                act.wait_ge(dtx_ready, HEAD + q + 1)
                act.wait_ge(lna_ready, HEAD + q)
                af(dte[:, 0, :], dtx[:], ACT.Relu)
                af(dte[:, 1, :], dtx[:], ACT.Abs).then_inc(abs_ready, 1)
                act.wait_ge(abs_ready, q + 1)
                af(dte[:, 2, :], dte[:, 1, :], ACT.Exp, scale=-1.0).then_inc(dt_exp, 1)

            def decay_factors(q, p):
                act.wait_ge(cum_mm, HEAD + q + 1)
                act.wait_ge(cum_ready, HEAD + q + 1)
                af(ec[p][:].rearrange("c a n -> c (a n)"), px[:, XS + GC:XS + 4 * GC], ACT.Exp).then_inc(cum_exp, 1)

            def copy_pre(k, i, b, xn, vn):
                act.wait_ge(x_mm, HEAD + xn + b + 1)
                act.wait_ge(acc_ready, HEAD + xn - 1)
                o = pre[k % 2]
                af(o[:, :, 0:3], past[i][:], ACT.Copy)
                af(o[:, :, 3:3 + UT], px[:, 0:XS].rearrange("c (t n) -> c t n", t=XT), ACT.Copy).then_inc(pre_copied, 1)
                act.wait_ge(xbc_ready, HEAD + vn - 1)
                act.wait_ge(pre_copied, HEAD + xn + 1)
                for t in range(XT):
                    ins = af(acc[k % 2][:, t, :], o[:, t, 0:UT], ACT.Copy, scale=conv_w[:, i, t, 0:1])
                ins.then_inc(tap0_ready, 1)
                af(past[i][:], o[:, :, UT:UT + 3], ACT.Copy).then_inc(past_kept, 1)

            def conv_tanh(k, xn, vn):
                act.wait_ge(acc_ready, HEAD + xn + 1)
                act.wait_ge(xbc_ready, HEAD + vn)
                af(th[:], acc[k % 2], ACT.Tanh).then_inc(conv_tanh_ready, 1)

            def copy_b(k, xn):
                act.wait_ge(xbc_ready, HEAD + xn + 1)
                af(bt[k % 2][C, :], xbc[k % 2][0:DS, 2, :], ACT.Copy).then_inc(bt_ready, 1)

            with act.Fori(0, NB) as b:
                step_sizes(b * (NG + 1))
                act.wait_ge(hd_ready, HEAD + b * (NG * NBR * 2))
                decay_factors(b * (NG + 1), 0)
                copy_pre(0, 0, b, b * CONVS, b * SILUS)
                conv_tanh(0, b * CONVS, b * SILUS)
                copy_pre(1, 1, b, b * CONVS + 1, b * SILUS + 1)
                copy_b(0, b * SILUS)

                def copy_tokens(j, m, q):
                    act.wait_ge(pairs_mm, HEAD + q + 1)
                    act.wait_ge(xd_ready, HEAD + m - 1)
                    act.wait_ge(dx_ready, HEAD + m - 1)
                    act.wait_ge(state_mm, HEAD + m - 1)
                    af(xtok[j][:], pt[:, 0:XT * P].rearrange("c (t n) -> c t n", t=XT), ACT.Copy).then_inc(xtok_ready, 1)
                    act.wait_ge(mix_ready, HEAD + m - 1)
                    af(gm[j][:], pt[:, XT * P:(XT + 1) * P], ACT.Copy).then_inc(gm_ready, 1)

                def decay_exp(m, q):
                    act.wait_ge(decay_mm, HEAD + q + 1)
                    act.wait_ge(mix_ready, HEAD + m)
                    af(ebuf[:].rearrange("c h t -> c (h t)"), pd[:], ACT.Exp).then_inc(ebuf_ready, 1)

                decay_exp(b * (NG * NBR * 2), b * AHEAD)
                copy_tokens(0, b * (NG * NBR * 2), b * AHEAD)
                conv_tanh(1, b * CONVS + 1, b * SILUS + 1)
                with act.Fori(0, NG // BG) as gg:
                    u, c = act.snap(b * (NG * NBR) + gg * BU), act.snap(b * (NG * NBR * 2) + gg * 2 * BU)
                    x, a_ = act.snap(b * CONVS + gg * BU), act.snap(b * AHEAD + gg * 2 * BU)
                    v_ = act.snap(b * SILUS + gg * BU)
                    g17 = act.snap(b * (NG + 1) + gg * BG)
                    g2 = act.snap(gg * BG)

                    def square(k, j, m):
                        act.wait_ge(y4_ready, HEAD + m + 1)
                        act.wait_ge(rs_ready, HEAD + u + k)
                        act.wait_ge(squared, HEAD + m)
                        af(sqj[:], y4[k % 2][:, j, :], ACT.Square, scale=DIN ** -0.5, accum_out=ss[:, j:j + 1]).then_inc(squared, 1)

                    def copy_turned(n):
                        act.wait_ge(yt_mm, HEAD + n + 1)
                        act.wait_ge(out_mm, HEAD + n)
                        af(yts[:].rearrange("c t n -> c (t n)"), pyt[:], ACT.Copy).then_inc(yts_ready, 1)

                    def store_branch(i, n, g):
                        act.wait_ge(out_mm, HEAD + n + 1)
                        pieces = scan_rows(i, pz[:, 0:UT].rearrange("c (r s) -> c r s", r=ROWS))
                        for rows, src in pieces:
                            ins = af(order(i, br[i][:], g)[:, rows, :], src, ACT.Copy)
                        ins.then_inc(branch_copied, 1)

                    def norm_outputs(k, n):
                        act.wait_ge(rs_ready, HEAD + n + 1)
                        act.wait_ge(yt_mm, HEAD + n)
                        for j in range(2):
                            ins = af(y5[:, j, :], y4[k % 2][:, j, :], ACT.Copy, scale=rs[:, j:j + 1])
                        ins.then_inc(y5_ready, 1)

                    for k in range(BU):
                        n, m = u + k, c + 2 * k
                        p, i = k // NBR, k % NBR
                        copy_pre(k + 2, (k + 2) % NBR, b, x + k + 2, v_ + k + 2)
                        if k > 0:
                            square(k - 1, 1, m - 1)
                        copy_tokens(1, m + 1, a_ + 2 * k + 1)
                        if i == 3:
                            act.wait_ge(y2_ready, HEAD + m - 6)
                            act.wait_ge(hd_ready, HEAD + m - 6)
                            decay_factors(g17 + p + 1, 1 - p)
                        decay_exp(m + 1, a_ + 2 * k + 1)
                        copy_b(k + 1, v_ + k + 1)
                        if k > 0:
                            norm_outputs(k - 1, n - 1)
                        act.wait_ge(z_mm, HEAD + n + 1)
                        act.wait_ge(zg_ready, HEAD + n)
                        af(tz[:].rearrange("c j d -> c (j d)"), pz[:], ACT.Tanh, scale=0.5).then_inc(tz_ready, 1)
                        if k > 0:
                            copy_turned(n - 1)
                        copy_tokens(0, m + 2, a_ + 2 * k + 2)
                        decay_exp(m + 2, a_ + 2 * k + 2)
                        if i == 2:
                            step_sizes(g17 + p + 1)
                        conv_tanh(k + 2, x + k + 2, v_ + k + 2)
                        if k > 0:
                            store_branch((k - 1) % NBR, n - 1, g2 + (k - 1) // NBR)
                        square(k, 0, m)
                    square(BU - 1, 1, c + 2 * BU - 1)
                    norm_outputs(BU - 1, u + BU - 1)
                    copy_turned(u + BU - 1)
                    store_branch(NBR - 1, u + BU - 1, g2 + BG - 1)

                act.wait_ge(branch_copied, HEAD + (b + 1) * (NG * NBR))
                act.wait_ge(local_ready, b + 1)
                af(brf[4], brf[4], ACT.Gelu_apprx_tanh, accum_out=sums[:, 0:1]).then_inc(sums_act, 1)
                for i in range(2):
                    af(brf[i], brf[i], ACT.Copy, accum_out=sums[:, i + 1:i + 2]).then_inc(sums_act, 1)
                act.wait_ge(se_step, b * SE_STEPS + 4)
                af(se[:, 20:22], se[:, 18:20], ACT.Gelu_apprx_tanh).then_inc(se_nonlin, 1)
                act.wait_ge(se_step, b * SE_STEPS + 7)
                af(se[:, 35:40], se[:, 30:35], ACT.Tanh, scale=0.5).then_inc(se_nonlin, 1)

                def tile(buf, t):
                    return buf[:, bass.ds(t * TT, TT)]

                with act.Fori(0, NT // 2) as tp:
                    for h in range(2):
                        t = tp * 2 + h
                        act.wait_ge(proj_mm, HEAD + b * NT + t + 1)
                        act.wait_ge(fused_ready, HEAD + b * NT + t + 1)
                        af(tile(brf[1], t), px[:, h * TT:(h + 1) * TT], ACT.Copy).then_inc(proj_copied, 1)
                act.wait_ge(affine_ready, b + 1)
                for q in range(4):
                    s = slice(q * L // 4, (q + 1) * L // 4)
                    af(brf[1][:, s], brf[1][:, s], ACT.Gelu_apprx_tanh, bias=gst[:, 12:13], scale=gst[:, 11:12]).then_inc(gelu_ready, 1)

                def norm_tokens(pass_):
                    with act.Fori(0, NT // 2) as tp:
                        for h in range(2):
                            t = tp * 2 + h
                            e = (b * 2 + pass_) * NT + t
                            act.wait_ge(centered, HEAD + e + 1)
                            af(tile(brf[2], t), tile(brf[1], t), ACT.Square).then_inc(squares_ready, 1)
                    with act.Fori(0, NT // 2) as tp:
                        for h in range(2):
                            t = tp * 2 + h
                            e = (b * 2 + pass_) * NT + t
                            act.wait_ge(var_mm, HEAD + e + 1)
                            af(tile(brf[2], t), (pt, pyt)[h][:], ACT.Ln, bias=eps[:, 0:1]).then_inc(ln_ready, 1)
                    with act.Fori(0, NT // 2) as tp:
                        for h in range(2):
                            t = tp * 2 + h
                            e = (b * 2 + pass_) * NT + t
                            act.wait_ge(ln_ready, HEAD + e + 1)
                            af(tile(brf[2], t), tile(brf[2], t), ACT.Exp, scale=-0.5).then_inc(rstd_ready, 1)

                norm_tokens(0)
                with act.Fori(0, NT // 2) as tp:
                    for h in range(2):
                        t = tp * 2 + h
                        act.wait_ge(kv_mm, HEAD + b * NT + t + 1)
                        act.wait_ge(kv_summed, HEAD + b * NT + t - 1)
                        act.wait_ge(normed, HEAD + b * (2 * NT) + NT)
                        af(ks[h], pd[:, h * TT:(h + 1) * TT], ACT.Identity, bias=par("bk")).then_inc(k_ready, 1)
                with act.Fori(0, NT // 2) as tp:
                    for h in range(2):
                        t = tp * 2 + h
                        act.wait_ge(q_mm, HEAD + b * NT + t + 1)
                        act.wait_ge(kv_step, b * 2 + 2)
                        af(tile(brf[2], t), (pz, py)[h][:], ACT.Identity, bias=kvp[:, 9:10], scale=kvp[:, 8:9]).then_inc(q_ready, 1)
                norm_tokens(1)
                act.wait_ge(logits_step, b * 3 + 3)
                g_ = [gates[:, q, :, :].rearrange("c s e -> c (s e)") for q in range(4)]
                af(g_[0], g_[2], ACT.Exp).then_inc(gates_exp, 1)
                for t in range(NT):
                    act.wait_ge(gates_turned, b * NT + t + 1)
                    af(brf[2][0:NE, t * TT:(t + 1) * TT], (pt, pyt)[t % 2][0:NE, :], ACT.Copy).then_inc(gates_copied, 1)
                with act.Fori(0, L // (2 * P)) as s2:
                    e = act.snap(b * (L // P) + s2 * 2)
                    for h in range(2):
                        act.wait_ge(expert_mm, HEAD + e + h - 1)
                        af(xst[h], brf[1][:, bass.ds(s2 * (2 * P) + h * P, P)], ACT.Copy).then_inc(xst_ready, 1)

        @block.vector
        def _(dve):
            v = nc.vector
            head_start(dve, (image_done, quarter_ready, dtx_ready, lna_ready, cum_ready, acc_ready, xbc_ready, mix_ready, xd_ready, state_ready,
                             y2_ready, zg_ready, fused_ready, centered, normed, kv_summed, x2_ready, weighed,
                             out_ready))
            v.memset(xp[:], 0.0)
            v.memset(eps[:], LN_EPS)
            dve.wait_ge(weights_in, 16 * len(loads))
            dve.wait_ge(pos_mm, 1)
            v.tensor_scalar(conv_w[:], conv_w[:], 0.5, None, ALU.mult)
            for i in range(NBR):
                for t in range(2):
                    v.tensor_scalar(w_out[:, i, t, :], w_out[:, i, t, :], norm_w[:, i, t:t + 1], None, ALU.mult)
            v.tensor_copy(pos[:, 0, :], pt[:, 0:HW])
            v.tensor_copy(pos[:, 1, :], pyt[:, 0:HW]).then_inc(params_scaled, 1)
            dve.wait_ge(params_scaled, 1)
            dve.wait_ge(a_step, 1)
            v.tensor_scalar(par("A"), par("A"), -1.0, None, ALU.mult).then_inc(a_step, 1)
            dve.wait_ge(a_step, 2)

            def step_bias(q):
                dve.wait_ge(dt_mm, HEAD + q + 1)
                dve.wait_ge(dt_exp, HEAD + q)
                v.tensor_tensor(dtx[:].rearrange("c (j n) -> c j n", j=2),
                                    px[:, XS:XS + GC].rearrange("c (j n) -> c j n", j=2),
                                    par("dtb").unsqueeze(1).broadcast_to([P, 2, NBR * NH]), ALU.add).then_inc(dtx_ready, 1)

            def softplus(q, p):
                dve.wait_ge(dt_exp, HEAD + q + 1)
                dve.wait_ge(cum_mm, HEAD + q)
                steps = len(LOG1P)
                e = dte[:, 2, :]
                v.tensor_scalar(dtp[:], e, LOG1P[-1], None, ALU.mult).then_inc(poly_step, 1)
                for r, cf in enumerate(LOG1P[-2::-1]):
                    dve.wait_ge(poly_step, q * steps + r + 1)
                    ins = v.scalar_tensor_tensor(dtp[:], dtp[:], cf, e, ALU.add, ALU.mult)
                    ins.then_inc(poly_step, 1)
                dve.wait_ge(poly_step, (q + 1) * steps)
                dt = wd[p][:, :, 0, :]
                v.tensor_tensor(dt, dtp[:].rearrange("c (u h) -> c u h", h=NH),
                                    dte[:, 0, :].rearrange("c (u h) -> c u h", h=NH), ALU.add).then_inc(log_step, 1)
                dve.wait_ge(log_step, q * 2 + 1)
                av = par("A").rearrange("c (i h) -> c i h", h=NH)
                for j in range(2):
                    ins = v.tensor_tensor(lna[:, j * 32:(j + 1) * 32].rearrange("c (i h) -> c i h", h=NH),
                                          wd[p][:, j * NBR:(j + 1) * NBR, 0, :], av, ALU.mult)
                ins.then_inc(log_step, 1)
                dve.wait_ge(log_step, q * 2 + 2)
                v.tensor_copy(lna3[:].rearrange("c j (a n) -> c j a n", a=3),
                                  lna[:].rearrange("c (j n) -> c j n", j=2).unsqueeze(2).broadcast_to([P, 2, 3, 32])).then_inc(lna_ready, 1)

            def split_sums(q, p):
                src = px[0:96, 2 * UT:3 * UT]
                base = q * 5
                dve.wait_ge(cum_mm, HEAD + q + 1)
                v.tensor_copy(cum[p][:], src).then_inc(part_step, 1)
                dve.wait_ge(part_step, base + 1)
                v.tensor_tensor(cr[:], src, cum[p][:], ALU.subtract).then_inc(part_step, 1)
                dve.wait_ge(part_step, base + 2)
                v.tensor_copy(cum[p][32:64, :], cr[32:64, :]).then_inc(part_step, 1)
                v.tensor_copy(cum[p][64:96, :], cr[64:96, :]).then_inc(part_step, 1)
                dve.wait_ge(part_step, base + 4)
                v.tensor_tensor(cr2[64:96, :], cr[64:96, :], cum[p][64:96, :], ALU.subtract).then_inc(part_step, 1)
                dve.wait_ge(part_step, base + 5)
                v.tensor_copy(cum[p][64:96, :], cr2[64:96, :]).then_inc(cum_ready, 1)

            def convolve(k, i, xn, taps):
                base = xn * (XT * (TAPS - 2))
                o = acc[k % 2]
                for r in taps:
                    for t in range(XT):
                        if r == 1:
                            dve.wait_ge(tap0_ready, HEAD + xn + 1)
                        else:
                            dve.wait_ge(tap_step, base + (r - 2) * XT + t + 1)
                        ins = v.scalar_tensor_tensor(o[:, t, :], pre[k % 2][:, t, r:r + UT], conv_w[:, i, t, r:r + 1],
                                                     o[:, t, :], ALU.mult, ALU.add)
                        if r < TAPS - 1:
                            ins.then_inc(tap_step, 1)
                if TAPS - 1 in taps:
                    ins.then_inc(acc_ready, 1)

            def silu(k, b, xn, m):
                dve.wait_ge(conv_tanh_ready, HEAD + xn + b + 1)
                dve.wait_ge(y_mm, HEAD + m)
                dve.wait_ge(bt_ready, HEAD + xn - 1)
                v.scalar_tensor_tensor(xbc[k % 2].rearrange("c t n -> c (t n)"),
                                           th[:].rearrange("c t n -> c (t n)"), 1.0,
                                           acc[k % 2].rearrange("c t n -> c (t n)"), ALU.add, ALU.mult).then_inc(xbc_ready, 1)

            with dve.Fori(0, NB) as b:
                dve.wait_ge(image_in, (b + 1) * 16)
                for i in range(NBR):
                    v.memset(state[i][:], 0.0)
                    v.memset(past[i][:], 0.0)
                v.tensor_tensor(interior[:, 0:HW, 0:HW], br[0][:], pos[:, 0, :].unsqueeze(2).broadcast_to([P, HW, HW]),
                                    ALU.add).then_inc(row_added, 1)
                dve.wait_ge(row_added, b + 1)
                v.tensor_tensor(interior[:, 0:HW, 0:HW], interior[:, 0:HW, 0:HW],
                                    pos[:, 1, :].unsqueeze(1).broadcast_to([P, HW, HW]), ALU.add).then_inc(xp_ready, 1)
                step_bias(b * (NG + 1))
                softplus(b * (NG + 1), 0)
                split_sums(b * (NG + 1), 0)
                convolve(0, 0, b * CONVS, (1, 2, 3))
                silu(0, b, b * SILUS, b * (NG * NBR * 2))
                convolve(1, 1, b * CONVS + 1, (1, 2, 3))
                with dve.Fori(0, NG // BG) as gg:
                    u, c = dve.snap(b * (NG * NBR) + gg * BU), dve.snap(b * (NG * NBR * 2) + gg * 2 * BU)
                    x, a_ = dve.snap(b * CONVS + gg * BU), dve.snap(b * AHEAD + gg * 2 * BU)
                    g17, v_ = dve.snap(b * (NG + 1) + gg * BG), dve.snap(b * SILUS + gg * BU)

                    def scale_tokens(k, j, m, q):
                        p, i = k // NBR, k % NBR
                        dve.wait_ge(xtok_ready, HEAD + q + 1)
                        dve.wait_ge(wd_ready, HEAD + g17 + p + 1)
                        dve.wait_ge(y_mm, HEAD + m - 1)
                        ji = j * NBR + i
                        v.tensor_tensor(
                            xd[j][:].rearrange("c q (h d) -> c q h d", h=NH),
                            xtok[j][:, 0:2, :].rearrange("c a (h d) -> c (a h) d", d=HD)
                            .unsqueeze(1).broadcast_to([P, 2, NH, HD]),
                            wd[p][:, ji, :, :].unsqueeze(3).broadcast_to([P, 2, NH, HD]), ALU.mult).then_inc(xd_ready, 1)

                    def mix_pairs(j, m, q):
                        dve.wait_ge(ebuf_ready, HEAD + q + 1)
                        dve.wait_ge(gm_ready, HEAD + q + 1)
                        dve.wait_ge(y_mm, HEAD + m - 1)
                        v.tensor_tensor(mix[j][:], ebuf[:], gm[j][:].unsqueeze(1)
                                            .broadcast_to([P, NH, P]), ALU.mult).then_inc(mix_ready, 1)

                    def update_state(i, j, m):
                        dve.wait_ge(state_mm, HEAD + m + 1)
                        dve.wait_ge(hd_ready, HEAD + m + 1)
                        v.tensor_tensor(state[i][C, 1 - j, :], hd[j][C, :], px[C, XS:XS + DIN], ALU.add).then_inc(state_ready, 1)

                    def add_outputs(k, j, m):
                        p, i = k // NBR, k % NBR
                        ji = j * NBR + i
                        dve.wait_ge(y_mm, HEAD + m + 1)
                        dve.wait_ge(y2_ready, HEAD + m)
                        v.tensor_tensor(y1[:].rearrange("c (h d) -> c h d", h=NH),
                                            py[:, DIN:2 * DIN].rearrange("c (h d) -> c h d", h=NH),
                                            ec[p][:, 0, ji * NH:(ji + 1) * NH].unsqueeze(2).broadcast_to([P, NH, HD]),
                                            ALU.mult).then_inc(y1_ready, 1)
                        dve.wait_ge(y1_ready, m + 1)
                        dve.wait_ge(y3_ready, m)
                        v.tensor_tensor(y2[:], y1[:], py[:, 0:DIN], ALU.add).then_inc(y2_ready, 1)

                    for k in range(BU):
                        n, m = u + k, c + 2 * k
                        p, i = k // NBR, k % NBR
                        mix_pairs(0, m, a_ + 2 * k)
                        scale_tokens(k, 0, m, a_ + 2 * k)
                        silu(k + 1, b, v_ + k + 1, m)
                        if i == 3:
                            split_sums(g17 + p + 1, 1 - p)
                        convolve(k + 2, (k + 2) % NBR, x + k + 2, (1,))
                        if i == 2:
                            step_bias(g17 + p + 1)
                        scale_tokens(k, 1, m + 1, a_ + 2 * k + 1)
                        mix_pairs(1, m + 1, a_ + 2 * k + 1)
                        add_outputs(k, 0, m)
                        update_state(i, 0, m)
                        convolve(k + 2, (k + 2) % NBR, x + k + 2, (2,))
                        update_state(i, 1, m + 1)
                        convolve(k + 2, (k + 2) % NBR, x + k + 2, (3,))
                        dve.wait_ge(tz_ready, HEAD + n + 1)
                        dve.wait_ge(y4_ready, HEAD + m - 2)
                        v.scalar_tensor_tensor(zg[k % 2][:].rearrange("c j d -> c (j d)"),
                                               tz[:].rearrange("c j d -> c (j d)"), 1.0, pz[:],
                                               ALU.add, ALU.mult).then_inc(zg_ready, 1)
                        add_outputs(k, 1, m + 1)
                        if i == 2:
                            softplus(g17 + p + 1, 1 - p)

                dve.wait_ge(branch_copied, HEAD + (b + 1) * (NG * NBR))
                dve.wait_ge(bt_ready, HEAD + (b + 1) * SILUS)
                dve.wait_ge(conv_tanh_ready, HEAD + (b + 1) * CONVS)
                dve.wait_ge(xp_ready, b + 1)
                v.tensor_scalar(br[4], xp[:, 0:HW, 0:HW], local_w[:, 0:1], None, ALU.mult).then_inc(local_step, 1)
                for r in range(1, 9):
                    dve.wait_ge(local_step, b * 8 + r)
                    dy, dx_ = r // 3, r % 3
                    ins = v.scalar_tensor_tensor(br[4], xp[:, dy:dy + HW, dx_:dx_ + HW], local_w[:, r:r + 1], br[4],
                                                 ALU.mult, ALU.add)
                    ins.then_inc(local_step if r < 8 else local_ready, 1)
                for i in range(2, 4):
                    v.tensor_reduce(sums[:, i + 1:i + 2], brf[i], AX.X, ALU.add).then_inc(sums_dve, 1)
                dve.wait_ge(desc_mm, b + 1)
                v.tensor_scalar(se[:, 0:5], pt[:, 0:5], 1.0 / (P * L), None, ALU.mult).then_inc(se_step, 1)
                dve.wait_ge(se_step, b * SE_STEPS + 1)
                v.tensor_tensor(se[:, 5:15].rearrange("c (a j) -> c a j", a=2),
                                    se[:, 0:5].unsqueeze(1).broadcast_to([P, 2, 5]),
                                    par("w1").rearrange("c (a j) -> c a j", a=2), ALU.mult).then_inc(se_step, 1)
                dve.wait_ge(se_step, b * SE_STEPS + 2)
                v.tensor_reduce(se[:, 15:17], se[:, 5:15].rearrange("c (a j) -> c a j", a=2), AX.X, ALU.add).then_inc(se_step, 1)
                dve.wait_ge(se_step, b * SE_STEPS + 3)
                v.tensor_tensor(se[:, 18:20], se[:, 15:17], par("b1"), ALU.add).then_inc(se_step, 1)
                dve.wait_ge(se_step, b * SE_STEPS + 4)
                dve.wait_ge(se_nonlin, b * 2 + 1)
                v.tensor_tensor(se[:, 5:15].rearrange("c (j a) -> c j a", a=2),
                                    se[:, 20:22].unsqueeze(1).broadcast_to([P, 5, 2]),
                                    par("w2").rearrange("c (j a) -> c j a", a=2), ALU.mult).then_inc(se_step, 1)
                dve.wait_ge(se_step, b * SE_STEPS + 5)
                v.tensor_reduce(se[:, 22:27], se[:, 5:15].rearrange("c (j a) -> c j a", a=2), AX.X, ALU.add).then_inc(se_step, 1)
                dve.wait_ge(se_step, b * SE_STEPS + 6)
                v.tensor_tensor(se[:, 30:35], se[:, 22:27], par("b2"), ALU.add).then_inc(se_step, 1)
                dve.wait_ge(se_step, b * SE_STEPS + 7)
                dve.wait_ge(se_nonlin, b * 2 + 2)
                v.tensor_scalar(sew[:], se[:, 35:40], 1.0, 0.5, ALU.add, ALU.mult).then_inc(se_ready, 1)

                def tile(buf, t):
                    return buf[:, bass.ds(t * TT, TT)]

                with dve.Fori(0, NT // 2) as tp:
                    for h in range(2):
                        t = tp * 2 + h
                        dve.wait_ge(se_ready, b + 1)
                        dve.wait_ge(proj_mm, HEAD + b * NT + t + 1)
                        dve.wait_ge(x_tile_in[h], (b * (NT // 2) + tp + 1) * 16)
                        out = tile(brf[0], t)
                        v.scalar_tensor_tensor(out, out, sew[:, 1:2], ks[h], ALU.mult, ALU.add).then_inc(fuse_step, 1)
                        for r, j in enumerate((1, 2, 3, 4)):
                            w = (j + 1) % 5
                            dve.wait_ge(fuse_step, (b * NT + t) * 4 + r + 1)
                            ins = v.scalar_tensor_tensor(out, tile(brf[j], t), sew[:, w:w + 1], out, ALU.mult, ALU.add)
                            ins.then_inc(fuse_step if r < 3 else fused_ready, 1)
                dve.wait_ge(proj_copied, HEAD + b * NT + NT)
                for t in range(NT):
                    ins = v.bn_stats(bnst[:, t, :], brf[1][:, t * TT:(t + 1) * TT])
                ins.then_inc(gn_step, 1)
                dve.wait_ge(gn_step, b * GN_STEPS + 1)
                v.memset(gst[:, 15:16], 0.0)
                v.bn_aggr(gst[:, 0:2], bnst[:]).then_inc(gn_step, 1)
                dve.wait_ge(gn_step, b * GN_STEPS + 2)
                v.tensor_copy(gst[:, 2:3], gst[:, 0:1])
                v.scalar_tensor_tensor(gst[:, 3:4], gst[:, 0:1], gst[:, 0:1], gst[:, 1:2], ALU.mult, ALU.add).then_inc(gn_step, 1)
                dve.wait_ge(gn_step, b * GN_STEPS + 3)
                dve.wait_ge(group_mm, b + 1)
                v.tensor_copy(gst[:, 5:6], pt[:, 8:9])
                v.tensor_scalar(gst[:, 6:7], pt[:, 9:10], GN_EPS, None, ALU.add).then_inc(norm_step, 1)
                dve.wait_ge(norm_step, b * 3 + 1)
                v.tensor_tensor(gst[:, 4:5], gst[:, 5:6], gst[:, 5:6], ALU.mult).then_inc(norm_step, 1)
                dve.wait_ge(norm_step, b * 3 + 2)
                v.tensor_tensor(gst[:, 7:8], gst[:, 6:7], gst[:, 4:5], ALU.subtract).then_inc(gn_step, 1)
                dve.wait_ge(gn_step, b * GN_STEPS + 4)
                dve.wait_ge(group_rsqrt, b + 1)
                v.tensor_tensor(gst[:, 11:12], gst[:, 8:9], par("gamma"), ALU.mult).then_inc(gn_step, 1)
                dve.wait_ge(gn_step, b * GN_STEPS + 5)
                v.tensor_tensor(gst[:, 13:14], gst[:, 5:6], gst[:, 11:12], ALU.mult).then_inc(norm_step, 1)
                dve.wait_ge(norm_step, b * 3 + 3)
                v.tensor_tensor(gst[:, 12:13], par("beta"), gst[:, 13:14], ALU.subtract).then_inc(affine_ready, 1)
                for q in range(4):
                    s = slice(q * L // 4, (q + 1) * L // 4)
                    dve.wait_ge(gelu_ready, b * 4 + q + 1)
                    v.tensor_tensor(brf[0][:, s], brf[0][:, s], brf[1][:, s], ALU.add).then_inc(x1_ready, 1)
                def norm_tokens(pass_):
                    with dve.Fori(0, NT // 2) as tp:
                        for h in range(2):
                            t = tp * 2 + h
                            e = (b * 2 + pass_) * NT + t
                            dve.wait_ge(mean_mm, HEAD + e + 1)
                            if pass_ == 0:
                                dve.wait_ge(x1_ready, b * 4 + tp + 1)
                            v.tensor_tensor(tile(brf[1], t), tile(brf[0], t), (pz, py)[h][:], ALU.subtract).then_inc(centered, 1)
                    with dve.Fori(0, NT // 2) as tp:
                        for h in range(2):
                            t = tp * 2 + h
                            e = (b * 2 + pass_) * NT + t
                            dve.wait_ge(rstd_ready, HEAD + e + 1)
                            v.tensor_tensor(tile(brf[1], t), tile(brf[1], t), tile(brf[2], t), ALU.mult).then_inc(normed, 1)

                norm_tokens(0)
                for t in range(NT):
                    h = t % 2
                    dve.wait_ge(kv_mm, HEAD + b * NT + t + 1)
                    dve.wait_ge(k_ready, HEAD + b * NT + t + 1)
                    if t >= 1:
                        dve.wait_ge(kv_summed, HEAD + b * NT + t)
                    v.scalar_tensor_tensor(dump, px[:, h * TT:(h + 1) * TT], par("bv"), ks[h], ALU.add, ALU.mult,
                                               accum_out=kvp[:, t:t + 1]).then_inc(kv_summed, 1)
                dve.wait_ge(kv_summed, HEAD + b * NT + NT)
                v.tensor_reduce(kvp[:, 8:9], kvp[:, 0:8], AX.X, ALU.add).then_inc(kv_step, 1)
                dve.wait_ge(kv_step, b * 2 + 1)
                v.tensor_tensor(kvp[:, 9:10], kvp[:, 8:9], par("bq"), ALU.mult).then_inc(kv_step, 1)
                with dve.Fori(0, NT // 2) as tp:
                    for h in range(2):
                        t = tp * 2 + h
                        dve.wait_ge(q_ready, HEAD + b * NT + t + 1)
                        v.tensor_tensor(tile(brf[0], t), tile(brf[0], t), tile(brf[2], t), ALU.add).then_inc(x2_ready, 1)
                norm_tokens(1)
                NS = L // P
                g3 = [gates[:, q, :, :] for q in range(4)]
                dve.wait_ge(logits_mm, b + 1)
                v.tensor_tensor(g3[1], pz[:, 0:NS * NE].rearrange("c (s e) -> c s e", e=NE),
                                    par("rb").unsqueeze(1).broadcast_to([P, NS, NE]), ALU.add).then_inc(logits_step, 1)
                dve.wait_ge(logits_step, b * 3 + 1)
                v.tensor_reduce(gmx[:, 0, :], g3[1], AX.X, ALU.max).then_inc(logits_step, 1)
                dve.wait_ge(logits_step, b * 3 + 2)
                v.tensor_tensor(g3[2], g3[1], gmx[:, 0, :].unsqueeze(2).broadcast_to([P, NS, NE]), ALU.subtract).then_inc(logits_step, 1)
                def spread(row):
                    return row.unsqueeze(2).broadcast_to([P, NS, NE])

                order_ = par("first").unsqueeze(1).broadcast_to([P, NS, NE])
                g = b * GATE_STEPS

                def best(logits, maximum, maximum_order, picked, g):
                    v.tensor_tensor(top[0], logits, spread(maximum), ALU.is_equal).then_inc(gate_step, 1)
                    dve.wait_ge(gate_step, g + 1)
                    v.tensor_tensor(top[1], top[0], order_, ALU.mult).then_inc(gate_step, 1)
                    dve.wait_ge(gate_step, g + 2)
                    v.tensor_reduce(maximum_order, top[1], AX.X, ALU.max).then_inc(gate_step, 1)
                    dve.wait_ge(gate_step, g + 3)
                    v.tensor_tensor(picked, top[1], spread(maximum_order), ALU.is_equal).then_inc(gate_step, 1)
                    dve.wait_ge(gate_step, g + 4)

                best(g3[1], gmx[:, 0, :], gmx[:, 1, :], top[2], g)
                v.scalar_tensor_tensor(top[3], top[2], NEVER, g3[1], ALU.mult, ALU.add).then_inc(gate_step, 1)
                dve.wait_ge(gate_step, g + 5)
                v.tensor_reduce(gmx[:, 2, :], top[3], AX.X, ALU.max).then_inc(gate_step, 1)
                dve.wait_ge(gate_step, g + 6)
                best(top[3], gmx[:, 2, :], gmx[:, 3, :], g3[3], g + 6)
                v.tensor_tensor(top[0], top[2], g3[3], ALU.add).then_inc(gate_step, 1)
                dve.wait_ge(gate_step, g + 11)
                dve.wait_ge(gates_exp, b + 1)
                v.tensor_tensor(g3[1], top[0], g3[0], ALU.mult).then_inc(gate_step, 1)
                dve.wait_ge(gate_step, g + 12)
                v.tensor_reduce(gmx[:, 0, :], g3[1], AX.X, ALU.add).then_inc(gate_step, 1)
                dve.wait_ge(gate_step, g + 13)
                v.reciprocal(gmx[:, 1, :], gmx[:, 0, :]).then_inc(gate_step, 1)
                dve.wait_ge(gate_step, g + 14)
                v.tensor_tensor(g3[0], g3[1], spread(gmx[:, 1, :]), ALU.mult).then_inc(gates_ready, 1)

                def weigh(h, e, s):
                    dve.wait_ge(gates_ready, b + 1)
                    dve.wait_ge(expert_mm, HEAD + e + 1)
                    dve.wait_ge(half_ready, HEAD + e - 1)
                    gate = gates[:, 0, s, :] if isinstance(s, int) else gates[:, 0, bass.ds(s, 1), :].rearrange("c o e -> c (o e)")
                    v.tensor_tensor(mix[h][:], (px, pd)[h][:].rearrange("c (e n) -> c e n", e=NE),
                                    gate.unsqueeze(2).broadcast_to([P, NE, P]), ALU.mult).then_inc(weighed, 1)

                def quarter(h, e):
                    dve.wait_ge(half_ready, HEAD + e + 1)
                    dve.wait_ge(comb_mm, HEAD + e - 1)
                    v.tensor_tensor(quarter_sum[h], half_sum[h][:, 0:2, :], half_sum[h][:, 2:4, :],
                                    ALU.add).then_inc(quarter_ready, 1)

                def finish(h, e, s):
                    dve.wait_ge(comb_mm, HEAD + e + 1)
                    cols = slice(s * P, (s + 1) * P) if isinstance(s, int) else bass.ds(s * P, P)
                    v.tensor_tensor(brf[3][:, cols], brf[0][:, cols], (pz, py)[h][:, 0:P], ALU.add).then_inc(out_ready, 1)

                e0 = dve.snap(b * NS)
                weigh(0, e0, 0)
                for s in (1, 2, 3):
                    weigh(s % 2, e0 + s, s)
                    quarter((s - 1) % 2, e0 + s - 1)
                    if s == 3:
                        finish(0, e0, 0)
                with dve.Fori(2, NS // 2) as s2:
                    e = dve.snap(b * NS + s2 * 2)
                    for h in range(2):
                        weigh(h, e + h, s2 * 2 + h)
                        quarter(1 - h, e + h - 1)
                        finish(1 - h, e + h - 3, s2 * 2 + h - 3)
                quarter(1, e0 + NS - 1)
                for s in (NS - 3, NS - 2, NS - 1):
                    finish(s % 2, e0 + s, s)
                dve.wait_ge(out_ready, HEAD + (b + 1) * NS)
                v.memset(y1[:, 0:1], 0.0).then_inc(image_done, 1)


def kernel(**inputs):
    import concourse.bacc as _bacc
    from concourse.bass_utils import run_bass_kernel_spmd as _run

    f32 = np.float32
    pre = "L0_conv_"
    w = {k: np.ascontiguousarray(v) for k, v in inputs.items()}
    half = P // 2
    dim_t = 10000.0 ** (np.arange(0, half, 2, dtype=f32) / half)
    ang = np.arange(HW, dtype=f32)[:, None] / dim_t
    emb = np.stack([np.sin(ang), np.cos(ang)], 2).reshape(HW, -1).T.astype(f32)
    r = np.arange(P)
    c_sel = np.tile(np.eye(NBR * NH, dtype=f32), (3, 1))
    first = np.arange(NE, 0, -1, dtype=f32)
    rows = [w[pre + "A_log"].reshape(-1), w[pre + "dt_bias"].reshape(-1), w[pre + "Dp"].reshape(-1),
            w[pre + "se_w1"].T.reshape(-1), w[pre + "se_b1"], w[pre + "se_w2"].T.reshape(-1), w[pre + "se_b2"],
            w["L1_ffn_router_b"], first]
    cols = [w[pre + "gn_gamma"], w[pre + "gn_beta"], w["L1_attn_bq"], w["L1_attn_bk"], w["L1_attn_bv"]]
    small = np.concatenate([np.broadcast_to(np.concatenate(rows), (P, sum(x.size for x in rows))),
                            np.stack(cols, 1)], 1)
    arrays = {
        "x": w["x"].reshape(NB, P, L),
        "c_ident": np.eye(P, dtype=f32),
        "c_upto": (r[:, None] <= r[None, :]).astype(f32),
        "c_after": (r[:, None] > r[None, :]).astype(f32),
        "c_group": (r[:, None] // 16 == r[None, :] // 16).astype(f32) / f32(16),
        "c_sel": c_sel,
        "c_pos": np.concatenate([emb, emb]),
        "small": small,
        "w_in": w[pre + "W_in"],
        "conv_w": w[pre + "conv_w"].reshape(NBR, TAPS, XT, P).transpose(3, 0, 2, 1),
        "w_out": w[pre + "W_out"].reshape(NBR, DIN, P),
        "norm_w": w[pre + "norm_w"].reshape(NBR, 2, P).transpose(2, 0, 1),
        "proj_w": w[pre + "proj_w"].T,
        "pos_w": w[pre + "pos_proj_w"].T,
        "local_w": w[pre + "local_w"].reshape(P, 9),
        "wq": w["L1_attn_Wq"], "wk": w["L1_attn_Wk"], "wv": w["L1_attn_Wv"],
        "router": w["L1_ffn_router_w"], "expert_w": w["L1_ffn_expert_w"], "expert_b": w["L1_ffn_expert_b"],
    }
    arrays = {k: np.ascontiguousarray(v) for k, v in arrays.items()}
    nc = _bacc.Bacc("TRN2", target_bir_lowering=False, num_devices=1)
    aps = {k: nc.dram_tensor(f"in_{k}", v.shape, mybir.dt.from_np(v.dtype), kind="ExternalInput").ap()
           for k, v in arrays.items()}
    aps["out"] = nc.dram_tensor("out_0", (NB, P, L), F32, kind="ExternalOutput").ap()
    hybrid_kernel(nc, aps)
    res = _run(nc, [{f"in_{k}": v for k, v in arrays.items()}], core_ids=[0])
    return res.results[0]["out_0"].reshape(NB, P, HW, HW)
```

```python
from contextlib import ExitStack

import numpy as np

import concourse.bass as bass
from concourse import mybir

F32 = mybir.dt.float32
BF16 = mybir.dt.bfloat16
ALU = mybir.AluOpType
ACT = mybir.ActivationFunctionType
AX = mybir.AxisListType

P = 128
NB = 8
HW = 64
L = HW * HW
NBR = 4
DIN, DS, NH, HD = 256, 64, 8, 32
TAPS = 4
XT = 3
Q = 128
UT = 2 * Q
ROWS = UT // HW
NG = L // UT
BG = 2
BU = BG * NBR
ROWF = HW + 6
SLABS = HW // ROWS
HEAD = 4
NE = 8
TT = 512
NT = L // TT
NEVER = -1e30
LN_EPS, GN_EPS = 1e-5, 1e-5
CONVS = NG * NBR + 2
SILUS = NG * NBR + 1
AHEAD = 2 * NG * NBR + 1
GC = 2 * NBR * NH
SE_STEPS, GN_STEPS, GATE_STEPS = 7, 5, 14
TROW = TT // HW
LOCAL_PE = 3
LOCAL_ROWS = HW - LOCAL_PE * TROW

LOG1P = [0.9999999991556807, -0.499999794913725, 0.33332497543045325, -0.24986496454167328, 0.19885820254416264,
         -0.16087622903223123, 0.12377995638908859, -0.0818804061299571, 0.041006571120306035,
         -0.013187825375511738, 0.0019866963583891365]


def hybrid_kernel(nc, a):
    with ExitStack() as ctx:
        def sb(name, shape, dt=F32):
            return ctx.enter_context(nc.sbuf_tensor(name, shape, dt))

        def sem(name):
            return ctx.enter_context(nc.semaphore(name))

        ident = sb("ident", [P, P])
        upto = sb("upto", [P, P])
        after = sb("after", [P, P])
        ones = sb("ones", [P, P])
        mean_w = sb("mean_w", [P, P])
        group_avg = sb("group_avg", [P, P])
        selbase = sb("selbase", [96, 32])
        sel = sb("sel", [96, 32], BF16)
        ident_b = sb("ident_b", [P, P], BF16)
        never = sb("never", [P, P], BF16)
        nsel = sb("nsel", [96, 32], BF16)
        small = sb("small", [P, 256])
        w_in = sb("w_in", [P, NBR, 648])
        conv_w = sb("conv_w", [P, NBR, XT, TAPS])
        w_out = sb("w_out", [P, NBR, 2, P])
        norm_w = sb("norm_w", [P, NBR, 2])
        proj_w = sb("proj_w", [P, 5, P])
        wqkv = sb("wqkv", [P, 3, P])
        router = sb("router", [P, NE])
        expert_b = sb("expert_b", [NE, P])
        pos_t = sb("pos_t", [P, HW])
        pos_w = sb("pos_w", [P, P])
        pos = sb("pos", [P, 2, HW])
        local_w = sb("local_w", [P, 9])
        local_diag = sb("local_diag", [P, 9, P])
        at = {}
        col = 0
        for name, n in (("A", 32), ("dtb", 32), ("Dp", 32), ("w1", 10), ("b1", 2), ("w2", 10), ("b2", 5), ("rb", NE),
                        ("first", NE), ("gamma", 1), ("beta", 1), ("bq", 1), ("bk", 1), ("bv", 1)):
            at[name] = (col, col + n)
            col += n
        assert col <= 256

        def par(name):
            return small[:, at[name][0]:at[name][1]]

        xp = sb("xp", [P, ROWF, ROWF])
        arena = sb("arena", [P, L])
        br = [sb(f"br{i}", [P, HW, HW]) for i in range(NBR)] + [arena[:].rearrange("c (h w) -> c h w", h=HW)]
        brf = [(t if t is br[4] else t[:]).rearrange("c h w -> c (h w)") for t in br]
        ust = [[sb(f"ust{p}{i}", [P, UT]) for i in range(NBR)] for p in range(2)]
        pre = [sb(f"pre{i}", [P, XT, 3 + UT]) for i in range(2)]
        past = [sb(f"past{i}", [P, XT, 3]) for i in range(NBR)]
        acc = [arena[:, i * XT * UT:(i + 1) * XT * UT].rearrange("c (t n) -> c t n", t=XT) for i in range(2)]
        th = sb("th", [P, XT, UT])
        xbc = [arena[:, i * XT * UT:(i + 1) * XT * UT].rearrange("c (t n) -> c t n", t=XT) for i in range(2, 4)]
        bt = [arena[:, 3072 + i * UT:3072 + (i + 1) * UT] for i in range(2)]
        xtok = [sb(f"xtok{i}", [P, XT, P]) for i in range(2)]
        ebuf = sb("ebuf", [P, NH, P])
        gm = [sb(f"gm{i}", [P, P]) for i in range(2)]
        mix = [sb(f"mix{i}", [P, NH, P]) for i in range(2)]
        xd = [sb(f"xd{i}", [P, 2, DIN]) for i in range(2)]
        dx = [sb(f"dx{i}", [P, DIN]) for i in range(2)]
        state = [sb(f"state{i}", [P, 2, DIN]) for i in range(NBR)]
        hd = [arena[:, 3584 + i * UT:3584 + (i + 1) * UT] for i in range(2)]
        y1 = sb("y1", [P, DIN])
        y2 = sb("y2", [P, DIN])
        y3 = sb("y3", [P, DIN])
        y4 = [sb(f"y4{i}", [P, 2, DIN]) for i in range(2)]
        sqj = sb("sqj", [P, DIN])
        ss = sb("ss", [P, 2])
        sv = sb("sv", [P, 2])
        rs = sb("rs", [P, 2])
        mhalf = sb("mhalf", [P, 2])
        epsy = sb("epsy", [P, 2])
        tz = sb("tz", [P, 2, DIN])
        zg = [sb(f"zg{i}", [P, 2, DIN]) for i in range(2)]
        y5 = sb("y5", [P, 2, DIN])
        yts = sb("yts", [P, 2, UT])
        dtx = sb("dtx", [P, GC])
        dte = sb("dte", [P, 3, GC])
        dtp = sb("dtp", [P, GC])
        lna = sb("lna", [P, GC])
        ec = [sb(f"ec{i}", [P, 3, GC]) for i in range(2)]
        wd = [sb(f"wd{i}", [P, 2 * NBR, 2, NH]) for i in range(2)]
        cum = [sb(f"cum{i}", [96, UT], BF16) for i in range(2)]
        cr = sb("cr", [96, UT])
        cr2 = sb("cr2", [96, UT])
        sums = sb("sums", [P, 8])
        bnst = sb("bnst", [P, NT, 6])
        gst = sb("gst", [P, 16])
        se = sb("se", [P, 40])
        sew = sb("sew", [P, 5])
        gmx = sb("gmx", [P, 4, L // P])
        eps = sb("eps", [P, 1])
        kvp = sb("kvp", [P, 16])
        expert_w = sb("expert_w", [P, NE, P])
        lna3 = sb("lna3", [P, 2, 96])
        ks = [zg[i][:].rearrange("c j d -> c (j d)") for i in range(2)]
        dump = tz[:].rearrange("c j d -> c (j d)")
        gates = ebuf[:].rearrange("c a (s e) -> c (a s) e", e=NE).rearrange("c (q s) e -> c q s e", q=4)
        xst = [y5[:, i, 0:P] for i in range(2)]
        top = [mix[0][:].rearrange("c e n -> c (e n)")[:, i * (L // P) * NE:(i + 1) * (L // P) * NE]
               .rearrange("c (s e) -> c s e", e=NE) for i in range(4)]
        half_sum = [y4[i][:].rearrange("c j (e n) -> c (j e) n", n=P) for i in range(2)]
        quarter_sum = [y[:].rearrange("c (e n) -> c e n", n=P) for y in (y2, y3)]
        C = slice(DS, P)

        def bank(name, n=1):
            return ctx.enter_context(nc.psum_tensor(name, [P, 512 * n], F32))
        px = bank("px", 2)
        pz = bank("pz")
        pd = bank("pd", 2)
        py = bank("py")
        pt = bank("pt")
        pyt = bank("pyt")
        XS = XT * UT

        def local_out(q):
            return (px[:, 0:TT], px[:, TT:2 * TT], pd[:, 0:TT])[q]

        x_tile_in = [sem("x_tile_in0"), sem("x_tile_in1")]
        pool_set, image_begun, row_added, local_step, fuse_step, norm_step = (sem(n) for n in
            ("pool_set", "image_begun", "row_added", "local_step", "fuse_step", "norm_step"))
        weights_in, pos_mm, params_scaled, selectors_made, a_step, image_in = (sem(n) for n in
            ("weights_in", "pos_mm", "params_scaled", "selectors_made", "a_step", "image_in"))
        xp_ready, local_ready, out_stored, abs_ready, log_step = (sem(n) for n in
            ("xp_ready", "local_ready", "out_stored", "abs_ready", "log_step"))
        poly_step, part_step, past_kept, tap_step, y1_ready, y3_ready = (sem(n) for n in
            ("poly_step", "part_step", "past_kept", "tap_step", "y1_ready", "y3_ready"))
        sv_ready, sums_act, desc_mm, se_step, se_nonlin = (sem(n) for n in
            ("sv_ready", "sums_act", "desc_mm", "se_step", "se_nonlin"))
        se_ready, gn_step, group_mm, group_rsqrt, affine_ready, gelu_ready = (sem(n) for n in
            ("se_ready", "gn_step", "group_mm", "group_rsqrt", "affine_ready", "gelu_ready"))
        local_mm, x1_ready, kv_step, logits_mm, logits_step, gate_step, gates_exp = (sem(n) for n in
            ("local_mm", "x1_ready", "kv_step", "logits_mm", "logits_step", "gate_step", "gates_exp"))
        gates_ready, gates_turned, gates_copied = (sem(n) for n in
            ("gates_ready", "gates_turned", "gates_copied"))
        staged, wd_ready, dx_ready, hd_ready, y4_ready, rs_ready = (sem(n) for n in
            ("staged", "wd_ready", "dx_ready", "hd_ready", "y4_ready", "rs_ready"))
        dt_mm, cum_mm, x_mm, bc_mm, pairs_mm, decay_mm = (sem(n) for n in
            ("dt_mm", "cum_mm", "x_mm", "bc_mm", "pairs_mm", "decay_mm"))
        y_mm, state_mm, z_mm, yt_mm, out_mm, proj_mm = (sem(n) for n in
            ("y_mm", "state_mm", "z_mm", "yt_mm", "out_mm", "proj_mm"))
        mean_mm, var_mm, kv_mm, q_mm, expert_mm, comb_mm = (sem(n) for n in
            ("mean_mm", "var_mm", "kv_mm", "q_mm", "expert_mm", "comb_mm"))
        dt_exp, cum_exp, bc_copied, conv_tanh_ready, bt_ready, xtok_ready = (sem(n) for n in
            ("dt_exp", "cum_exp", "bc_copied", "conv_tanh_ready", "bt_ready", "xtok_ready"))
        gm_ready, ebuf_ready, squared, tz_ready, yts_ready, branch_copied = (sem(n) for n in
            ("gm_ready", "ebuf_ready", "squared", "tz_ready", "yts_ready", "branch_copied"))
        proj_copied, squares_ready, rstd_ready, k_ready, q_ready, xst_ready = (sem(n) for n in
            ("proj_copied", "squares_ready", "rstd_ready", "k_ready", "q_ready", "xst_ready"))
        ln_ready, half_ready, quarter_ready, y5_ready, x_copied, x_tap0, bc_tap0 = (sem(n) for n in
            ("ln_ready", "half_ready", "quarter_ready", "y5_ready", "x_copied", "x_tap0", "bc_tap0"))
        dtx_ready, lna_ready, cum_ready, acc_ready, xbc_ready, mix_ready = (sem(n) for n in
            ("dtx_ready", "lna_ready", "cum_ready", "acc_ready", "xbc_ready", "mix_ready"))
        xd0_ready, xd1_ready, state_ready, y2_ready, zg_ready, fused_ready = (sem(n) for n in
            ("xd0_ready", "xd1_ready", "state_ready", "y2_ready", "zg_ready", "fused_ready"))
        centered, normed, kv_summed, x2_ready, weighed, out_ready = (sem(n) for n in
            ("centered", "normed", "kv_summed", "x2_ready", "weighed", "out_ready"))

        def head_start(eng, guards):
            for guard in guards:
                eng.sem_inc(guard, HEAD)

        def order(i, image, g):
            if i % 2 == 0:
                return image[:, bass.ds(g * ROWS, ROWS), 0:HW]
            return image[:, 0:HW, bass.ds(g * ROWS, ROWS)].rearrange("c s r -> c r s")

        def scan_rows(i, seq):
            if i < 2:
                return [(slice(0, ROWS), seq)]
            return [(slice(0, ROWS, 2), seq[:, 0:ROWS:2, :]), (slice(1, ROWS, 2), seq[:, 1:ROWS:2, ::-1])]

        interior = xp[:, 1:ROWF, 1:ROWF]
        loads = [
            (ident[:], a["c_ident"]), (upto[:], a["c_upto"]), (after[:], a["c_after"]),
            (group_avg[:], a["c_group"]), (selbase[:], a["c_sel"]), (pos_t[:], a["c_pos"]),
            (small[:, 0:col], a["small"]), (w_in[:], a["w_in"].rearrange("i c n -> c i n")),
            (conv_w[:], a["conv_w"]), *[(w_out[:, i, :, :], a["w_out"][i].rearrange("(k c) n -> c k n", k=2)) for i in range(NBR)],
            (norm_w[:], a["norm_w"]), (proj_w[:], a["proj_w"].rearrange("(j i) o -> i j o", j=5)),
            (wqkv[:, 0, :], a["wq"]), (wqkv[:, 1, :], a["wk"]), (wqkv[:, 2, :], a["wv"]),
            (router[:], a["router"]), (expert_b[:], a["expert_b"]), (pos_w[:], a["pos_w"]), (local_w[:], a["local_w"]),
            (expert_w[:], a["expert_w"].rearrange("e d c -> d e c")),
        ]
        block = ctx.enter_context(nc.Block())

        @block.sync
        def _(sp):
            head_start(sp, (out_stored,))
            for dst, src in loads:
                sp.dma_start(dst, src).then_inc(weights_in, 16)
            sp.dma_start(brf[4], a["x"][0]).then_inc(image_in, 16)

            def image(b, following):
                with sp.Fori(0, NT // 2) as tp:
                    for h in range(2):
                        t = tp * 2 + h
                        sp.wait_ge(se_ready, b + 1)
                        sp.wait_ge(fused_ready, HEAD + b * NT + t - 1)
                        sp.dma_start(ks[h], tokens_of("x", b, t * TT, TT)).then_inc(x_tile_in[h], 16)
                sp.wait_ge(fused_ready, HEAD + (b + 1) * NT)
                sp.dma_start(brf[4], following).then_inc(image_in, 16)
                with sp.Fori(0, L // (2 * P)) as sp2:
                    sp.wait_ge(out_ready, HEAD + b * (L // P) + sp2 * 2 + 2)
                    sp.dma_start(tokens_of("out", b, sp2 * 2 * P, 2 * P),
                                 brf[3][:, bass.ds(sp2 * 2 * P, 2 * P)]).then_inc(out_stored, 16)

            def tokens_of(name, b, start, n):
                rows = slice(b, b + 1) if isinstance(b, int) else bass.ds(b, 1)
                return a[name][rows, :, bass.ds(start, n)].rearrange("o c n -> (o c) n")

            with sp.Fori(0, NB - 1) as b:
                image(b, a["x"][bass.ds(b + 1, 1)].rearrange("o c n -> (o c) n"))
            image(NB - 1, a["x"][0])
            sp.wait_ge(out_stored, HEAD + NB * 16 * (L // (2 * P)))

        @block.gpsimd
        def _(pool):
            head_start(pool, (staged, wd_ready, dx_ready, hd_ready, y4_ready, rs_ready, half_ready, xd1_ready))
            pool.memset(ones[:], 1.0)
            pool.memset(mean_w[:], 1.0 / P)
            pool.memset(epsy[:], 4e-5)
            pool.memset(mhalf[:], -0.5).then_inc(pool_set, 1)
            pool.wait_ge(weights_in, 16 * len(loads))
            pool.wait_ge(pool_set, 1)

            def stage(b, g, i, p):
                pieces = scan_rows(i, ust[p][i][:].rearrange("c (r s) -> c r s", r=ROWS))
                for k, (rows, dst) in enumerate(pieces):
                    ins = pool.tensor_copy(dst, order(i, interior, g)[:, rows, :])
                ins.then_inc(staged, 1)

            def add_rows(rows):
                n = HW if rows == slice(0, HW) else ROWS
                pool.tensor_tensor(interior[:, rows, 0:HW], br[4][:, rows, :],
                                   pos[:, 0, rows].unsqueeze(2).broadcast_to([P, n, HW]), ALU.add).then_inc(row_added, 1)

            def add_columns(rows):
                n = HW if rows == slice(0, HW) else ROWS
                return pool.tensor_tensor(interior[:, rows, 0:HW], interior[:, rows, 0:HW],
                                          pos[:, 1, :].unsqueeze(1).broadcast_to([P, n, HW]), ALU.add)

            pool.wait_ge(params_scaled, 1)
            pool.wait_ge(image_in, 16)
            add_rows(slice(0, HW))
            pool.wait_ge(row_added, 1)
            add_columns(slice(0, HW)).then_inc(xp_ready, SLABS)
            with pool.Fori(0, NB) as b:
                pool.wait_ge(xp_ready, (b + 1) * SLABS)
                pool.tensor_tensor(sv[:], epsy[:], epsy[:], ALU.mult).then_inc(image_begun, 1)
                for i in range(NBR):
                    pieces = scan_rows(i, ust[0][i][:].rearrange("c (r s) -> c r s", r=ROWS))
                    src = (interior[:, 0:ROWS, 0:HW] if i % 2 == 0 else
                           interior[:, 0:HW, 0:ROWS].rearrange("c s r -> c r s"))
                    for rows, dst in pieces:
                        ins = pool.tensor_copy(dst, src[:, rows, :])
                    ins.then_inc(staged, 1)
                pool.wait_ge(cum_exp, HEAD + b * (NG + 1) + 1)
                pool.tensor_tensor(wd[0][:, :, 1, :], ec[0][:, 1, :].rearrange("c (u h) -> c u h", h=NH),
                                       wd[0][:, :, 0, :], ALU.mult).then_inc(wd_ready, 1)

                def y34(n, m, j, k):
                    pool.wait_ge(y2_ready, HEAD + m + 1)
                    pool.wait_ge(y4_ready, HEAD + m)
                    pool.wait_ge(dx_ready, HEAD + m + 1)
                    pool.tensor_tensor(y3[:], y2[:], dx[j][:], ALU.add).then_inc(y3_ready, 1)
                    pool.wait_ge(y3_ready, m + 1)
                    pool.wait_ge(zg_ready, HEAD + n + 1)
                    pool.wait_ge(y5_ready, HEAD + n - 1)
                    pool.tensor_tensor(y4[k % 2][:, j, :], y3[:], zg[k % 2][:, j, :], ALU.mult).then_inc(y4_ready, 1)

                def norm_factor(n):
                    pool.wait_ge(squared, HEAD + 2 * n + 2)
                    pool.wait_ge(y5_ready, HEAD + n)
                    pool.tensor_tensor(sv[:], ss[:], epsy[:], ALU.add).then_inc(sv_ready, 1)
                    pool.wait_ge(sv_ready, n + 1)
                    pool.tensor_tensor(rs[:], sv[:], mhalf[:], ALU.pow).then_inc(rs_ready, 1)

                def body(gg, head):
                    u, c = pool.snap(b * (NG * NBR) + gg * BU), pool.snap(b * (NG * NBR * 2) + gg * 2 * BU)
                    a_ = pool.snap(b * AHEAD + gg * 2 * BU)
                    g17, g2 = pool.snap(b * (NG + 1) + gg * BG), gg * BG if head else pool.snap(gg * BG)
                    def skip_term(j, m, t):
                        pool.wait_ge(xtok_ready, HEAD + t + 1)
                        pool.wait_ge(y4_ready, HEAD + m - 1)
                        pool.tensor_tensor(
                            dx[j][:].rearrange("c (h d) -> c h d", h=NH),
                            xtok[j][:, 0:2, :].rearrange("c a (h d) -> c (a h) d", d=HD),
                            par("Dp")[:, i * NH:(i + 1) * NH].unsqueeze(2).broadcast_to([P, NH, HD]),
                            ALU.mult).then_inc(dx_ready, 1)

                    def scale_tokens(m, t):
                        pool.wait_ge(xtok_ready, HEAD + t + 1)
                        pool.wait_ge(wd_ready, HEAD + g17 + p + 1)
                        pool.wait_ge(y_mm, HEAD + m - 1)
                        pool.tensor_tensor(
                            xd[1][:].rearrange("c q (h d) -> c q h d", h=NH),
                            xtok[1][:, 0:2, :].rearrange("c a (h d) -> c (a h) d", d=HD)
                            .unsqueeze(1).broadcast_to([P, 2, NH, HD]),
                            wd[p][:, NBR + i, :, :].unsqueeze(3).broadcast_to([P, 2, NH, HD]),
                            ALU.mult).then_inc(xd1_ready, 1)

                    def decay_state(j, m):
                        pool.wait_ge(cum_exp, HEAD + g17 + p + 1)
                        pool.wait_ge(state_ready, HEAD + (m - 1 if j == 0 else m))
                        dec = ec[p][:, 2, (j * NBR + i) * NH:(j * NBR + i + 1) * NH]
                        pool.tensor_tensor(
                            hd[j].rearrange("c (h d) -> c h d", h=NH),
                            state[i][:, j, :].rearrange("c (h d) -> c h d", h=NH),
                            dec.unsqueeze(2).broadcast_to([P, NH, HD]), ALU.mult).then_inc(hd_ready, 1)

                    for k in range(BU):
                        i, p = k % NBR, k // NBR
                        n, m = u + k, c + 2 * k
                        decay_state(0, m)
                        if k > 0 or not head:
                            y34(n - 1, m - 1, 1, k - 1)
                        skip_term(0, m, a_ + 2 * k)
                        if k > 0 or not head:
                            norm_factor(n - 1)
                        if i == 0:
                            pool.wait_ge(z_mm, HEAD + n)
                        scale_tokens(m + 1, a_ + 2 * k + 1)
                        skip_term(1, m + 1, a_ + 2 * k + 1)
                        decay_state(1, m + 1)
                        if i < 2:
                            for q in (2 * i, 2 * i + 1):
                                stage(b, g2 + p + 1, q, 1 - p)
                        if i == 3:
                            pool.wait_ge(cum_exp, HEAD + g17 + p + 2)
                            pool.wait_ge(xd0_ready, HEAD + n - 3)
                            pool.wait_ge(xd1_ready, HEAD + n - 3)
                            w = 1 - p
                            pool.tensor_tensor(
                                wd[w][:, :, 1, :], ec[w][:, 1, :].rearrange("c (u h) -> c u h", h=NH),
                                wd[w][:, :, 0, :], ALU.mult).then_inc(wd_ready, 1)
                        y34(n, m, 0, k)

                body(0, True)
                with pool.Fori(1, NG // BG) as gg:
                    body(gg, False)
                units = pool.snap((b + 1) * (NG * NBR))
                y34(units - 1, 2 * units - 1, 1, BU - 1)
                norm_factor(units - 1)
                pool.wait_ge(gn_step, b * GN_STEPS + 4)
                pool.tensor_tensor(gst[:, 8:9], gst[:, 7:8], mhalf[:, 0:1], ALU.pow).then_inc(group_rsqrt, 1)
                with pool.Fori(0, L // (2 * P)) as s2:
                    e = pool.snap(b * (L // P) + s2 * 2)
                    rows = bass.ds(s2 * ROWS, ROWS)
                    for h in range(2):
                        if h == 0:
                            pool.wait_ge(image_in, (b + 2) * 16)
                            pool.wait_ge(local_ready, b + 1)
                            pool.wait_ge(local_mm, (b + 1) * LOCAL_PE)
                        else:
                            pool.wait_ge(row_added, b * SLABS + s2 + 2)
                        pool.wait_ge(weighed, HEAD + e + h + 1)
                        pool.wait_ge(quarter_ready, HEAD + e + h - 1)
                        pool.tensor_tensor(half_sum[h], mix[h][:, 0:4, :], mix[h][:, 4:8, :], ALU.add).then_inc(half_ready, 1)
                        if h == 0:
                            add_rows(rows)
                        else:
                            add_columns(rows).then_inc(xp_ready, 1)

        @block.tensor
        def _(pe):
            mm = nc.tensor.matmul
            head_start(pe, (dt_mm, cum_mm, x_mm, bc_mm, pairs_mm, decay_mm, y_mm, state_mm, z_mm, yt_mm, out_mm,
                            proj_mm, mean_mm, var_mm, kv_mm, q_mm, expert_mm, comb_mm))
            pe.wait_ge(weights_in, 16 * len(loads))
            mm(pt[:, 0:HW], pos_w[0:DS, :], pos_t[0:DS, :], start=True, stop=True)
            mm(pyt[:, 0:HW], pos_w[DS:P, :], pos_t[DS:P, :], start=True, stop=True).then_inc(pos_mm, 1)
            pe.wait_ge(selectors_made, 1)
            pe.wait_ge(params_scaled, 1)

            def project_steps(p):
                for j in range(2):
                    for i in range(NBR):
                        o = XS + (j * NBR + i) * NH
                        ins = mm(px[:, o:o + NH], ust[p][i][:, j * Q:(j + 1) * Q], w_in[:, i, 640:648],
                                 start=True, stop=True, skip_group_check=True)
                ins.then_inc(dt_mm, 1)

            def sum_decays(p):
                for q, w in enumerate((upto, after, ones)):
                    mm(px[:, XS + GC * (q + 1):XS + GC * (q + 2)], w[:], lna[:], start=True, stop=True,
                       skip_group_check=True)
                for j in range(2):
                    rows = lna3[:, j, :]
                    ins = mm(px[0:96, 2 * UT + j * Q:2 * UT + (j + 1) * Q], rows, upto[:], start=True, stop=True,
                             skip_group_check=True)
                ins.then_inc(cum_mm, 1)

            def project_x(i, p, tiles, done):
                for t in tiles:
                    ins = mm(px[:, t * UT:(t + 1) * UT], w_in[:, i, DIN + t * P:DIN + (t + 1) * P], ust[p][i][:],
                             start=True, stop=True, skip_group_check=True)
                ins.then_inc(done, 1)

            with pe.Fori(0, NB) as b:
                pe.wait_ge(xp_ready, (b + 1) * SLABS)
                pe.wait_ge(staged, HEAD + (b * (NG + 1) + 1) * NBR)
                project_steps(0)
                pe.wait_ge(lna_ready, HEAD + b * (NG + 1) + 1)
                sum_decays(0)
                pe.wait_ge(cum_exp, HEAD + b * (NG + 1) + 1)
                pe.wait_ge(cum_ready, HEAD + b * (NG + 1) + 1)
                project_x(0, 0, (0, 1), x_mm)
                project_x(0, 0, (2,), bc_mm)

                def decays(k, j, g, q):
                    p, i = k // NBR % 2, k % NBR
                    pe.wait_ge(cum_ready, HEAD + g + k // NBR + 1)
                    pe.wait_ge(ebuf_ready, HEAD + q)
                    part = cum[p][:, j * Q:(j + 1) * Q]
                    for half in range(2):
                        r = i * NH + half * 4
                        mm(pd[:, half * 512:(half + 1) * 512], ident_b[:], never[:].unsqueeze(1).broadcast_to([P, 4, P]),
                           start=True, stop=False, skip_group_check=True)
                        mm(pd[:, half * 512:(half + 1) * 512], part, nsel[:, r:r + 4].unsqueeze(2).broadcast_to([96, 4, P]),
                           start=False, stop=False, skip_group_check=True)
                        for h in range(4):
                            ins = mm(pd[:, half * 512 + h * Q:half * 512 + (h + 1) * Q],
                                     sel[:, r + h:r + h + 1].broadcast_to([96, P]), part,
                                     start=False, stop=(h == 3), skip_group_check=True)
                    ins.then_inc(decay_mm, 1)

                def turn_and_pair(k, j, v_, q):
                    pe.wait_ge(xbc_ready, HEAD + v_ + k + 1)
                    pe.wait_ge(xtok_ready, HEAD + q)
                    pe.wait_ge(gm_ready, HEAD + q)
                    for t in range(XT):
                        nc.tensor.transpose(pt[:, t * P:(t + 1) * P], xbc[k % 2][:, t, j * Q:(j + 1) * Q], ident[:])
                    pe.wait_ge(bt_ready, HEAD + v_ + k + 1)
                    mm(pt[:, XT * P:XT * P + P], bt[k % 2][C, j * Q:(j + 1) * Q],
                       xbc[k % 2][C, 2, j * Q:(j + 1) * Q], start=True, stop=True,
                       skip_group_check=True).then_inc(pairs_mm, 1)

                decays(0, 0, b * (NG + 1), b * AHEAD)
                pe.wait_ge(x_copied, HEAD + b * (CONVS + 1) + 1)
                project_x(1, 0, (0, 1), x_mm)
                pe.wait_ge(bc_copied, HEAD + b * CONVS + 1)
                project_x(1, 0, (2,), bc_mm)
                turn_and_pair(0, 0, b * SILUS, b * AHEAD)
                pe.wait_ge(x_copied, HEAD + b * (CONVS + 1) + 2)
                project_x(2, 0, (0, 1), x_mm)
                pe.wait_ge(bc_copied, HEAD + b * CONVS + 2)
                project_x(2, 0, (2,), bc_mm)
                def turn_back(n):
                    pe.wait_ge(y5_ready, HEAD + n + 1)
                    pe.wait_ge(yts_ready, HEAD + n)
                    for j in range(2):
                        for t in range(2):
                            ins = nc.tensor.transpose(pyt[:, t * UT + j * Q:t * UT + (j + 1) * Q],
                                                      y5[:, j, t * P:(t + 1) * P], ident[:])
                    ins.then_inc(yt_mm, 1)

                def project_out(i, n, last):
                    pe.wait_ge(yts_ready, HEAD + n + 1)
                    pe.wait_ge(zg_ready, HEAD + (n + 1 if last else n + 2))
                    for t in range(2):
                        ins = mm(pz[:, 0:UT], w_out[:, i, t, :], yts[:, t, :], start=(t == 0), stop=(t == 1),
                                 skip_group_check=True)
                    ins.then_inc(out_mm, 1)

                def body(gg, head):
                    u, c = pe.snap(b * (NG * NBR) + gg * BU), pe.snap(b * (NG * NBR * 2) + gg * 2 * BU)
                    x, g17 = pe.snap(b * CONVS + gg * BU), pe.snap(b * (NG + 1) + gg * BG)
                    us, a_ = pe.snap(b * ((NG + 1) * NBR) + gg * BU), pe.snap(b * AHEAD + gg * 2 * BU)
                    v_, xl = pe.snap(b * SILUS + gg * BU), pe.snap(b * (CONVS + 1) + gg * BU)

                    def project_x_ahead(k):
                        pe.wait_ge(staged, HEAD + us + k + 4)
                        pe.wait_ge(x_copied, HEAD + xl + k + 3)
                        project_x((k + 3) % NBR, ((k + 3) // NBR) % 2, (0, 1), x_mm)

                    def add_state(k, j, m):
                        pe.wait_ge((xd0_ready, xd1_ready)[j], HEAD + u + k + 1)
                        pe.wait_ge(state_ready, HEAD + m)
                        if j == 0:
                            pe.wait_ge(bc_copied, HEAD + x + k + 3)
                        mm(px[C, XS:XS + DIN], xtok[j][:, 2, 0:DS], xd[j][:, 1, :], start=True, stop=True,
                               skip_group_check=True).then_inc(state_mm, 1)

                    def outputs(k, j, m):
                        pe.wait_ge(mix_ready, HEAD + m + 1)
                        pe.wait_ge((xd0_ready, xd1_ready)[j], HEAD + u + k + 1)
                        pe.wait_ge(y2_ready, HEAD + m)
                        pe.wait_ge(state_ready, HEAD + m)
                        for h in range(NH):
                            mm(py[:, h * HD:(h + 1) * HD], mix[j][:, h, :], xd[j][:, 0, h * HD:(h + 1) * HD],
                               start=True, stop=True, skip_group_check=True)
                        mm(py[:, DIN:2 * DIN], xbc[k % 2][C, 2, j * Q:(j + 1) * Q], state[k % NBR][C, j, :],
                               start=True, stop=True, skip_group_check=True).then_inc(y_mm, 1)

                    def gate(k, n):
                        pe.wait_ge(branch_copied, HEAD + (n if k == 0 and head else n - 1))
                        p, i = k // NBR, k % NBR
                        for j in range(2):
                            ins = mm(pz[:, j * DIN:(j + 1) * DIN], ust[p][i][:, j * Q:(j + 1) * Q], w_in[:, i, 0:DIN],
                                     start=True, stop=True, skip_group_check=True)
                        ins.then_inc(z_mm, 1)

                    for k in range(BU):
                        n, m = u + k, c + 2 * k
                        p, i = k // NBR, k % NBR
                        decays(k, 1, g17, a_ + 2 * k + 1)
                        turn_and_pair(k, 1, v_, a_ + 2 * k + 1)
                        if i == 2:
                            pe.wait_ge(staged, HEAD + us + NBR * (p + 2))
                            pe.wait_ge(bc_copied, HEAD + x + k + 3)
                            pe.wait_ge(state_ready, HEAD + m)
                            project_steps(1 - p)
                            project_x_ahead(k)
                        if i == 3:
                            pe.wait_ge(lna_ready, HEAD + g17 + p + 2)
                            pe.wait_ge(bc_copied, HEAD + x + k + 3)
                            pe.wait_ge(state_ready, HEAD + m)
                            sum_decays(1 - p)
                        outputs(k, 0, m)
                        if i == 2:
                            pe.wait_ge(dtx_ready, HEAD + g17 + p + 2)
                        if i == 3:
                            pe.wait_ge(cum_exp, HEAD + g17 + p + 2)
                            pe.wait_ge(part_step, (g17 + p + 1) * 5 + 2)
                        add_state(k, 0, m)
                        gate(k, n)
                        if i != 2:
                            project_x_ahead(k)
                        decays(k + 1, 0, g17, a_ + 2 * k + 2)
                        if k > 0 or not head:
                            turn_back(n - 1)
                        turn_and_pair(k + 1, 0, v_, a_ + 2 * k + 2)
                        add_state(k, 1, m + 1)
                        outputs(k, 1, m + 1)
                        if k > 0 or not head:
                            project_out((k - 1) % NBR, n - 1, False)
                        pe.wait_ge(bc_copied, HEAD + x + k + 3)
                        pe.wait_ge(state_ready, HEAD + m + 2)
                        project_x((k + 3) % NBR, ((k + 3) // NBR) % 2, (2,), bc_mm)

                body(0, True)
                with pe.Fori(1, NG // BG) as gg:
                    body(gg, False)
                units = pe.snap((b + 1) * (NG * NBR))
                turn_back(units - 1)
                project_out(NBR - 1, units - 1, True)
                pe.wait_ge(x_copied, HEAD + (b + 1) * (CONVS + 1))
                pe.wait_ge(bc_copied, HEAD + (b + 1) * CONVS)
                pe.wait_ge(state_ready, HEAD + (b + 1) * (2 * NG * NBR))
                pe.wait_ge(ebuf_ready, HEAD + (b + 1) * AHEAD)
                for q in range(LOCAL_PE):
                    row = LOCAL_ROWS + q * TROW
                    for r in range(9):
                        dy, dx_ = r // 3, r % 3
                        ins = mm(local_out(q).rearrange("c (h w) -> c h w", w=HW), local_diag[:, r, :],
                                 xp[:, row + dy:row + dy + TROW, dx_:dx_ + HW], start=(r == 0), stop=(r == 8))
                    ins.then_inc(local_mm, 1)
                pe.wait_ge(sums_act, (b + 1) * (5 + LOCAL_PE))
                mm(pt[:, 0:5], ones[:], sums[:, 0:5], start=True, stop=False, skip_group_check=True)
                for q in range(LOCAL_PE):
                    ins = mm(pt[:, 0:1], ones[:], sums[:, 5 + q:6 + q], start=False, stop=(q == LOCAL_PE - 1),
                             skip_group_check=True)
                ins.then_inc(desc_mm, 1)
                with pe.Fori(0, NT // 2) as tp:
                    for h in range(2):
                        t = tp * 2 + h
                        pe.wait_ge(proj_copied, HEAD + b * NT + t - 1)
                        for j in range(5):
                            src = brf[(j + 4) % 5][:, bass.ds(t * TT, TT)]
                            ins = mm(px[:, h * TT:(h + 1) * TT], proj_w[:, j, :], src, start=(j == 0), stop=(j == 4))
                        ins.then_inc(proj_mm, 1)
                pe.wait_ge(gn_step, b * GN_STEPS + 3)
                mm(pt[:, 8:10], group_avg[:], gst[:, 2:4], start=True, stop=True).then_inc(group_mm, 1)

                def tile(buf, t):
                    return buf[:, bass.ds(t * TT, TT)]

                def norm_tokens(pass_):
                    with pe.Fori(0, NT // 2) as tp:
                        for h in range(2):
                            t = tp * 2 + h
                            e = (b * 2 + pass_) * NT + t
                            pe.wait_ge(centered, HEAD + e - 1)
                            if pass_ == 0:
                                pe.wait_ge(x1_ready, b * 4 + tp + 1)
                            else:
                                pe.wait_ge(q_ready, HEAD + (b + 1) * NT)
                            if pass_ == 1:
                                pe.wait_ge(x2_ready, HEAD + b * NT + t + 1)
                            mm((pz, py)[h][:], mean_w[:], tile(brf[0], t), start=True, stop=True).then_inc(mean_mm, 1)
                    with pe.Fori(0, NT // 2) as tp:
                        for h in range(2):
                            t = tp * 2 + h
                            e = (b * 2 + pass_) * NT + t
                            pe.wait_ge(ln_ready, HEAD + e - 1)
                            pe.wait_ge(squares_ready, HEAD + e + 1)
                            mm((pt, pyt)[h][:], mean_w[:], tile(brf[2], t), start=True, stop=True).then_inc(var_mm, 1)

                norm_tokens(0)
                with pe.Fori(0, NT // 2) as tp:
                    for h in range(2):
                        t = tp * 2 + h
                        pe.wait_ge(normed, HEAD + b * (2 * NT) + t + 1)
                        pe.wait_ge(kv_summed, HEAD + b * NT + t - 1)
                        mm(pd[:, h * TT:(h + 1) * TT], wqkv[:, 1, :], tile(brf[1], t), start=True, stop=True)
                        mm(px[:, h * TT:(h + 1) * TT], wqkv[:, 2, :], tile(brf[1], t), start=True, stop=True).then_inc(kv_mm, 1)
                with pe.Fori(0, NT // 2) as tp:
                    for h in range(2):
                        t = tp * 2 + h
                        pe.wait_ge(q_ready, HEAD + b * NT + t - 1)
                        mm((pz, py)[h][:], wqkv[:, 0, :], tile(brf[1], t), start=True, stop=True).then_inc(q_mm, 1)
                norm_tokens(1)
                for s in range(L // P):
                    pe.wait_ge(normed, HEAD + b * (2 * NT) + NT + s * P // TT + 1)
                    ins = mm(pz[:, s * NE:(s + 1) * NE], brf[1][:, s * P:(s + 1) * P], router[:], start=True, stop=True,
                             skip_group_check=True)
                ins.then_inc(logits_mm, 1)
                pe.wait_ge(gates_ready, b + 1)
                for t in range(NT):
                    if t >= 2:
                        pe.wait_ge(gates_copied, b * NT + t - 1)
                    for s in range(4):
                        ins = nc.tensor.transpose((pt, pyt)[t % 2][0:NE, s * P:(s + 1) * P],
                                                  gates[:, 0, 4 * t + s, :], ident[:])
                    ins.then_inc(gates_turned, 1)

                def experts(h, e, s):
                    pe.wait_ge(xst_ready, HEAD + e + 1)
                    pe.wait_ge(weighed, HEAD + e - 1)
                    for half in range(2):
                        ins = mm((px, pd)[h][:, half * 512:(half + 1) * 512], xst[h],
                                 expert_w[:, 4 * half:4 * half + 4, :].rearrange("d e c -> d (e c)"),
                                 start=True, stop=True)
                    ins.then_inc(expert_mm, 1)

                def combine(h, e, s):
                    pe.wait_ge(quarter_ready, HEAD + e + 1)
                    pe.wait_ge(out_ready, HEAD + e - 1)
                    pe.wait_ge(gates_copied, b * NT + NT)
                    o = (pz, py)[h][:, 0:P]
                    cols = slice(s * P, (s + 1) * P) if isinstance(s, int) else bass.ds(s * P, P)
                    mm(o, expert_b[:], brf[2][0:NE, cols], start=True, stop=False)
                    for half in range(2):
                        ins = mm(o, quarter_sum[h][:, half, :], ident[:], start=False, stop=(half == 1))
                    ins.then_inc(comb_mm, 1)

                e0 = pe.snap(b * (L // P))
                for h in range(2):
                    experts(h, e0 + h, h)
                with pe.Fori(1, L // (2 * P)) as s2:
                    e = pe.snap(b * (L // P) + s2 * 2)
                    for h in range(2):
                        experts(h, e + h, s2 * 2 + h)
                        combine(h, e + h - 2, s2 * 2 + h - 2)
                for h in range(2):
                    combine(h, e0 + L // P - 2 + h, L // P - 2 + h)

        @block.scalar
        def _(act):
            af = nc.scalar.activation
            head_start(act, (rstd_ready, ln_ready, dt_exp, cum_exp, bc_copied, conv_tanh_ready, bt_ready,
                             xtok_ready, gm_ready, ebuf_ready, squared, tz_ready, yts_ready, branch_copied,
                             proj_copied, squares_ready, k_ready, q_ready, xst_ready, y5_ready, x_copied, x_tap0,
                             bc_tap0))
            act.wait_ge(weights_in, 16 * len(loads))
            af(sel[:], selbase[:], ACT.Copy)
            af(ident_b[:], ident[:], ACT.Copy)
            af(never[:], after[:], ACT.Copy, scale=NEVER)
            af(nsel[:], selbase[:], ACT.Copy, scale=-1.0).then_inc(selectors_made, 1)
            af(par("A"), par("A"), ACT.Exp).then_inc(a_step, 1)

            def step_sizes(q):
                act.wait_ge(dtx_ready, HEAD + q + 1)
                act.wait_ge(lna_ready, HEAD + q)
                af(dte[:, 0, :], dtx[:], ACT.Relu)
                af(dte[:, 1, :], dtx[:], ACT.Abs).then_inc(abs_ready, 1)
                act.wait_ge(abs_ready, q + 1)
                af(dte[:, 2, :], dte[:, 1, :], ACT.Exp, scale=-1.0).then_inc(dt_exp, 1)

            def decay_factors(q, p):
                act.wait_ge(cum_mm, HEAD + q + 1)
                act.wait_ge(part_step, q * 5 + 2)
                af(ec[p][:].rearrange("c a n -> c (a n)"), px[:, XS + GC:XS + 4 * GC], ACT.Exp).then_inc(cum_exp, 1)

            def copy_x(k, i, xl, xn, vn):
                act.wait_ge(x_mm, HEAD + xl + 1)
                act.wait_ge(acc_ready, HEAD + xn - 1)
                o = pre[k % 2]
                af(o[:, 0:2, 0:3], past[i][:, 0:2, :], ACT.Copy)
                af(o[:, 0:2, 3:3 + UT], px[:, 0:2 * UT].rearrange("c (t n) -> c t n", t=2), ACT.Copy).then_inc(x_copied, 1)
                act.wait_ge(xbc_ready, HEAD + vn - 1)
                act.wait_ge(x_copied, HEAD + xl + 1)
                for t in range(2):
                    ins = af(acc[k % 2][:, t, :], o[:, t, 0:UT], ACT.Copy, scale=conv_w[:, i, t, 0:1])
                ins.then_inc(x_tap0, 1)
                af(past[i][:, 0:2, :], o[:, 0:2, UT:UT + 3], ACT.Copy).then_inc(past_kept, 1)

            def copy_bc(k, i, b, xn, vn):
                act.wait_ge(bc_mm, HEAD + xn + b + 1)
                act.wait_ge(acc_ready, HEAD + xn - 1)
                o = pre[k % 2]
                af(o[:, 2, 0:3], past[i][:, 2, :], ACT.Copy)
                af(o[:, 2, 3:3 + UT], px[:, 2 * UT:3 * UT], ACT.Copy).then_inc(bc_copied, 1)
                act.wait_ge(xbc_ready, HEAD + vn - 1)
                act.wait_ge(bc_copied, HEAD + xn + 1)
                af(acc[k % 2][:, 2, :], o[:, 2, 0:UT], ACT.Copy, scale=conv_w[:, i, 2, 0:1]).then_inc(bc_tap0, 1)
                af(past[i][:, 2, :], o[:, 2, UT:UT + 3], ACT.Copy).then_inc(past_kept, 1)

            def conv_tanh(k, xn, vn):
                act.wait_ge(acc_ready, HEAD + xn + 1)
                act.wait_ge(xbc_ready, HEAD + vn)
                af(th[:], acc[k % 2], ACT.Tanh).then_inc(conv_tanh_ready, 1)

            def copy_b(k, xn):
                act.wait_ge(xbc_ready, HEAD + xn + 1)
                af(bt[k % 2][C, :], xbc[k % 2][0:DS, 2, :], ACT.Copy).then_inc(bt_ready, 1)

            with act.Fori(0, NB) as b:
                act.wait_ge(out_stored, HEAD + b * 16 * (L // (2 * P)))
                step_sizes(b * (NG + 1))
                act.wait_ge(hd_ready, HEAD + b * (NG * NBR * 2))
                decay_factors(b * (NG + 1), 0)
                xl = act.snap(b * (CONVS + 1))
                copy_x(0, 0, xl, b * CONVS, b * SILUS)
                copy_bc(0, 0, b, b * CONVS, b * SILUS)
                conv_tanh(0, b * CONVS, b * SILUS)
                copy_x(1, 1, xl + 1, b * CONVS + 1, b * SILUS + 1)
                copy_bc(1, 1, b, b * CONVS + 1, b * SILUS + 1)
                copy_b(0, b * SILUS)

                def copy_tokens(j, n, m, q):
                    act.wait_ge(pairs_mm, HEAD + q + 1)
                    act.wait_ge((xd0_ready, xd1_ready)[j], HEAD + n)
                    act.wait_ge(dx_ready, HEAD + m - 1)
                    act.wait_ge(state_mm, HEAD + m - 1)
                    af(xtok[j][:], pt[:, 0:XT * P].rearrange("c (t n) -> c t n", t=XT), ACT.Copy).then_inc(xtok_ready, 1)
                    act.wait_ge(mix_ready, HEAD + m - 1)
                    af(gm[j][:], pt[:, XT * P:(XT + 1) * P], ACT.Copy).then_inc(gm_ready, 1)

                def decay_exp(m, q):
                    act.wait_ge(decay_mm, HEAD + q + 1)
                    act.wait_ge(mix_ready, HEAD + m)
                    af(ebuf[:].rearrange("c h t -> c (h t)"), pd[:], ACT.Exp).then_inc(ebuf_ready, 1)

                decay_exp(b * (NG * NBR * 2), b * AHEAD)
                copy_tokens(0, b * (NG * NBR), b * (NG * NBR * 2), b * AHEAD)
                conv_tanh(1, b * CONVS + 1, b * SILUS + 1)
                copy_x(2, 2, xl + 2, b * CONVS + 2, b * SILUS + 2)
                def square(k, j, n, m):
                    act.wait_ge(y4_ready, HEAD + m + 1)
                    act.wait_ge(rs_ready, HEAD + n)
                    act.wait_ge(squared, HEAD + m)
                    af(sqj[:], y4[k % 2][:, j, :], ACT.Square, scale=DIN ** -0.5, accum_out=ss[:, j:j + 1]).then_inc(squared, 1)

                def copy_turned(n):
                    act.wait_ge(yt_mm, HEAD + n + 1)
                    act.wait_ge(out_mm, HEAD + n)
                    af(yts[:].rearrange("c t n -> c (t n)"), pyt[:], ACT.Copy).then_inc(yts_ready, 1)

                def store_branch(i, n, g):
                    act.wait_ge(out_mm, HEAD + n + 1)
                    pieces = scan_rows(i, pz[:, 0:UT].rearrange("c (r s) -> c r s", r=ROWS))
                    for rows, src in pieces:
                        ins = af(order(i, br[i][:], g)[:, rows, :], src, ACT.Copy)
                    ins.then_inc(branch_copied, 1)

                def norm_outputs(k, n):
                    act.wait_ge(rs_ready, HEAD + n + 1)
                    act.wait_ge(yt_mm, HEAD + n)
                    for j in range(2):
                        ins = af(y5[:, j, :], y4[k % 2][:, j, :], ACT.Copy, scale=rs[:, j:j + 1])
                    ins.then_inc(y5_ready, 1)

                def body(gg, head):
                    u, c = act.snap(b * (NG * NBR) + gg * BU), act.snap(b * (NG * NBR * 2) + gg * 2 * BU)
                    x, a_ = act.snap(b * CONVS + gg * BU), act.snap(b * AHEAD + gg * 2 * BU)
                    v_, xl_ = act.snap(b * SILUS + gg * BU), act.snap(b * (CONVS + 1) + gg * BU)
                    g17 = act.snap(b * (NG + 1) + gg * BG)
                    g2 = gg * BG if head else act.snap(gg * BG)

                    for k in range(BU):
                        n, m = u + k, c + 2 * k
                        p, i = k // NBR, k % NBR
                        copy_bc(k + 2, (k + 2) % NBR, b, x + k + 2, v_ + k + 2)
                        if k > 0 or not head:
                            square(k - 1, 1, n - 1, m - 1)
                        copy_tokens(1, n, m + 1, a_ + 2 * k + 1)
                        if i == 3:
                            act.wait_ge(y2_ready, HEAD + m - 6)
                            act.wait_ge(hd_ready, HEAD + m - 6)
                            decay_factors(g17 + p + 1, 1 - p)
                        decay_exp(m + 1, a_ + 2 * k + 1)
                        copy_b(k + 1, v_ + k + 1)
                        if k > 0 or not head:
                            norm_outputs(k - 1, n - 1)
                        if i == 2:
                            step_sizes(g17 + p + 1)
                        act.wait_ge(z_mm, HEAD + n + 1)
                        act.wait_ge(zg_ready, HEAD + n)
                        af(tz[:].rearrange("c j d -> c (j d)"), pz[:], ACT.Tanh, scale=0.5).then_inc(tz_ready, 1)
                        if k > 0 or not head:
                            copy_turned(n - 1)
                        copy_tokens(0, n + 1, m + 2, a_ + 2 * k + 2)
                        decay_exp(m + 2, a_ + 2 * k + 2)
                        copy_x(k + 3, (k + 3) % NBR, xl_ + k + 3, x + k + 3, v_ + k + 3)
                        conv_tanh(k + 2, x + k + 2, v_ + k + 2)
                        if k > 0 or not head:
                            store_branch((k - 1) % NBR, n - 1, g2 + (k - 1) // NBR)
                        square(k, 0, n, m)

                body(0, True)
                with act.Fori(1, NG // BG) as gg:
                    body(gg, False)
                units = act.snap((b + 1) * (NG * NBR))
                square(BU - 1, 1, units - 1, 2 * units - 1)
                norm_outputs(BU - 1, units - 1)
                copy_turned(units - 1)
                store_branch(NBR - 1, units - 1, NG - 1)
                act.wait_ge(branch_copied, HEAD + (b + 1) * (NG * NBR))
                for i in range(NBR):
                    af(brf[i], brf[i], ACT.Copy, accum_out=sums[:, i + 1:i + 2]).then_inc(sums_act, 1)
                for q in range(LOCAL_PE):
                    act.wait_ge(local_mm, b * LOCAL_PE + q + 1)
                    af(brf[4][:, LOCAL_ROWS * HW + q * TT:LOCAL_ROWS * HW + (q + 1) * TT], local_out(q),
                       ACT.Gelu_apprx_tanh, accum_out=sums[:, 5 + q:6 + q]).then_inc(sums_act, 1)
                act.wait_ge(local_ready, b + 1)
                af(brf[4][:, 0:LOCAL_ROWS * HW], brf[4][:, 0:LOCAL_ROWS * HW],
                   ACT.Gelu_apprx_tanh, accum_out=sums[:, 0:1]).then_inc(sums_act, 1)
                act.wait_ge(se_step, b * SE_STEPS + 4)
                af(se[:, 20:22], se[:, 18:20], ACT.Gelu_apprx_tanh).then_inc(se_nonlin, 1)
                act.wait_ge(se_step, b * SE_STEPS + 7)
                af(se[:, 35:40], se[:, 30:35], ACT.Tanh, scale=0.5).then_inc(se_nonlin, 1)

                def tile(buf, t):
                    return buf[:, bass.ds(t * TT, TT)]

                with act.Fori(0, NT // 2) as tp:
                    for h in range(2):
                        t = tp * 2 + h
                        act.wait_ge(proj_mm, HEAD + b * NT + t + 1)
                        act.wait_ge(fused_ready, HEAD + b * NT + t + 1)
                        af(tile(brf[1], t), px[:, h * TT:(h + 1) * TT], ACT.Copy).then_inc(proj_copied, 1)
                act.wait_ge(affine_ready, b + 1)
                for q in range(4):
                    s = slice(q * L // 4, (q + 1) * L // 4)
                    af(brf[1][:, s], brf[1][:, s], ACT.Gelu_apprx_tanh, bias=gst[:, 12:13], scale=gst[:, 11:12]).then_inc(gelu_ready, 1)

                def norm_tokens(pass_):
                    with act.Fori(0, NT // 2) as tp:
                        for h in range(2):
                            t = tp * 2 + h
                            e = (b * 2 + pass_) * NT + t
                            act.wait_ge(centered, HEAD + e + 1)
                            af(tile(brf[2], t), tile(brf[1], t), ACT.Square).then_inc(squares_ready, 1)
                    with act.Fori(0, NT // 2) as tp:
                        for h in range(2):
                            t = tp * 2 + h
                            e = (b * 2 + pass_) * NT + t
                            act.wait_ge(var_mm, HEAD + e + 1)
                            af(tile(brf[2], t), (pt, pyt)[h][:], ACT.Ln, bias=eps[:, 0:1]).then_inc(ln_ready, 1)
                    with act.Fori(0, NT // 2) as tp:
                        for h in range(2):
                            t = tp * 2 + h
                            e = (b * 2 + pass_) * NT + t
                            act.wait_ge(ln_ready, HEAD + e + 1)
                            af(tile(brf[2], t), tile(brf[2], t), ACT.Exp, scale=-0.5).then_inc(rstd_ready, 1)

                norm_tokens(0)
                with act.Fori(0, NT // 2) as tp:
                    for h in range(2):
                        t = tp * 2 + h
                        act.wait_ge(kv_mm, HEAD + b * NT + t + 1)
                        act.wait_ge(kv_summed, HEAD + b * NT + t - 1)
                        act.wait_ge(normed, HEAD + b * (2 * NT) + NT)
                        af(ks[h], pd[:, h * TT:(h + 1) * TT], ACT.Identity, bias=par("bk")).then_inc(k_ready, 1)
                with act.Fori(0, NT // 2) as tp:
                    for h in range(2):
                        t = tp * 2 + h
                        act.wait_ge(q_mm, HEAD + b * NT + t + 1)
                        act.wait_ge(kv_step, b * 2 + 2)
                        af(tile(brf[2], t), (pz, py)[h][:], ACT.Identity, bias=kvp[:, 9:10], scale=kvp[:, 8:9]).then_inc(q_ready, 1)
                norm_tokens(1)
                act.wait_ge(logits_step, b * 3 + 3)
                g_ = [gates[:, q, :, :].rearrange("c s e -> c (s e)") for q in range(4)]
                af(g_[0], g_[2], ACT.Exp).then_inc(gates_exp, 1)
                for t in range(NT):
                    act.wait_ge(gates_turned, b * NT + t + 1)
                    af(brf[2][0:NE, t * TT:(t + 1) * TT], (pt, pyt)[t % 2][0:NE, :], ACT.Copy).then_inc(gates_copied, 1)
                with act.Fori(0, L // (2 * P)) as s2:
                    e = act.snap(b * (L // P) + s2 * 2)
                    for h in range(2):
                        act.wait_ge(expert_mm, HEAD + e + h - 1)
                        af(xst[h], brf[1][:, bass.ds(s2 * (2 * P) + h * P, P)], ACT.Copy).then_inc(xst_ready, 1)

        @block.vector
        def _(dve):
            v = nc.vector
            head_start(dve, (quarter_ready, dtx_ready, lna_ready, cum_ready, acc_ready, xbc_ready, mix_ready,
                             xd0_ready, state_ready, y2_ready, zg_ready, fused_ready, centered, normed, kv_summed,
                             x2_ready, weighed, out_ready))
            v.memset(xp[:], 0.0)
            v.memset(eps[:], LN_EPS)
            dve.wait_ge(weights_in, 16 * len(loads))
            dve.wait_ge(pos_mm, 1)
            for r in range(9):
                v.tensor_scalar(local_diag[:, r, :], ident[:], local_w[:, r:r + 1], None, ALU.mult)
            v.tensor_scalar(conv_w[:], conv_w[:], 0.5, None, ALU.mult)
            for i in range(NBR):
                for t in range(2):
                    v.tensor_scalar(w_out[:, i, t, :], w_out[:, i, t, :], norm_w[:, i, t:t + 1], None, ALU.mult)
            v.tensor_copy(pos[:, 0, :], pt[:, 0:HW])
            v.tensor_copy(pos[:, 1, :], pyt[:, 0:HW]).then_inc(params_scaled, 1)
            dve.wait_ge(params_scaled, 1)
            dve.wait_ge(a_step, 1)
            v.tensor_scalar(par("A"), par("A"), -1.0, None, ALU.mult).then_inc(a_step, 1)
            dve.wait_ge(a_step, 2)

            def step_bias(q):
                dve.wait_ge(dt_mm, HEAD + q + 1)
                dve.wait_ge(dt_exp, HEAD + q)
                v.tensor_tensor(dtx[:].rearrange("c (j n) -> c j n", j=2),
                                    px[:, XS:XS + GC].rearrange("c (j n) -> c j n", j=2),
                                    par("dtb").unsqueeze(1).broadcast_to([P, 2, NBR * NH]), ALU.add).then_inc(dtx_ready, 1)

            def softplus(q, p, r):
                steps = len(LOG1P)
                e = dte[:, 2, :]
                if r == 0:
                    dve.wait_ge(dt_exp, HEAD + q + 1)
                    dve.wait_ge(cum_mm, HEAD + q)
                    v.tensor_scalar(dtp[:], e, LOG1P[-1], None, ALU.mult).then_inc(poly_step, 1)
                elif r < steps:
                    dve.wait_ge(poly_step, q * steps + r)
                    v.scalar_tensor_tensor(dtp[:], dtp[:], LOG1P[-1 - r], e, ALU.add, ALU.mult).then_inc(poly_step, 1)
                elif r == steps:
                    dve.wait_ge(poly_step, (q + 1) * steps)
                    v.tensor_tensor(wd[p][:, :, 0, :], dtp[:].rearrange("c (u h) -> c u h", h=NH),
                                    dte[:, 0, :].rearrange("c (u h) -> c u h", h=NH), ALU.add).then_inc(log_step, 1)
                elif r == steps + 1:
                    dve.wait_ge(log_step, q * 2 + 1)
                    av = par("A").rearrange("c (i h) -> c i h", h=NH)
                    for j in range(2):
                        ins = v.tensor_tensor(lna[:, j * 32:(j + 1) * 32].rearrange("c (i h) -> c i h", h=NH),
                                              wd[p][:, j * NBR:(j + 1) * NBR, 0, :], av, ALU.mult)
                    ins.then_inc(log_step, 1)
                else:
                    dve.wait_ge(log_step, q * 2 + 2)
                    v.tensor_copy(lna3[:].rearrange("c j (a n) -> c j a n", a=3),
                                  lna[:].rearrange("c (j n) -> c j n", j=2).unsqueeze(2).broadcast_to([P, 2, 3, 32])
                                  ).then_inc(lna_ready, 1)

            SOFTPLUS = len(LOG1P) + 3

            def split_sums(q, p, r):
                src = px[0:96, 2 * UT:3 * UT]
                if r == 0:
                    dve.wait_ge(cum_mm, HEAD + q + 1)
                    v.tensor_copy(cum[p][:], src).then_inc(part_step, 1)
                elif r == 1:
                    dve.wait_ge(part_step, q * 5 + 1)
                    v.tensor_tensor(cr[:], src, cum[p][:], ALU.subtract).then_inc(part_step, 1)
                elif r == 2:
                    dve.wait_ge(part_step, q * 5 + 2)
                    v.tensor_copy(cum[p][32:64, :], cr[32:64, :]).then_inc(part_step, 1)
                    v.tensor_copy(cum[p][64:96, :], cr[64:96, :]).then_inc(part_step, 1)
                elif r == 3:
                    dve.wait_ge(part_step, q * 5 + 4)
                    v.tensor_tensor(cr2[64:96, :], cr[64:96, :], cum[p][64:96, :], ALU.subtract).then_inc(part_step, 1)
                else:
                    dve.wait_ge(part_step, q * 5 + 5)
                    v.tensor_copy(cum[p][64:96, :], cr2[64:96, :]).then_inc(cum_ready, 1)

            def convolve(k, i, b, xn, r, t):
                if r > 1:
                    dve.wait_ge(tap_step, xn * (XT * (TAPS - 2)) + (r - 2) * XT + t + 1)
                elif t < 2:
                    dve.wait_ge(x_tap0, HEAD + xn + b + 1)
                else:
                    dve.wait_ge(bc_tap0, HEAD + xn + 1)
                o = acc[k % 2][:, t, :]
                ins = v.scalar_tensor_tensor(o, pre[k % 2][:, t, r:r + UT], conv_w[:, i, t, r:r + 1], o, ALU.mult, ALU.add)
                if r < TAPS - 1:
                    ins.then_inc(tap_step, 1)
                elif t == XT - 1:
                    ins.then_inc(acc_ready, 1)

            def silu(k, b, xn, m):
                dve.wait_ge(conv_tanh_ready, HEAD + xn + b + 1)
                dve.wait_ge(y_mm, HEAD + m)
                dve.wait_ge(bt_ready, HEAD + xn - 1)
                v.scalar_tensor_tensor(xbc[k % 2].rearrange("c t n -> c (t n)"),
                                           th[:].rearrange("c t n -> c (t n)"), 1.0,
                                           acc[k % 2].rearrange("c t n -> c (t n)"), ALU.add, ALU.mult).then_inc(xbc_ready, 1)

            with dve.Fori(0, NB) as b:
                for i in range(NBR):
                    v.memset(state[i][:], 0.0)
                    v.memset(past[i][:], 0.0)
                step_bias(b * (NG + 1))
                for r in range(SOFTPLUS):
                    softplus(b * (NG + 1), 0, r)
                for r in range(5):
                    split_sums(b * (NG + 1), 0, r)
                for r in range(1, TAPS):
                    for t in range(XT):
                        convolve(0, 0, b, b * CONVS, r, t)
                silu(0, b, b * SILUS, b * (NG * NBR * 2))
                for r in range(1, TAPS):
                    for t in range(XT):
                        convolve(1, 1, b, b * CONVS + 1, r, t)
                with dve.Fori(0, NG // BG) as gg:
                    u, c = dve.snap(b * (NG * NBR) + gg * BU), dve.snap(b * (NG * NBR * 2) + gg * 2 * BU)
                    x, a_ = dve.snap(b * CONVS + gg * BU), dve.snap(b * AHEAD + gg * 2 * BU)
                    g17, v_ = dve.snap(b * (NG + 1) + gg * BG), dve.snap(b * SILUS + gg * BU)

                    def scale_tokens(k, m, q):
                        p, i = k // NBR, k % NBR
                        dve.wait_ge(xtok_ready, HEAD + q + 1)
                        dve.wait_ge(wd_ready, HEAD + g17 + p + 1)
                        dve.wait_ge(y_mm, HEAD + m - 1)
                        v.tensor_tensor(
                            xd[0][:].rearrange("c q (h d) -> c q h d", h=NH),
                            xtok[0][:, 0:2, :].rearrange("c a (h d) -> c (a h) d", d=HD)
                            .unsqueeze(1).broadcast_to([P, 2, NH, HD]),
                            wd[p][:, i, :, :].unsqueeze(3).broadcast_to([P, 2, NH, HD]), ALU.mult).then_inc(xd0_ready, 1)

                    def mix_pairs(j, m, q):
                        dve.wait_ge(ebuf_ready, HEAD + q + 1)
                        dve.wait_ge(gm_ready, HEAD + q + 1)
                        dve.wait_ge(y_mm, HEAD + m - 1)
                        v.tensor_tensor(mix[j][:], ebuf[:], gm[j][:].unsqueeze(1)
                                            .broadcast_to([P, NH, P]), ALU.mult).then_inc(mix_ready, 1)

                    def update_state(i, j, m):
                        dve.wait_ge(state_mm, HEAD + m + 1)
                        dve.wait_ge(hd_ready, HEAD + m + 1)
                        v.tensor_tensor(state[i][C, 1 - j, :], hd[j][C, :], px[C, XS:XS + DIN], ALU.add).then_inc(state_ready, 1)

                    def decay_outputs(k, j, m):
                        p, i = k // NBR, k % NBR
                        ji = j * NBR + i
                        dve.wait_ge(y_mm, HEAD + m + 1)
                        dve.wait_ge(y2_ready, HEAD + m)
                        v.tensor_tensor(y1[:].rearrange("c (h d) -> c h d", h=NH),
                                            py[:, DIN:2 * DIN].rearrange("c (h d) -> c h d", h=NH),
                                            ec[p][:, 0, ji * NH:(ji + 1) * NH].unsqueeze(2).broadcast_to([P, NH, HD]),
                                            ALU.mult).then_inc(y1_ready, 1)

                    def add_outputs(m):
                        dve.wait_ge(y1_ready, m + 1)
                        dve.wait_ge(y3_ready, m)
                        v.tensor_tensor(y2[:], y1[:], py[:, 0:DIN], ALU.add).then_inc(y2_ready, 1)

                    for k in range(BU):
                        n, m = u + k, c + 2 * k
                        p, i = k // NBR, k % NBR
                        mix_pairs(0, m, a_ + 2 * k)
                        scale_tokens(k, m, a_ + 2 * k)
                        silu(k + 1, b, v_ + k + 1, m)
                        for t in range(XT):
                            if i == 3:
                                split_sums(g17 + p + 1, 1 - p, t)
                            convolve(k + 2, (k + 2) % NBR, b, x + k + 2, 1, t)
                        if i == 3:
                            split_sums(g17 + p + 1, 1 - p, 3)
                        if i == 2:
                            step_bias(g17 + p + 1)
                        if i == 3:
                            split_sums(g17 + p + 1, 1 - p, 4)
                        mix_pairs(1, m + 1, a_ + 2 * k + 1)
                        decay_outputs(k, 0, m)
                        if i == 2:
                            softplus(g17 + p + 1, 1 - p, 0)
                        add_outputs(m)
                        update_state(i, 0, m)
                        for t in range(XT):
                            if i == 2:
                                softplus(g17 + p + 1, 1 - p, 1 + t)
                            convolve(k + 2, (k + 2) % NBR, b, x + k + 2, 2, t)
                        if i == 2:
                            softplus(g17 + p + 1, 1 - p, 4)
                        update_state(i, 1, m + 1)
                        for t in range(XT):
                            if i == 2:
                                softplus(g17 + p + 1, 1 - p, 5 + t)
                            convolve(k + 2, (k + 2) % NBR, b, x + k + 2, 3, t)
                        if i == 2:
                            softplus(g17 + p + 1, 1 - p, 8)
                        dve.wait_ge(tz_ready, HEAD + n + 1)
                        dve.wait_ge(y4_ready, HEAD + m - 2)
                        v.scalar_tensor_tensor(zg[k % 2][:].rearrange("c j d -> c (j d)"),
                                               tz[:].rearrange("c j d -> c (j d)"), 1.0, pz[:],
                                               ALU.add, ALU.mult).then_inc(zg_ready, 1)
                        if i == 2:
                            softplus(g17 + p + 1, 1 - p, 9)
                        decay_outputs(k, 1, m + 1)
                        add_outputs(m + 1)
                        if i == 2:
                            for r in range(10, SOFTPLUS):
                                softplus(g17 + p + 1, 1 - p, r)

                dve.wait_ge(branch_copied, HEAD + (b + 1) * (NG * NBR))
                dve.wait_ge(bt_ready, HEAD + (b + 1) * SILUS)
                dve.wait_ge(conv_tanh_ready, HEAD + (b + 1) * CONVS)
                dve.wait_ge(x_tap0, HEAD + (b + 1) * (CONVS + 1))
                dve.wait_ge(xp_ready, (b + 1) * SLABS)
                v.tensor_scalar(br[4][:, 0:LOCAL_ROWS, :], xp[:, 0:LOCAL_ROWS, 0:HW], local_w[:, 0:1], None, ALU.mult).then_inc(local_step, 1)
                for r in range(1, 9):
                    dve.wait_ge(local_step, b * 8 + r)
                    dy, dx_ = r // 3, r % 3
                    ins = v.scalar_tensor_tensor(br[4][:, 0:LOCAL_ROWS, :], xp[:, dy:dy + LOCAL_ROWS, dx_:dx_ + HW],
                                                 local_w[:, r:r + 1], br[4][:, 0:LOCAL_ROWS, :],
                                                 ALU.mult, ALU.add)
                    ins.then_inc(local_step if r < 8 else local_ready, 1)
                dve.wait_ge(desc_mm, b + 1)
                v.tensor_scalar(se[:, 0:5], pt[:, 0:5], 1.0 / (P * L), None, ALU.mult).then_inc(se_step, 1)
                dve.wait_ge(se_step, b * SE_STEPS + 1)
                v.tensor_tensor(se[:, 5:15].rearrange("c (a j) -> c a j", a=2),
                                    se[:, 0:5].unsqueeze(1).broadcast_to([P, 2, 5]),
                                    par("w1").rearrange("c (a j) -> c a j", a=2), ALU.mult).then_inc(se_step, 1)
                dve.wait_ge(se_step, b * SE_STEPS + 2)
                v.tensor_reduce(se[:, 15:17], se[:, 5:15].rearrange("c (a j) -> c a j", a=2), AX.X, ALU.add).then_inc(se_step, 1)
                dve.wait_ge(se_step, b * SE_STEPS + 3)
                v.tensor_tensor(se[:, 18:20], se[:, 15:17], par("b1"), ALU.add).then_inc(se_step, 1)
                dve.wait_ge(se_step, b * SE_STEPS + 4)
                dve.wait_ge(se_nonlin, b * 2 + 1)
                v.tensor_tensor(se[:, 5:15].rearrange("c (j a) -> c j a", a=2),
                                    se[:, 20:22].unsqueeze(1).broadcast_to([P, 5, 2]),
                                    par("w2").rearrange("c (j a) -> c j a", a=2), ALU.mult).then_inc(se_step, 1)
                dve.wait_ge(se_step, b * SE_STEPS + 5)
                v.tensor_reduce(se[:, 22:27], se[:, 5:15].rearrange("c (j a) -> c j a", a=2), AX.X, ALU.add).then_inc(se_step, 1)
                dve.wait_ge(se_step, b * SE_STEPS + 6)
                v.tensor_tensor(se[:, 30:35], se[:, 22:27], par("b2"), ALU.add).then_inc(se_step, 1)
                dve.wait_ge(se_step, b * SE_STEPS + 7)
                dve.wait_ge(se_nonlin, b * 2 + 2)
                v.tensor_scalar(sew[:], se[:, 35:40], 1.0, 0.5, ALU.add, ALU.mult).then_inc(se_ready, 1)

                def tile(buf, t):
                    return buf[:, bass.ds(t * TT, TT)]

                with dve.Fori(0, NT // 2) as tp:
                    for h in range(2):
                        t = tp * 2 + h
                        dve.wait_ge(se_ready, b + 1)
                        dve.wait_ge(proj_mm, HEAD + b * NT + t + 1)
                        dve.wait_ge(x_tile_in[h], (b * (NT // 2) + tp + 1) * 16)
                        out = tile(brf[0], t)
                        v.scalar_tensor_tensor(out, out, sew[:, 1:2], ks[h], ALU.mult, ALU.add).then_inc(fuse_step, 1)
                        for r, j in enumerate((1, 2, 3, 4)):
                            w = (j + 1) % 5
                            dve.wait_ge(fuse_step, (b * NT + t) * 4 + r + 1)
                            ins = v.scalar_tensor_tensor(out, tile(brf[j], t), sew[:, w:w + 1], out, ALU.mult, ALU.add)
                            ins.then_inc(fuse_step if r < 3 else fused_ready, 1)
                dve.wait_ge(proj_copied, HEAD + b * NT + NT)
                for t in range(NT):
                    ins = v.bn_stats(bnst[:, t, :], brf[1][:, t * TT:(t + 1) * TT])
                ins.then_inc(gn_step, 1)
                dve.wait_ge(gn_step, b * GN_STEPS + 1)
                v.memset(gst[:, 15:16], 0.0)
                v.bn_aggr(gst[:, 0:2], bnst[:]).then_inc(gn_step, 1)
                dve.wait_ge(gn_step, b * GN_STEPS + 2)
                v.tensor_copy(gst[:, 2:3], gst[:, 0:1])
                v.scalar_tensor_tensor(gst[:, 3:4], gst[:, 0:1], gst[:, 0:1], gst[:, 1:2], ALU.mult, ALU.add).then_inc(gn_step, 1)
                dve.wait_ge(gn_step, b * GN_STEPS + 3)
                dve.wait_ge(group_mm, b + 1)
                v.tensor_copy(gst[:, 5:6], pt[:, 8:9])
                v.tensor_scalar(gst[:, 6:7], pt[:, 9:10], GN_EPS, None, ALU.add).then_inc(norm_step, 1)
                dve.wait_ge(norm_step, b * 3 + 1)
                v.tensor_tensor(gst[:, 4:5], gst[:, 5:6], gst[:, 5:6], ALU.mult).then_inc(norm_step, 1)
                dve.wait_ge(norm_step, b * 3 + 2)
                v.tensor_tensor(gst[:, 7:8], gst[:, 6:7], gst[:, 4:5], ALU.subtract).then_inc(gn_step, 1)
                dve.wait_ge(gn_step, b * GN_STEPS + 4)
                dve.wait_ge(group_rsqrt, b + 1)
                v.tensor_tensor(gst[:, 11:12], gst[:, 8:9], par("gamma"), ALU.mult).then_inc(gn_step, 1)
                dve.wait_ge(gn_step, b * GN_STEPS + 5)
                v.tensor_tensor(gst[:, 13:14], gst[:, 5:6], gst[:, 11:12], ALU.mult).then_inc(norm_step, 1)
                dve.wait_ge(norm_step, b * 3 + 3)
                v.tensor_tensor(gst[:, 12:13], par("beta"), gst[:, 13:14], ALU.subtract).then_inc(affine_ready, 1)
                for q in range(4):
                    s = slice(q * L // 4, (q + 1) * L // 4)
                    dve.wait_ge(gelu_ready, b * 4 + q + 1)
                    v.tensor_tensor(brf[0][:, s], brf[0][:, s], brf[1][:, s], ALU.add).then_inc(x1_ready, 1)
                def norm_tokens(pass_):
                    with dve.Fori(0, NT // 2) as tp:
                        for h in range(2):
                            t = tp * 2 + h
                            e = (b * 2 + pass_) * NT + t
                            dve.wait_ge(mean_mm, HEAD + e + 1)
                            if pass_ == 0:
                                dve.wait_ge(x1_ready, b * 4 + tp + 1)
                            v.tensor_tensor(tile(brf[1], t), tile(brf[0], t), (pz, py)[h][:], ALU.subtract).then_inc(centered, 1)
                    with dve.Fori(0, NT // 2) as tp:
                        for h in range(2):
                            t = tp * 2 + h
                            e = (b * 2 + pass_) * NT + t
                            dve.wait_ge(rstd_ready, HEAD + e + 1)
                            v.tensor_tensor(tile(brf[1], t), tile(brf[1], t), tile(brf[2], t), ALU.mult).then_inc(normed, 1)

                norm_tokens(0)
                for t in range(NT):
                    h = t % 2
                    dve.wait_ge(kv_mm, HEAD + b * NT + t + 1)
                    dve.wait_ge(k_ready, HEAD + b * NT + t + 1)
                    if t >= 1:
                        dve.wait_ge(kv_summed, HEAD + b * NT + t)
                    v.scalar_tensor_tensor(dump, px[:, h * TT:(h + 1) * TT], par("bv"), ks[h], ALU.add, ALU.mult,
                                               accum_out=kvp[:, t:t + 1]).then_inc(kv_summed, 1)
                dve.wait_ge(kv_summed, HEAD + b * NT + NT)
                v.tensor_reduce(kvp[:, 8:9], kvp[:, 0:8], AX.X, ALU.add).then_inc(kv_step, 1)
                dve.wait_ge(kv_step, b * 2 + 1)
                v.tensor_tensor(kvp[:, 9:10], kvp[:, 8:9], par("bq"), ALU.mult).then_inc(kv_step, 1)
                with dve.Fori(0, NT // 2) as tp:
                    for h in range(2):
                        t = tp * 2 + h
                        dve.wait_ge(q_ready, HEAD + b * NT + t + 1)
                        v.tensor_tensor(tile(brf[0], t), tile(brf[0], t), tile(brf[2], t), ALU.add).then_inc(x2_ready, 1)
                norm_tokens(1)
                NS = L // P
                g3 = [gates[:, q, :, :] for q in range(4)]
                dve.wait_ge(logits_mm, b + 1)
                v.tensor_tensor(g3[1], pz[:, 0:NS * NE].rearrange("c (s e) -> c s e", e=NE),
                                    par("rb").unsqueeze(1).broadcast_to([P, NS, NE]), ALU.add).then_inc(logits_step, 1)
                dve.wait_ge(logits_step, b * 3 + 1)
                v.tensor_reduce(gmx[:, 0, :], g3[1], AX.X, ALU.max).then_inc(logits_step, 1)
                dve.wait_ge(logits_step, b * 3 + 2)
                v.tensor_tensor(g3[2], g3[1], gmx[:, 0, :].unsqueeze(2).broadcast_to([P, NS, NE]), ALU.subtract).then_inc(logits_step, 1)
                def spread(row):
                    return row.unsqueeze(2).broadcast_to([P, NS, NE])

                order_ = par("first").unsqueeze(1).broadcast_to([P, NS, NE])
                g = b * GATE_STEPS

                def best(logits, maximum, maximum_order, picked, g):
                    v.tensor_tensor(top[0], logits, spread(maximum), ALU.is_equal).then_inc(gate_step, 1)
                    dve.wait_ge(gate_step, g + 1)
                    v.tensor_tensor(top[1], top[0], order_, ALU.mult).then_inc(gate_step, 1)
                    dve.wait_ge(gate_step, g + 2)
                    v.tensor_reduce(maximum_order, top[1], AX.X, ALU.max).then_inc(gate_step, 1)
                    dve.wait_ge(gate_step, g + 3)
                    v.tensor_tensor(picked, top[1], spread(maximum_order), ALU.is_equal).then_inc(gate_step, 1)
                    dve.wait_ge(gate_step, g + 4)

                best(g3[1], gmx[:, 0, :], gmx[:, 1, :], top[2], g)
                v.scalar_tensor_tensor(top[3], top[2], NEVER, g3[1], ALU.mult, ALU.add).then_inc(gate_step, 1)
                dve.wait_ge(gate_step, g + 5)
                v.tensor_reduce(gmx[:, 2, :], top[3], AX.X, ALU.max).then_inc(gate_step, 1)
                dve.wait_ge(gate_step, g + 6)
                best(top[3], gmx[:, 2, :], gmx[:, 3, :], g3[3], g + 6)
                v.tensor_tensor(top[0], top[2], g3[3], ALU.add).then_inc(gate_step, 1)
                dve.wait_ge(gate_step, g + 11)
                dve.wait_ge(gates_exp, b + 1)
                v.tensor_tensor(g3[1], top[0], g3[0], ALU.mult).then_inc(gate_step, 1)
                dve.wait_ge(gate_step, g + 12)
                v.tensor_reduce(gmx[:, 0, :], g3[1], AX.X, ALU.add).then_inc(gate_step, 1)
                dve.wait_ge(gate_step, g + 13)
                v.reciprocal(gmx[:, 1, :], gmx[:, 0, :]).then_inc(gate_step, 1)
                dve.wait_ge(gate_step, g + 14)
                v.tensor_tensor(g3[0], g3[1], spread(gmx[:, 1, :]), ALU.mult).then_inc(gates_ready, 1)

                def weigh(h, e, s):
                    dve.wait_ge(gates_ready, b + 1)
                    dve.wait_ge(expert_mm, HEAD + e + 1)
                    dve.wait_ge(half_ready, HEAD + e - 1)
                    gate = gates[:, 0, s, :] if isinstance(s, int) else gates[:, 0, bass.ds(s, 1), :].rearrange("c o e -> c (o e)")
                    v.tensor_tensor(mix[h][:], (px, pd)[h][:].rearrange("c (e n) -> c e n", e=NE),
                                    gate.unsqueeze(2).broadcast_to([P, NE, P]), ALU.mult).then_inc(weighed, 1)

                def quarter(h, e):
                    dve.wait_ge(half_ready, HEAD + e + 1)
                    dve.wait_ge(comb_mm, HEAD + e - 1)
                    v.tensor_tensor(quarter_sum[h], half_sum[h][:, 0:2, :], half_sum[h][:, 2:4, :],
                                    ALU.add).then_inc(quarter_ready, 1)

                def finish(h, e, s):
                    dve.wait_ge(comb_mm, HEAD + e + 1)
                    cols = slice(s * P, (s + 1) * P) if isinstance(s, int) else bass.ds(s * P, P)
                    v.tensor_tensor(brf[3][:, cols], brf[0][:, cols], (pz, py)[h][:, 0:P], ALU.add).then_inc(out_ready, 1)

                e0 = dve.snap(b * NS)
                weigh(0, e0, 0)
                for s in (1, 2, 3):
                    weigh(s % 2, e0 + s, s)
                    quarter((s - 1) % 2, e0 + s - 1)
                    if s == 3:
                        finish(0, e0, 0)
                with dve.Fori(2, NS // 2) as s2:
                    e = dve.snap(b * NS + s2 * 2)
                    for h in range(2):
                        weigh(h, e + h, s2 * 2 + h)
                        quarter(1 - h, e + h - 1)
                        finish(1 - h, e + h - 3, s2 * 2 + h - 3)
                quarter(1, e0 + NS - 1)
                for s in (NS - 3, NS - 2, NS - 1):
                    finish(s % 2, e0 + s, s)
                dve.wait_ge(out_ready, HEAD + (b + 1) * NS)


def kernel(**inputs):
    import concourse.bacc as _bacc
    from concourse.bass_utils import run_bass_kernel_spmd as _run

    f32 = np.float32
    pre = "L0_conv_"
    w = {k: np.ascontiguousarray(v) for k, v in inputs.items()}
    half = P // 2
    dim_t = 10000.0 ** (np.arange(0, half, 2, dtype=f32) / half)
    ang = np.arange(HW, dtype=f32)[:, None] / dim_t
    emb = np.stack([np.sin(ang), np.cos(ang)], 2).reshape(HW, -1).T.astype(f32)
    r = np.arange(P)
    c_sel = np.tile(np.eye(NBR * NH, dtype=f32), (3, 1))
    first = np.arange(NE, 0, -1, dtype=f32)
    rows = [w[pre + "A_log"].reshape(-1), w[pre + "dt_bias"].reshape(-1), w[pre + "Dp"].reshape(-1),
            w[pre + "se_w1"].T.reshape(-1), w[pre + "se_b1"], w[pre + "se_w2"].T.reshape(-1), w[pre + "se_b2"],
            w["L1_ffn_router_b"], first]
    cols = [w[pre + "gn_gamma"], w[pre + "gn_beta"], w["L1_attn_bq"], w["L1_attn_bk"], w["L1_attn_bv"]]
    small = np.concatenate([np.broadcast_to(np.concatenate(rows), (P, sum(x.size for x in rows))),
                            np.stack(cols, 1)], 1)
    arrays = {
        "x": w["x"].reshape(NB, P, L),
        "c_ident": np.eye(P, dtype=f32),
        "c_upto": (r[:, None] <= r[None, :]).astype(f32),
        "c_after": (r[:, None] > r[None, :]).astype(f32),
        "c_group": (r[:, None] // 16 == r[None, :] // 16).astype(f32) / f32(16),
        "c_sel": c_sel,
        "c_pos": np.concatenate([emb, emb]),
        "small": small,
        "w_in": w[pre + "W_in"],
        "conv_w": w[pre + "conv_w"].reshape(NBR, TAPS, XT, P).transpose(3, 0, 2, 1),
        "w_out": w[pre + "W_out"].reshape(NBR, DIN, P),
        "norm_w": w[pre + "norm_w"].reshape(NBR, 2, P).transpose(2, 0, 1),
        "proj_w": w[pre + "proj_w"].T,
        "pos_w": w[pre + "pos_proj_w"].T,
        "local_w": w[pre + "local_w"].reshape(P, 9),
        "wq": w["L1_attn_Wq"], "wk": w["L1_attn_Wk"], "wv": w["L1_attn_Wv"],
        "router": w["L1_ffn_router_w"], "expert_w": w["L1_ffn_expert_w"], "expert_b": w["L1_ffn_expert_b"],
    }
    arrays = {k: np.ascontiguousarray(v) for k, v in arrays.items()}
    nc = _bacc.Bacc("TRN2", target_bir_lowering=False, num_devices=1)
    aps = {k: nc.dram_tensor(f"in_{k}", v.shape, mybir.dt.from_np(v.dtype), kind="ExternalInput").ap()
           for k, v in arrays.items()}
    aps["out"] = nc.dram_tensor("out_0", (NB, P, L), F32, kind="ExternalOutput").ap()
    hybrid_kernel(nc, aps)
    res = _run(nc, [{f"in_{k}": v for k, v in arrays.items()}], core_ids=[0])
    return res.results[0]["out_0"].reshape(NB, P, HW, HW)
```
